# Optimizing a Trainium2 kernel written in Bass

```python
import numpy as np
import jax
import jax.numpy as jnp

def _softmax(x, axis=-1):
    return jax.nn.softmax(x, axis=axis)

def _gelu(x):
    return jax.nn.gelu(x, approximate=True)

def _silu(x):
    return jax.nn.silu(x)

def _sigmoid(x):
    return jax.nn.sigmoid(x)

def _layernorm(x, axis=-1, eps=1e-05):
    m = jnp.mean(x, axis=axis, keepdims=True)
    v = jnp.var(x, axis=axis, keepdims=True)
    return (x - m) / jnp.sqrt(v + eps)

def _scatter_add(tgt, idx, src, axis=0):
    return tgt.at[idx].add(src)

def _segment_sum(src, seg, n):
    return jax.ops.segment_sum(src, seg, n)
kernel_name = 'mk_xattn_ffn_d1_seqx_r8_5b15f4'

def setup_inputs(seed: int=0):
    np.random.seed(seed)
    _w = jnp.asarray

    def _rec_inputs():
        import jax
        import jax.numpy as jnp
        _rk = jax.random.key(seed)
        x = -0.0005207 + 1.001 * jax.random.normal(jax.random.fold_in(_rk, 1), (8, 256, 128), jnp.float32)
        _lenS = 256 - jax.random.randint(jax.random.fold_in(_rk, 7), (8,), 0, max(1, 256 // 4) + 1, jnp.int32)
        _lenS2 = 256 - jax.random.randint(jax.random.fold_in(_rk, 8), (8,), 0, max(1, 256 // 4) + 1, jnp.int32)
        _ctx_1024P = jax.random.normal(jax.random.fold_in(_rk, 11), (8, 16, 128), jnp.float32)
        _ctx_1024c = jax.random.dirichlet(jax.random.fold_in(_rk, 511), 0.3 * jnp.ones((16,), jnp.float32), (8, 256))
        _ctx_1024t = jnp.einsum('bsk,bkd->bsd', _ctx_1024c, _ctx_1024P)
        _ctx_1024t = _ctx_1024t * jax.lax.rsqrt(jnp.mean(jnp.square(_ctx_1024t)) + 1e-12) * 0.953939
        ctx_1024 = -0.000514642 + 1.00011 * (_ctx_1024t + 0.3 * jax.random.normal(jax.random.fold_in(_rk, 611), (8, 256, 128), jnp.float32))
        return (x, ctx_1024)
    x, ctx_1024 = _rec_inputs()

    def _L0_xattn_setup():
        import jax, jax.numpy as jnp
        import numpy as np
        B, S, E, NH = (1, 256, 128, 8)
        DH = E // NH
        EPS_BACKEND = 1e-06
        EPS_NORM = 1e-05
        key = jax.random.key(seed)
        ks = jax.random.split(key, 8)
        q = jax.random.normal(ks[0], (B, S, E), jnp.float32)
        k = jax.random.normal(ks[1], (B, S, E), jnp.float32)
        v = jax.random.normal(ks[2], (B, S, E), jnp.float32)
        igate_w = jax.random.normal(ks[3], (NH, 3 * E), jnp.float32) * 0.02
        igate_b = jax.random.normal(ks[4], (NH,), jnp.float32) * 0.1
        fgate_w = jax.random.normal(ks[5], (NH, 3 * E), jnp.float32) * 0.02
        fgate_b = jnp.linspace(3.0, 6.0, NH).astype(jnp.float32)
        norm_w = 1.0 + 0.1 * jax.random.normal(ks[6], (E,), jnp.float32)
        return dict(q=q, k=k, v=v, igate_w=igate_w, igate_b=igate_b, fgate_w=fgate_w, fgate_b=fgate_b, norm_w=norm_w)
    _L0_xattn_all = _L0_xattn_setup()
    _L0_xattn_in = {k: v for k, v in _L0_xattn_all.items() if k in ('igate_w', 'igate_b', 'fgate_w', 'fgate_b', 'norm_w')}
    del _L0_xattn_all

    def _L0_ffn_setup():
        import jax, jax.numpy as jnp
        import numpy as np
        H_DIM, E_DIM = (128, 64)
        N_SHARED, N_ROUTED, TOP_K = (2, 16, 4)
        B, S = (4, 256)
        key = jax.random.key(seed)
        ks = jax.random.split(key, 6)
        sc = 1.0 / np.sqrt(H_DIM)
        ec = 1.0 / np.sqrt(E_DIM)
        return {'x': jax.random.normal(ks[0], (B, S, H_DIM), dtype=jnp.float32), 'shared_up': jax.random.uniform(ks[1], (N_SHARED, E_DIM, H_DIM), jnp.float32, -sc, sc), 'shared_down': jax.random.uniform(ks[2], (N_SHARED, H_DIM, E_DIM), jnp.float32, -ec, ec), 'routed_up': jax.random.uniform(ks[3], (N_ROUTED, E_DIM, H_DIM), jnp.float32, -sc, sc), 'routed_down': jax.random.uniform(ks[4], (N_ROUTED, H_DIM, E_DIM), jnp.float32, -ec, ec), 'router_w': jax.random.uniform(ks[5], (N_ROUTED, H_DIM), jnp.float32, -sc, sc)}
    _L0_ffn_all = _L0_ffn_setup()
    _L0_ffn_in = {k: v for k, v in _L0_ffn_all.items() if k in ('shared_up', 'shared_down', 'routed_up', 'routed_down', 'router_w')}
    del _L0_ffn_all
    return {'x': x, 'ctx_1024': ctx_1024, 'L0_xattn_igate_w': _L0_xattn_in['igate_w'], 'L0_xattn_igate_b': _L0_xattn_in['igate_b'], 'L0_xattn_fgate_w': _L0_xattn_in['fgate_w'], 'L0_xattn_fgate_b': _L0_xattn_in['fgate_b'], 'L0_xattn_norm_w': _L0_xattn_in['norm_w'], 'L0_ffn_shared_up': _L0_ffn_in['shared_up'], 'L0_ffn_shared_down': _L0_ffn_in['shared_down'], 'L0_ffn_routed_up': _L0_ffn_in['routed_up'], 'L0_ffn_routed_down': _L0_ffn_in['routed_down'], 'L0_ffn_router_w': _L0_ffn_in['router_w']}

def reference(x, ctx_1024, L0_xattn_igate_w, L0_xattn_igate_b, L0_xattn_fgate_w, L0_xattn_fgate_b, L0_xattn_norm_w, L0_ffn_shared_up, L0_ffn_shared_down, L0_ffn_routed_up, L0_ffn_routed_down, L0_ffn_router_w):
    import jax
    import jax.numpy as jnp

    def _L0_xattn_ref(q, k, v, igate_w, igate_b, fgate_w, fgate_b, norm_w):
        import jax, jax.numpy as jnp
        import numpy as np
        B, S, E, NH = (1, 256, 128, 8)
        DH = E // NH
        EPS_BACKEND = 1e-06
        EPS_NORM = 1e-05
        Bq, Sq, Eq = q.shape
        nh = igate_w.shape[0]
        dh = Eq // nh
        gate_in = jnp.concatenate([q, k, v], axis=-1)
        ig = jnp.transpose(gate_in @ igate_w.T + igate_b, (0, 2, 1))
        fg = jnp.transpose(gate_in @ fgate_w.T + fgate_b, (0, 2, 1))
        qh = q.reshape(Bq, Sq, nh, dh).transpose(0, 2, 1, 3)
        kh = k.reshape(Bq, Sq, nh, dh).transpose(0, 2, 1, 3)
        vh = v.reshape(Bq, Sq, nh, dh).transpose(0, 2, 1, 3)
        log_f_cum = jnp.cumsum(jax.nn.log_sigmoid(fg), axis=-1)
        log_fg_mat = log_f_cum[:, :, :, None] - log_f_cum[:, :, None, :]
        ltr = jnp.tril(jnp.ones((Sq, Sq), dtype=bool))
        log_D = jnp.where(ltr, log_fg_mat + ig[:, :, None, :], -jnp.inf)
        max_log_D = jnp.max(log_D, axis=-1, keepdims=True)
        D = jnp.exp(log_D - max_log_D)
        qk = jnp.einsum('bhsd,bhtd->bhst', qh, kh) / jnp.sqrt(jnp.float32(dh))
        C = qk * D
        normalizer = jnp.maximum(jnp.abs(jnp.sum(C, axis=-1, keepdims=True)), jnp.exp(-max_log_D))
        h = jnp.einsum('bhst,bhtd->bhsd', C / (normalizer + EPS_BACKEND), vh)
        mean = jnp.mean(h, axis=-1, keepdims=True)
        var = jnp.var(h, axis=-1, keepdims=True)
        h_norm = (h - mean) / jnp.sqrt(var + EPS_NORM)
        h_norm = h_norm * norm_w.reshape(nh, dh)[None, :, None, :]
        return h_norm.transpose(0, 2, 1, 3).reshape(Bq, Sq, Eq)

    def _L0_ffn_ref(x, shared_up, shared_down, routed_up, routed_down, router_w):
        import jax, jax.numpy as jnp
        import numpy as np
        H_DIM, E_DIM = (128, 64)
        N_SHARED, N_ROUTED, TOP_K = (2, 16, 4)
        B, S = (4, 256)
        b, s, h = x.shape
        xt = x.reshape(-1, h)
        up_s = jnp.einsum('th,seh->tse', xt, shared_up)
        shared = jnp.einsum('tse,she->th', jax.nn.gelu(up_s, approximate=False), shared_down)
        probs = jax.nn.softmax(xt @ router_w.T, axis=-1)
        topk_p, topk_i = jax.lax.top_k(probs, TOP_K)
        gate = jnp.zeros_like(probs).at[jnp.arange(xt.shape[0])[:, None], topk_i].add(topk_p)
        up_r = jnp.einsum('th,reh->tre', xt, routed_up)
        act = jax.nn.gelu(up_r, approximate=False) * gate[:, :, None]
        routed = jnp.einsum('tre,rhe->th', act, routed_down)
        return (shared + routed).reshape(b, s, h)
    x = x + _L0_xattn_ref(_layernorm(x, axis=-1), ctx_1024, ctx_1024, L0_xattn_igate_w, L0_xattn_igate_b, L0_xattn_fgate_w, L0_xattn_fgate_b, L0_xattn_norm_w)
    x = x + _L0_ffn_ref(_layernorm(x, axis=-1), L0_ffn_shared_up, L0_ffn_shared_down, L0_ffn_routed_up, L0_ffn_routed_down, L0_ffn_router_w)
    return x

_drawn_inputs = setup_inputs


def setup_inputs(seed=0):
    import zlib

    import numpy as np

    out = dict(_drawn_inputs(seed))
    spreads = {}
    factors = {'L0_xattn_igate_b': 64.0, 'L0_xattn_fgate_w': 4.798}
    for name, (base, spread) in spreads.items():
        noise = np.random.default_rng([zlib.crc32(name.encode()), seed]).standard_normal(out[name].shape)
        drawn = base * np.exp(spread * noise) if base else spread * noise
        out[name] = jnp.asarray(drawn.astype(out[name].dtype))
    for name, factor in factors.items():
        out[name] = (out[name] * factor).astype(out[name].dtype)
    return out
```

```python
from contextlib import ExitStack

import concourse.bass as bass
from concourse import mybir

P = 128
BATCH, SEQ, DIM = 8, 256, 128
HEADS, HD = 8, 16
TILES = SEQ // P
PAIRS = BATCH // 2
PTILES = 2 * TILES
PTOK = 2 * SEQ
NT = BATCH * TILES
UHEADS = HEADS // 2
VW = 32
ROWS = 2 * HEADS
LO = 32
EXPERTS, TOPK, HID = 16, 4, 64
CHUNKS = EXPERTS // 2 + 1
EPS_LN, EPS_HEAD, EPS_NORMALIZER = 1e-5, 1e-5, 1e-6
LOWEST = -3.0e38

F32 = mybir.dt.float32
F32R = mybir.dt.float32r
ALU = mybir.AluOpType
ACT = mybir.ActivationFunctionType
AX = mybir.AxisListType

CONST_PARTS = [("ident", P), ("headmask", HEADS), ("blockmask", HEADS * VW), ("spread", 2 * P),
               ("selcol", ROWS), ("normw", DIM), ("reset", PTILES * EXPERTS), ("gwq", 2 * 48),
               ("gwk", 2 * 48), ("gwv", 2 * 48), ("gbias", 1), ("router", EXPERTS)]
CONST_AT, CONSTS = {}, 0
for _name, _width in CONST_PARTS:
    CONST_AT[_name] = (CONSTS, _width)
    CONSTS += _width

MIN_STEP, F_STEP, G_STEP, M_STEP, SUM_STEP, NEGC_STEP, GATE_STEPS = 1, 2, 3, 4, 5, 6, 6
N_NEG, N_MAX, N_EPS, N_INV, N_SCALED, N_SUM, N_CENTRED, N_SQUARED, N_VAR, NORM_STEPS = 1, 2, 3, 4, 5, 6, 7, 8, 9, 9
(R_MAX, R_DIF, R_SUM, R_INV, R_TOP, R_ABOVE, R_EQUAL, R_NABOVE, R_RANK, R_PLACE, R_TIES, R_CHOSEN,
 R_PROB, ROUTER_STEPS) = 1, 2, 3, 4, 5, 6, 7, 8, 9, 10, 11, 12, 13, 13


def build(nc, x, ctx_rows, ctx_cols, consts, up_w, down_w, out):
    with ExitStack() as stack:
        def sb(name, shape, dt=F32):
            return stack.enter_context(nc.sbuf_tensor(name, shape, dt))

        def sem(name):
            return stack.enter_context(nc.semaphore(name))

        cst = sb("cst", [P, CONSTS])
        x_sb = sb("x_sb", [P, NT, DIM])
        ctx_sb = sb("ctx_sb", [P, NT, DIM])
        ctxT = sb("ctxT", [P, NT * P])
        up_sb = sb("up_sb", [P, CHUNKS * P])
        down_sb = sb("down_sb", [P, CHUNKS, DIM])

        def const(name, rows=P):
            a, n = CONST_AT[name]
            return cst[0:rows, a:a + n]

        ident = const("ident")
        sel = sb("sel", [P, ROWS, P], F32R)
        esel = sb("esel", [P, EXPERTS, HID], F32R)
        gwc = sb("gwc", [P, 2, 48])
        power = sb("power", [P, PTILES])
        st1 = sb("st1", [P, PTILES, 6])
        mv1 = sb("mv1", [P, PTILES, 2])
        var1 = sb("var1", [P, PTILES])
        rstd1 = sb("rstd1", [P, PTILES])
        xhat = sb("xhat", [P, PTILES, DIM])
        qT = sb("qT", [P, 2, PTOK])
        qmask = sb("qmask", [P, 2, HEADS, SEQ])
        z = sb("z", [ROWS, SEQ])
        ig = sb("ig", [ROWS, SEQ])
        zmin = sb("zmin", [ROWS, SEQ])
        zabs = sb("zabs", [ROWS, SEQ])
        zexp = sb("zexp", [ROWS, SEQ])
        soft = sb("soft", [ROWS, SEQ])
        Frow = sb("Frow", [ROWS, SEQ])
        Grow = sb("Grow", [ROWS, SEQ])
        Mrow = sb("Mrow", [ROWS, SEQ])
        FM = sb("FM", [ROWS, SEQ])
        negc = sb("negc", [ROWS, 1])
        rowq = sb("rowq", [48, SEQ])
        erow = sb("erow", [ROWS, P])
        Gst = sb("Gst", [P, 2, SEQ], F32R)
        Mst = sb("Mst", [P, 2, SEQ], F32R)
        tokq = sb("tokq", [P, 2, TILES, 48])
        qdec = sb("qdec", [P, 2, 2, P])
        vx = sb("vx", [P, NT, HEADS, VW])
        vw = sb("vw", [P, 2, HEADS, VW])
        state = sb("state", [P, 2, HEADS * VW])
        D = sb("D", [P, 2, UHEADS, TILES, P])
        C = sb("C", [P, 2, UHEADS, TILES, P])
        hT = sb("hT", [P, 2, TILES * P])
        nrm = sb("nrm", [P, 16])
        nrm2 = sb("nrm2", [P, 16])
        nrm3 = sb("nrm3", [P, 16])
        rinv = sb("rinv", [P, 16])
        h = sb("h", [P, 16, HD])
        hsum = sb("hsum", [P, 16])
        hc = sb("hc", [P, 2, 16, HD])
        hsq = sb("hsq", [P, 16, HD])
        hvar = sb("hvar", [P, 2, 16])
        hln = sb("hln", [P, 2, 16])
        hrstd = sb("hrstd", [P, 2, 16])
        y1 = sb("y1", [P, 16, HD])
        y2 = sb("y2", [P, 16, HD])
        x1 = sb("x1", [P, NT, DIM])
        st2 = sb("st2", [P, PTILES, 6])
        mv2 = sb("mv2", [P, PTILES, 2])
        var2 = sb("var2", [P, PTILES])
        rstd2 = sb("rstd2", [P, PTILES])
        x2hat = sb("x2hat", [P, PTILES, DIM])
        x2T = sb("x2T", [P, NT * P])
        rmax = sb("rmax", [P, PTILES])
        rdif = sb("rdif", [P, PTILES, EXPERTS])
        rexp = sb("rexp", [P, PTILES, EXPERTS])
        rsum = sb("rsum", [P, PTILES])
        rrec = sb("rrec", [P, PTILES])
        top8 = sb("top8", [P, PTILES, 8])
        above = sb("above", [P, PTILES, EXPERTS])
        equal = sb("equal", [P, PTILES, EXPERTS])
        nabove = sb("nabove", [P, PTILES])
        rank = sb("rank", [P, PTILES, EXPERTS])
        rank2 = sb("rank2", [P, PTILES, EXPERTS])
        ties = sb("ties", [P, PTILES, EXPERTS])
        chosen = sb("chosen", [P, PTILES, EXPERTS])
        prob = sb("prob", [P, PTILES, EXPERTS])
        gate = sb("gate", [P, PTILES, EXPERTS])
        gflat = sb("gflat", [EXPERTS, PTOK])
        gateT = sb("gateT", [P, NT * P], F32R)
        act = sb("act", [P, 2, PTOK])
        gact = sb("gact", [P, 2, PTOK])
        yT = sb("yT", [P, 2, PTOK])
        res = sb("res", [P, 2, PTILES, DIM])
        one1 = sb("one1", [P, 1])
        eps_head = sb("eps_head", [P, 1])

        pE = stack.enter_context(nc.psum_tensor("pE", [P, UHEADS, TILES, P], F32))
        pQK = stack.enter_context(nc.psum_tensor("pQK", [P, UHEADS, TILES, P], F32))
        pH = [stack.enter_context(nc.psum_tensor(f"pH{k}", [P, 512], F32)) for k in range(2)]
        pS = stack.enter_context(nc.psum_tensor("pS", [P, 512], F32))
        pT = stack.enter_context(nc.psum_tensor("pT", [P, 512], F32))

        def up_bank(n):
            return pE[:, 2 * (n % 2):2 * (n % 2) + 2, :, :].rearrange("p h k s -> p (h k s)")

        def spread_bank(n):
            return pQK[:, 2 * (n % 2):2 * (n % 2) + 2, :, :].rearrange("p h k s -> p (h k s)")

        def routed(n):
            g, c = divmod(n, CHUNKS)
            return g * (CHUNKS - 1) + min(c + 1, CHUNKS - 1)

        consts_loaded = sem("consts_loaded")
        weights_loaded = sem("weights_loaded")
        x_loaded = [sem(f"x_loaded{i}") for i in range(PAIRS)]
        ctx_loaded = [sem(f"ctx_loaded{i}") for i in range(PAIRS)]
        ctxT_loaded = [sem(f"ctxT_loaded{i}") for i in range(PAIRS)]
        pool_consts = sem("pool_consts")
        dve_consts = sem("dve_consts")
        vx_zeroed = sem("vx_zeroed")
        vx_ready = sem("vx_ready")
        ln1_stats = sem("ln1_stats")
        ln1_moments = sem("ln1_moments")
        ln1_var = sem("ln1_var")
        ln1_rstd = sem("ln1_rstd")
        xhat_ready = sem("xhat_ready")
        qT_in_psum = sem("qT_in_psum")
        qT_ready = sem("qT_ready")
        qmask_ready = sem("qmask_ready")
        gates_in_psum = sem("gates_in_psum")
        gates_ready = sem("gates_ready")
        softplus_steps = sem("softplus_steps")
        gate_steps = sem("gate_steps")
        split_hi = sem("split_hi")
        split_ready = sem("split_ready")
        row_exps = sem("row_exps")
        rows_in_psum = sem("rows_in_psum")
        rows_read = sem("rows_read")
        vw_ready = sem("vw_ready")
        state_in_psum = sem("state_in_psum")
        state_ready = sem("state_ready")
        E_in_psum = sem("E_in_psum")
        QK_in_psum = sem("QK_in_psum")
        exp_done = sem("exp_done")
        D_ready = sem("D_ready")
        C_ready = sem("C_ready")
        hT_in_psum = sem("hT_in_psum")
        hT_ready = sem("hT_ready")
        h_in_psum = sem("h_in_psum")
        norm_steps = sem("norm_steps")
        rstd_steps = sem("rstd_steps")
        hrstd_ready = sem("hrstd_ready")
        out_steps = sem("out_steps")
        x1_ready = sem("x1_ready")
        ln2_stats = sem("ln2_stats")
        ln2_moments = sem("ln2_moments")
        ln2_var = sem("ln2_var")
        ln2_rstd = sem("ln2_rstd")
        x2hat_ready = sem("x2hat_ready")
        x2T_in_psum = sem("x2T_in_psum")
        x2T_ready = sem("x2T_ready")
        logits_in_psum = sem("logits_in_psum")
        router_steps = sem("router_steps")
        rexp_ready = sem("rexp_ready")
        gate_ready = sem("gate_ready")
        gate_in_psum = sem("gate_in_psum")
        gflat_ready = sem("gflat_ready")
        gate_hi = sem("gate_hi")
        gateT_ready = sem("gateT_ready")
        spread_in_psum = sem("spread_in_psum")
        up_in_psum = sem("up_in_psum")
        gelu_ready = sem("gelu_ready")
        gact_ready = sem("gact_ready")
        down_done = sem("down_done")
        yT_ready = sem("yT_ready")
        y_turned = sem("y_turned")
        res_ready = sem("res_ready")
        stored = [sem(f"stored{g}") for g in range(PAIRS)]

        block = stack.enter_context(nc.Block())

        STEPS = BATCH + 4

        @block.sync
        def _(sp):
            sp.dma_start(cst[:, :], consts).then_inc(consts_loaded, 16)
            xr = x.rearrange("(i k p) d -> i p k d", k=PTILES, p=P)
            cr = ctx_rows.rearrange("(i k p) d -> i p k d", k=PTILES, p=P)
            orr = out.rearrange("(i k p) d -> i p k d", k=PTILES, p=P)
            for i in range(PAIRS):
                t = slice(i * PTILES, (i + 1) * PTILES)
                sp.dma_start(x_sb[:, t, :], xr[i]).then_inc(x_loaded[i], 16)
                sp.dma_start(ctxT[:, i * PTOK:(i + 1) * PTOK],
                             ctx_cols[:, i * PTOK:(i + 1) * PTOK]).then_inc(ctxT_loaded[i], 16)
                sp.dma_start(ctx_sb[:, t, :], cr[i]).then_inc(ctx_loaded[i], 16)
            sp.dma_start(up_sb[:, :], up_w).then_inc(weights_loaded, 16)
            sp.dma_start(down_sb[:, :, :], down_w).then_inc(weights_loaded, 16)
            for g in range(PAIRS):
                sp.wait_ge(res_ready, g + 1)
                sp.dma_start(orr[g], res[:, g % 2, :, :]).then_inc(stored[g], 16)
            for g in range(PAIRS):
                sp.wait_ge(stored[g], 16)

        @block.gpsimd
        def _(pool):
            def values(i):
                t = slice(i * PTILES, (i + 1) * PTILES)
                pool.wait_ge(ctx_loaded[i], 16)
                nc.gpsimd.tensor_copy(vx[:, t, :, 0:HD],
                                      ctx_sb[:, t, :].rearrange("p t (h d) -> p t h d", d=HD)).then_inc(vx_ready, 1)

            def rstd_first(i):
                pool.wait_ge(ln1_moments, i + 1)
                if i:
                    pool.wait_ge(ln1_rstd, i)
                nc.gpsimd.tensor_scalar(var1[:, :], mv1[:, :, 1], EPS_LN, None, ALU.add).then_inc(ln1_var, 1)
                pool.wait_ge(ln1_var, i + 1)
                if i:
                    pool.wait_ge(xhat_ready, i)
                nc.gpsimd.tensor_tensor(rstd1[:, :], var1[:, :], power[:, :], ALU.pow).then_inc(ln1_rstd, 1)

            def mask_queries(b):
                i, bb = b // 2, b % 2
                pool.wait_ge(qT_ready, i + 1)
                if b >= 2:
                    pool.wait_ge(QK_in_psum, 2 * b - 2)
                q = qT[:, i % 2, bb * SEQ:(bb + 1) * SEQ].unsqueeze(1).to_broadcast([P, HEADS, SEQ])
                m = const("headmask").unsqueeze(2).to_broadcast([P, HEADS, SEQ])
                nc.gpsimd.tensor_tensor(qmask[:, bb, :, :], q, m, ALU.mult).then_inc(qmask_ready, 1)

            def causal(u):
                pool.wait_ge(exp_done, u + 1)
                d = D[:, u % 2, :, :, :].rearrange("p h k s -> p (h k) s")
                nc.gpsimd.affine_select(out=d, in_=d, pattern=[[0, UHEADS * TILES], [1, P]],
                                        compare_op=ALU.is_ge, fill=0.0, base=0,
                                        channel_multiplier=-1).then_inc(D_ready, 1)

            def finish(b):
                pool.wait_ge(hrstd_ready, b + 1)
                if b:
                    pool.wait_ge(x1_ready, b)
                nc.gpsimd.tensor_tensor(y1[:, :, :], hc[:, b % 2, :, :],
                                        hrstd[:, b % 2, :].unsqueeze(2).to_broadcast([P, 16, HD]),
                                        ALU.mult).then_inc(out_steps, 1)
                pool.wait_ge(out_steps, 2 * b + 1)
                w = const("normw").unsqueeze(1).to_broadcast([P, TILES, DIM])
                nc.gpsimd.tensor_tensor(y2[:, :, :].rearrange("p (k h) d -> p k (h d)", k=TILES),
                                        y1[:, :, :].rearrange("p (k h) d -> p k (h d)", k=TILES), w,
                                        ALU.mult).then_inc(out_steps, 1)
                pool.wait_ge(out_steps, 2 * b + 2)
                t = slice(2 * b, 2 * b + 2)
                nc.gpsimd.tensor_tensor(x1[:, t, :], y2[:, :, :].rearrange("p (k h) d -> p k (h d)", k=TILES),
                                        x_sb[:, t, :], ALU.add).then_inc(x1_ready, 1)

            def rstd_second(i):
                pool.wait_ge(ln2_moments, i + 1)
                if i:
                    pool.wait_ge(ln2_rstd, i)
                nc.gpsimd.tensor_scalar(var2[:, :], mv2[:, :, 1], EPS_LN, None, ALU.add).then_inc(ln2_var, 1)
                pool.wait_ge(ln2_var, i + 1)
                if i:
                    pool.wait_ge(x2hat_ready, i)
                nc.gpsimd.tensor_tensor(rstd2[:, :], var2[:, :], power[:, :], ALU.pow).then_inc(ln2_rstd, 1)

            nc.gpsimd.memset(power[:, :], -0.5)
            nc.gpsimd.memset(rowq[:, :], 0.0)
            nc.gpsimd.memset(Gst[:, :, :].bitcast(F32), 0.0)
            nc.gpsimd.memset(Mst[:, :, :].bitcast(F32), 0.0).then_inc(pool_consts, 1)
            pool.wait_ge(pool_consts, 1)
            rstd_first(0)
            nc.gpsimd.memset(vx[:, :, :, HD + 1:], 0.0)
            nc.gpsimd.memset(vx[:, :, :, HD:HD + 1], 1.0).then_inc(vx_zeroed, 1)
            values(0)
            mask_queries(0)
            mask_queries(1)
            nc.gpsimd.memset(gateT[:, :].bitcast(F32), 0.0).then_inc(pool_consts, 1)
            for b in range(STEPS):
                i = b // 2
                if b < BATCH:
                    causal(2 * b)
                if b % 2 == 0 and i + 1 < PAIRS:
                    rstd_first(i + 1)
                    values(i + 1)
                if b < BATCH:
                    causal(2 * b + 1)
                if 1 <= b <= BATCH:
                    finish(b - 1)
                if b % 2 == 0 and i + 1 < PAIRS:
                    mask_queries(2 * i + 2)
                if b % 2 == 1 and i + 1 < PAIRS:
                    mask_queries(2 * i + 3)
                if b % 2 == 0 and 1 <= i <= PAIRS:
                    rstd_second(i - 1)

        @block.scalar
        def _(act_e):
            def take_queries(i):
                act_e.wait_ge(qT_in_psum, i + 1)
                if i >= 2:
                    act_e.wait_ge(qmask_ready, 2 * i - 2)
                    act_e.wait_ge(rows_read, i - 1)
                nc.scalar.activation(qT[:, i % 2, :], pS[:, :], ACT.Copy).then_inc(qT_ready, 1)

            def take_gates(i):
                act_e.wait_ge(gates_in_psum, i + 1)
                if i:
                    act_e.wait_ge(gate_steps, GATE_STEPS * i)
                nc.scalar.activation(z[:, :], pS[0:ROWS, 0:SEQ], ACT.Identity, bias=const("gbias")[0:ROWS, :])
                nc.scalar.activation(ig[:, :], pS[32:32 + ROWS, 0:SEQ], ACT.Identity,
                                     bias=const("gbias")[32:32 + ROWS, :]).then_inc(gates_ready, 1)
                act_e.wait_ge(gates_ready, i + 1)
                nc.scalar.activation(zabs[:, :], z[:, :], ACT.Abs).then_inc(softplus_steps, 1)
                act_e.wait_ge(softplus_steps, 3 * i + 1)
                nc.scalar.activation(zexp[:, :], zabs[:, :], ACT.Exp, scale=-1.0).then_inc(softplus_steps, 1)
                act_e.wait_ge(softplus_steps, 3 * i + 2)
                nc.scalar.activation(soft[:, :], zexp[:, :], ACT.Ln, bias=one1[0:ROWS, :]).then_inc(softplus_steps, 1)

            def row_factors(i):
                act_e.wait_ge(gate_steps, GATE_STEPS * i + NEGC_STEP)
                if i:
                    act_e.wait_ge(rows_in_psum, i)
                nc.scalar.activation(rowq[0:ROWS, 0:P], Grow[:, 0:P], ACT.Exp, bias=negc[:, :])
                nc.scalar.activation(rowq[32:32 + ROWS, :], FM[:, :], ACT.Exp, scale=-1.0)
                nc.scalar.activation(erow[:, :], Mrow[:, P:SEQ], ACT.Exp, scale=-1.0,
                                     bias=Mrow[:, P - 1:P]).then_inc(row_exps, 1)

            def decay(u):
                act_e.wait_ge(E_in_psum, u + 1)
                if u >= 2:
                    act_e.wait_ge(C_ready, u - 1)
                nc.scalar.activation(D[:, u % 2, :, :, :].rearrange("p h k s -> p (h k s)"),
                                     pE[:, :, :, :].rearrange("p h k s -> p (h k s)"), ACT.Exp).then_inc(exp_done, 1)

            def take_heads(u):
                act_e.wait_ge(hT_in_psum, u + 1)
                if u >= 2:
                    act_e.wait_ge(h_in_psum, u - 1)
                nc.scalar.activation(hT[:, u % 2, :], pH[u % 2][:, 0:TILES * P], ACT.Copy).then_inc(hT_ready, 1)

            def head_rstd(b):
                act_e.wait_ge(norm_steps, NORM_STEPS * (b + 1))
                if b >= 2:
                    act_e.wait_ge(x1_ready, b - 1)
                nc.scalar.activation(hln[:, b % 2, :], hvar[:, b % 2, :], ACT.Ln, bias=eps_head[:, :], scale=1.0 / HD
                                     ).then_inc(rstd_steps, 1)
                act_e.wait_ge(rstd_steps, b + 1)
                nc.scalar.activation(hrstd[:, b % 2, :], hln[:, b % 2, :], ACT.Exp, scale=-0.5).then_inc(hrstd_ready, 1)

            def take_x2(i):
                act_e.wait_ge(x2T_in_psum, i + 1)
                nc.scalar.activation(x2T[:, i * PTOK:(i + 1) * PTOK], pS[:, :], ACT.Copy).then_inc(x2T_ready, 1)

            def router_exp(i):
                act_e.wait_ge(router_steps, ROUTER_STEPS * i + 2)
                nc.scalar.activation(rexp[:, :, :], rdif[:, :, :], ACT.Exp).then_inc(rexp_ready, 1)

            def take_gateT(i):
                act_e.wait_ge(gate_in_psum, i + 1)
                if i:
                    act_e.wait_ge(gateT_ready, i)
                nc.scalar.activation(gflat[:, :], pS[0:EXPERTS, :], ACT.Copy).then_inc(gflat_ready, 1)

            def take_y(g):
                act_e.wait_ge(down_done, CHUNKS * (g + 1))
                if g >= 2:
                    act_e.wait_ge(y_turned, g - 1)
                nc.scalar.activation(yT[:, g % 2, :], pH[g % 2][:, :], ACT.Copy).then_inc(yT_ready, 1)

            act_e.wait_ge(consts_loaded, 16)
            act_e.wait_ge(dve_consts, 1)
            take_queries(0)
            take_gates(0)
            row_factors(0)
            for b in range(STEPS):
                i = b // 2
                if b < BATCH:
                    decay(2 * b)
                if b % 2 == 1 and i >= 2 and i - 2 < PAIRS:
                    take_gateT(i - 2)
                if b % 2 == 0 and i >= 2 and i - 2 < PAIRS:
                    router_exp(i - 2)
                if 1 <= b <= BATCH:
                    head_rstd(b - 1)
                if b % 2 == 0 and i + 1 < PAIRS:
                    take_queries(i + 1)
                if b < BATCH:
                    decay(2 * b + 1)
                    take_heads(2 * b)
                    take_heads(2 * b + 1)
                if b % 2 == 0 and i + 1 < PAIRS:
                    take_gates(i + 1)
                    row_factors(i + 1)
                if b % 2 == 1 and 1 <= i <= PAIRS:
                    take_x2(i - 1)

            for n in range(PAIRS * CHUNKS):
                g, c = divmod(n, CHUNKS)
                act_e.wait_ge(up_in_psum, n + 1)
                if c == EXPERTS // 2:
                    act_e.wait_ge(down_done, n - 1)
                    nc.scalar.activation(gact[:, n % 2, :], up_bank(n), ACT.Gelu).then_inc(gelu_ready, 1)
                else:
                    if n >= 2:
                        act_e.wait_ge(gact_ready, routed(n - 2))
                    nc.scalar.activation(act[:, n % 2, :], up_bank(n), ACT.Gelu).then_inc(gelu_ready, 1)
                if c == 1 and g:
                    take_y(g - 1)
            take_y(PAIRS - 1)

        @block.tensor
        def _(pe):
            def turn_queries(i):
                pe.wait_ge(xhat_ready, i + 1)
                if 1 <= i <= 2:
                    pe.wait_ge(rows_read, i)
                if i >= 3:
                    pe.wait_ge(router_steps, ROUTER_STEPS * (i - 3) + R_DIF)
                for k in range(PTILES):
                    last = nc.tensor.transpose(pS[:, k * P:(k + 1) * P], xhat[:, k, :], ident)
                last.then_inc(qT_in_psum, 1)

            def gates(i):
                pe.wait_ge(qT_ready, i + 1)
                pe.wait_ge(ctxT_loaded[i], 16)
                for bb in range(2):
                    w = slice(bb * 48, bb * 48 + 48)
                    nc.tensor.matmul(pS[0:48, 0:SEQ], const("gwq")[:, w], qT[:, i % 2, bb * SEQ:(bb + 1) * SEQ],
                                     start=(bb == 0), stop=False)
                    a = i * PTOK + bb * SEQ
                    last = nc.tensor.matmul(pS[0:48, 0:SEQ], gwc[:, bb, :], ctxT[:, a:a + SEQ],
                                            start=False, stop=(bb == 1))
                last.then_inc(gates_in_psum, 1)

            def turn_rows(i):
                pe.wait_ge(row_exps, i + 1)
                if i >= 3:
                    pe.wait_ge(gflat_ready, i - 2)
                for bb in range(2):
                    nc.tensor.matmul(pS[:, bb * P:(bb + 1) * P], const("spread", ROWS)[:, bb * P:(bb + 1) * P],
                                     erow[:, :], start=True, stop=True)
                for k in range(TILES):
                    last = nc.tensor.transpose(pS[:, 256 + 64 * k:256 + 64 * k + 48],
                                               rowq[0:48, k * P:(k + 1) * P], ident[0:48, 0:48])
                last.then_inc(rows_in_psum, 1)

            def exponents(u):
                b, q = divmod(u, 2)
                i, bb = divmod(b, 2)
                pe.wait_ge(split_ready, i + 1)
                if u:
                    pe.wait_ge(exp_done, u)
                for k in range(TILES):
                    for half in range(2):
                        r = bb * HEADS + q * UHEADS + 2 * half
                        nc.tensor.matmul(pE[:, 2 * half:2 * half + 2, k, :], Gst[:, i % 2, k * P:(k + 1) * P],
                                         sel[:, r:r + 2, :], start=(k == 0), stop=False, skip_group_check=True)
                for j in range(UHEADS):
                    last = nc.tensor.matmul(pE[:, j, :, :], sel[:, bb * HEADS + q * UHEADS + j, :],
                                            Mst[:, i % 2, :], start=False, stop=True, skip_group_check=True)
                last.then_inc(E_in_psum, 1)

            def products(u):
                b, q = divmod(u, 2)
                pe.wait_ge(qmask_ready, b + 1)
                if u:
                    pe.wait_ge(C_ready, u)
                for k in range(TILES):
                    t = (2 * b + k) * P
                    for half in range(2):
                        hh = q * UHEADS + 2 * half
                        last = nc.tensor.matmul(pQK[:, 2 * half:2 * half + 2, k, :], ctxT[:, t:t + P],
                                                qmask[:, b % 2, hh:hh + 2, k * P:(k + 1) * P],
                                                start=True, stop=True, skip_group_check=True)
                last.then_inc(QK_in_psum, 1)

            def make_state(b):
                pe.wait_ge(vw_ready, b + 1)
                if b:
                    pe.wait_ge(norm_steps, NORM_STEPS * (b - 1) + N_SCALED)
                nc.tensor.matmul(pT[:, 0:HEADS * VW], ctx_sb[:, 2 * b, :],
                                 vw[:, b % 2, :, :].rearrange("p h v -> p (h v)"), start=True, stop=True
                                 ).then_inc(state_in_psum, 1)

            def heads(u):
                b, q = divmod(u, 2)
                i, bb = divmod(b, 2)
                bank = pH[u % 2]
                pe.wait_ge(C_ready, u + 1)
                pe.wait_ge(state_ready, b + 1)
                if u >= 2:
                    pe.wait_ge(hT_ready, u - 1)
                for j in range(UHEADS):
                    nc.tensor.matmul(bank[32 * j:32 * j + 32, 0:P], vx[:, 2 * b, q * UHEADS + j, :],
                                     C[:, u % 2, j, 0, :], start=True, stop=True, skip_group_check=True)
                nc.tensor.matmul(bank[:, P:2 * P], state[:, b % 2, q * P:(q + 1) * P], qdec[:, i % 2, bb, :],
                                 start=True, stop=False, skip_group_check=True)
                for j in range(UHEADS):
                    last = nc.tensor.matmul(bank[32 * j:32 * j + 32, P:2 * P], vx[:, 2 * b + 1, q * UHEADS + j, :],
                                            C[:, u % 2, j, 1, :], start=False, stop=True, skip_group_check=True)
                last.then_inc(hT_in_psum, 1)

            def turn_heads(u):
                b, q = divmod(u, 2)
                pe.wait_ge(hT_ready, u + 1)
                if q == 0:
                    pe.wait_ge(state_ready, b + 1)
                for k in range(TILES):
                    a = k * 256 + q * P
                    last = nc.tensor.transpose(pT[:, a:a + P], hT[:, u % 2, k * P:(k + 1) * P], ident)
                last.then_inc(h_in_psum, 1)

            def turn_x2(i):
                pe.wait_ge(x2hat_ready, i + 1)
                if i + 2 < PAIRS:
                    pe.wait_ge(rows_read, i + 3)
                elif i >= 1:
                    pe.wait_ge(gflat_ready, i)
                for k in range(PTILES):
                    last = nc.tensor.transpose(pS[:, k * P:(k + 1) * P], x2hat[:, k, :], ident)
                last.then_inc(x2T_in_psum, 1)

            def logits(i):
                pe.wait_ge(x2T_ready, i + 1)
                for k in range(PTILES):
                    a = i * PTOK + k * P
                    last = nc.tensor.matmul(pS[:, k * EXPERTS:(k + 1) * EXPERTS], x2T[:, a:a + P],
                                            const("router"), start=True, stop=True)
                last.then_inc(logits_in_psum, 1)

            def turn_gate(i):
                pe.wait_ge(gate_ready, i + 1)
                if i + 3 < PAIRS:
                    pe.wait_ge(gates_ready, i + 4)
                for k in range(PTILES):
                    last = nc.tensor.transpose(pS[0:EXPERTS, k * P:(k + 1) * P], gate[:, k, :], ident)
                last.then_inc(gate_in_psum, 1)

            pe.wait_ge(consts_loaded, 16)
            turn_queries(0)
            pe.wait_ge(dve_consts, 1)
            gates(0)
            pe.wait_ge(pool_consts, 1)
            turn_rows(0)
            for b in range(STEPS):
                i = b // 2
                if b % 2 == 0 and i >= 2:
                    logits(i - 2)
                if b % 2 == 1 and i >= 2:
                    turn_gate(i - 2)
                if b < BATCH:
                    exponents(2 * b)
                    products(2 * b)
                if b % 2 == 0 and i + 1 < PAIRS:
                    turn_queries(i + 1)
                if b % 2 == 1 and i + 1 < PAIRS:
                    turn_rows(i + 1)
                if b < BATCH:
                    make_state(b)
                    exponents(2 * b + 1)
                    products(2 * b + 1)
                    heads(2 * b)
                    heads(2 * b + 1)
                if b % 2 == 0 and i + 1 < PAIRS:
                    gates(i + 1)
                if b % 2 == 1 and 1 <= i <= PAIRS:
                    turn_x2(i - 1)
                if b < BATCH:
                    turn_heads(2 * b)
                    turn_heads(2 * b + 1)

            def spread_gate(n):
                g, c = divmod(n, CHUNKS)
                pe.wait_ge(gateT_ready, g + 1)
                if n < 2:
                    pe.wait_ge(C_ready, 2 * BATCH)
                else:
                    pe.wait_ge(gact_ready, routed(n - 2))
                nc.tensor.matmul(spread_bank(n), esel[:, 2 * c:2 * c + 2, :].rearrange("p e n -> p (e n)"),
                                 gateT[:, g * PTOK:(g + 1) * PTOK], start=True, stop=True).then_inc(spread_in_psum, 1)

            def up(n):
                g, c = divmod(n, CHUNKS)
                if n >= 2:
                    pe.wait_ge(gelu_ready, n - 1)
                else:
                    pe.wait_ge(exp_done, 2 * BATCH)
                nc.tensor.matmul(up_bank(n), up_sb[:, c * P:(c + 1) * P], x2T[:, g * PTOK:(g + 1) * PTOK],
                                 start=True, stop=True).then_inc(up_in_psum, 1)

            def down(n):
                g, c = divmod(n, CHUNKS)
                if c == EXPERTS // 2:
                    pe.wait_ge(gelu_ready, n + 1)
                else:
                    pe.wait_ge(gact_ready, routed(n))
                if c == 0:
                    pe.wait_ge(hT_ready, 2 * BATCH)
                    if g >= 2:
                        pe.wait_ge(yT_ready, g - 1)
                last = nc.tensor.matmul(pH[g % 2][:, :], down_sb[:, c, :], gact[:, n % 2, :],
                                        start=(c == 0), stop=(c == CHUNKS - 1))
                last.then_inc(down_done, 1)

            def turn_y(g):
                pe.wait_ge(yT_ready, g + 1)
                if g:
                    pe.wait_ge(res_ready, g)
                for k in range(PTILES):
                    last = nc.tensor.transpose(pS[:, k * P:(k + 1) * P], yT[:, g % 2, k * P:(k + 1) * P], ident)
                last.then_inc(y_turned, 1)

            pe.wait_ge(weights_loaded, 32)
            pe.wait_ge(gflat_ready, PAIRS)
            for n in range(PAIRS * CHUNKS + 1):
                g, c = divmod(n, CHUNKS)
                if n < PAIRS * CHUNKS:
                    if c < EXPERTS // 2:
                        spread_gate(n)
                    up(n)
                if n:
                    down(n - 1)
                if c == 3 and g:
                    turn_y(g - 1)
            turn_y(PAIRS - 1)

        @block.vector
        def _(dve):
            def first_stats(i):
                dve.wait_ge(x_loaded[i], 16)
                for k in range(PTILES):
                    last = nc.vector.bn_stats(st1[:, k, :], x_sb[:, i * PTILES + k, :])
                last.then_inc(ln1_stats, 1)
                dve.wait_ge(ln1_stats, i + 1)
                if i:
                    dve.wait_ge(ln1_rstd, i)
                for k in range(PTILES):
                    last = nc.vector.bn_aggr(mv1[:, k, :], st1[:, k, :])
                last.then_inc(ln1_moments, 1)

            def first_norm(i):
                dve.wait_ge(ln1_rstd, i + 1)
                if i:
                    dve.wait_ge(qT_in_psum, i)
                for k in range(PTILES):
                    last = nc.vector.tensor_scalar(xhat[:, k, :], x_sb[:, i * PTILES + k, :], mv1[:, k, 0:1],
                                                   rstd1[:, k:k + 1], ALU.subtract, ALU.mult)
                last.then_inc(xhat_ready, 1)

            def gate_rows(i):
                base = GATE_STEPS * i
                dve.wait_ge(gates_ready, i + 1)
                nc.vector.tensor_scalar(zmin[:, :], z[:, :], 0.0, None, ALU.min).then_inc(gate_steps, 1)
                dve.wait_ge(gate_steps, base + MIN_STEP)
                dve.wait_ge(softplus_steps, 3 * i + 3)
                nc.vector.tensor_tensor_scan(Frow[:, :], zmin[:, :], soft[:, :], 0.0, ALU.add,
                                             ALU.subtract).then_inc(gate_steps, 1)
                dve.wait_ge(gate_steps, base + F_STEP)
                if i:
                    dve.wait_ge(row_exps, i)
                nc.vector.tensor_tensor(Grow[:, :], ig[:, :], Frow[:, :], ALU.subtract).then_inc(gate_steps, 1)
                dve.wait_ge(gate_steps, base + G_STEP)
                nc.vector.tensor_tensor_scan(Mrow[:, :], Grow[:, :], Grow[:, :], LOWEST, ALU.max,
                                             ALU.max).then_inc(gate_steps, 1)
                dve.wait_ge(gate_steps, base + M_STEP)
                nc.vector.tensor_tensor(FM[:, :], Frow[:, :], Mrow[:, :], ALU.add).then_inc(gate_steps, 1)
                nc.vector.tensor_scalar(negc[:, :], Mrow[:, P - 1:P], -1.0, None, ALU.mult).then_inc(gate_steps, 1)
                if i >= 2:
                    dve.wait_ge(E_in_psum, 4 * (i - 1))
                nc.vector.tensor_copy(Gst[0:ROWS, i % 2, :], Grow[:, :])
                nc.vector.tensor_scalar(Mst[0:ROWS, i % 2, :], Mrow[:, :], -1.0, None, ALU.mult).then_inc(split_hi, 1)
                dve.wait_ge(split_hi, i + 1)
                nc.vector.tensor_tensor(Gst[LO:LO + ROWS, i % 2, :], Grow[:, :],
                                        Gst[0:ROWS, i % 2, :].bitcast(F32), ALU.subtract)
                nc.vector.scalar_tensor_tensor(out=Mst[LO:LO + ROWS, i % 2, :], in0=Mrow[:, :], scalar=-1.0,
                                               in1=Mst[0:ROWS, i % 2, :].bitcast(F32), op0=ALU.mult,
                                               op1=ALU.subtract).then_inc(split_ready, 1)

            def read_rows(i):
                dve.wait_ge(rows_in_psum, i + 1)
                if i >= 2:
                    dve.wait_ge(hT_in_psum, 4 * (i - 1))
                nc.vector.tensor_tensor(qdec[:, i % 2, :, :], pS[:, 0:2 * P].rearrange("p (b s) -> p b s", b=2),
                                        qT[:, i % 2, :].rearrange("p (b s) -> p b s", b=2)[:, :, P:SEQ], ALU.mult)
                nc.vector.tensor_copy(tokq[:, i % 2, :, :],
                                      pS[:, 256:384].rearrange("p (k c) -> p k c", k=TILES)[:, :, 0:48]
                                      ).then_inc(rows_read, 1)

            def weigh_values(b):
                i, bb = divmod(b, 2)
                dve.wait_ge(rows_read, i + 1)
                dve.wait_ge(vx_zeroed, 1)
                dve.wait_ge(vx_ready, i + 1)
                if b >= 2:
                    dve.wait_ge(state_in_psum, b - 1)
                w = tokq[:, i % 2, 0, bb * HEADS:(bb + 1) * HEADS].unsqueeze(2).to_broadcast([P, HEADS, VW])
                nc.vector.tensor_tensor(vw[:, b % 2, :, :], vx[:, 2 * b, :, :], w, ALU.mult).then_inc(vw_ready, 1)

            def weigh(u):
                dve.wait_ge(QK_in_psum, u + 1)
                dve.wait_ge(D_ready, u + 1)
                if u >= 2:
                    dve.wait_ge(hT_in_psum, u - 1)
                flat = "p h k s -> p (h k s)"
                nc.vector.tensor_tensor(C[:, u % 2, :, :, :].rearrange(flat), pQK[:, :, :, :].rearrange(flat),
                                        D[:, u % 2, :, :, :].rearrange(flat), ALU.mult).then_inc(C_ready, 1)

            def mask_state(b):
                dve.wait_ge(state_in_psum, b + 1)
                if b >= 2:
                    dve.wait_ge(hT_in_psum, 2 * b - 2)
                nc.vector.tensor_tensor(state[:, b % 2, :], pT[:, 0:HEADS * VW], const("blockmask"),
                                        ALU.mult).then_inc(state_ready, 1)

            def norm_heads(b):
                i, bb = divmod(b, 2)
                base = NORM_STEPS * b
                hp = pT[:, :].rearrange("p (n v) -> p n v", v=VW)
                floor = tokq[:, i % 2, :, 32 + bb * HEADS:32 + (bb + 1) * HEADS]
                dve.wait_ge(h_in_psum, 2 * b + 2)
                nrm_rows = nrm[:, :].rearrange("p (k h) -> p k h", k=TILES)
                nsum = hp[:, :, HD].rearrange("p (k h) -> p k h", k=TILES)
                nc.vector.scalar_tensor_tensor(out=nrm_rows, in0=nsum, scalar=-1.0, in1=floor, op0=ALU.mult,
                                               op1=ALU.max).then_inc(norm_steps, 1)
                dve.wait_ge(norm_steps, base + N_NEG)
                nc.vector.tensor_tensor(nrm2[:, :].rearrange("p (k h) -> p k h", k=TILES), nsum, nrm_rows,
                                        ALU.max).then_inc(norm_steps, 1)
                dve.wait_ge(norm_steps, base + N_MAX)
                nc.vector.tensor_scalar(nrm3[:, :], nrm2[:, :], EPS_NORMALIZER, None, ALU.add).then_inc(norm_steps, 1)
                dve.wait_ge(norm_steps, base + N_EPS)
                nc.vector.reciprocal(rinv[:, :], nrm3[:, :]).then_inc(norm_steps, 1)
                dve.wait_ge(norm_steps, base + N_INV)
                nc.vector.tensor_tensor(h[:, :, :], hp[:, :, 0:HD], rinv[:, :].unsqueeze(2).to_broadcast([P, 16, HD]),
                                        ALU.mult).then_inc(norm_steps, 1)
                dve.wait_ge(norm_steps, base + N_SCALED)
                nc.vector.tensor_reduce(hsum[:, :], h[:, :, :], AX.X, ALU.add).then_inc(norm_steps, 1)
                dve.wait_ge(norm_steps, base + N_SUM)
                if b >= 2:
                    dve.wait_ge(x1_ready, b - 1)
                nc.vector.scalar_tensor_tensor(out=hc[:, b % 2, :, :],
                                               in0=hsum[:, :].unsqueeze(2).to_broadcast([P, 16, HD]),
                                               scalar=-1.0 / HD, in1=h[:, :, :], op0=ALU.mult,
                                               op1=ALU.add).then_inc(norm_steps, 1)
                dve.wait_ge(norm_steps, base + N_CENTRED)
                nc.vector.tensor_tensor(hsq[:, :, :], hc[:, b % 2, :, :], hc[:, b % 2, :, :],
                                        ALU.mult).then_inc(norm_steps, 1)
                dve.wait_ge(norm_steps, base + N_SQUARED)
                nc.vector.tensor_reduce(hvar[:, b % 2, :], hsq[:, :, :], AX.X, ALU.add).then_inc(norm_steps, 1)

            def second_stats(i):
                dve.wait_ge(x1_ready, 2 * i + 2)
                for k in range(PTILES):
                    last = nc.vector.bn_stats(st2[:, k, :], x1[:, i * PTILES + k, :])
                last.then_inc(ln2_stats, 1)
                dve.wait_ge(ln2_stats, i + 1)
                for k in range(PTILES):
                    last = nc.vector.bn_aggr(mv2[:, k, :], st2[:, k, :])
                last.then_inc(ln2_moments, 1)

            def second_norm(i):
                dve.wait_ge(ln2_rstd, i + 1)
                if i:
                    dve.wait_ge(x2T_in_psum, i)
                for k in range(PTILES):
                    last = nc.vector.tensor_scalar(x2hat[:, k, :], x1[:, i * PTILES + k, :], mv2[:, k, 0:1],
                                                   rstd2[:, k:k + 1], ALU.subtract, ALU.mult)
                last.then_inc(x2hat_ready, 1)

            def router_differences(i):
                base = ROUTER_STEPS * i
                logit = pS[:, 0:PTILES * EXPERTS].rearrange("p (k e) -> p k e", k=PTILES)
                dve.wait_ge(logits_in_psum, i + 1)
                nc.vector.tensor_reduce(rmax[:, :], logit, AX.X, ALU.max).then_inc(router_steps, 1)
                dve.wait_ge(router_steps, base + R_MAX)
                if i:
                    dve.wait_ge(rexp_ready, i)
                nc.vector.tensor_tensor(rdif[:, :, :], logit, rmax[:, :].unsqueeze(2).to_broadcast([P, PTILES, EXPERTS]),
                                        ALU.subtract).then_inc(router_steps, 1)

            def route(i):
                base = ROUTER_STEPS * i
                wide = [P, PTILES, EXPERTS]
                dve.wait_ge(rexp_ready, i + 1)
                nc.vector.tensor_reduce(rsum[:, :], rexp[:, :, :], AX.X, ALU.add).then_inc(router_steps, 1)
                dve.wait_ge(router_steps, base + R_SUM)
                nc.vector.reciprocal(rrec[:, :], rsum[:, :]).then_inc(router_steps, 1)
                for k in range(PTILES):
                    last = nc.vector.max(top8[:, k, :], rexp[:, k, :])
                last.then_inc(router_steps, 1)
                dve.wait_ge(router_steps, base + R_TOP)
                fourth = top8[:, :, TOPK - 1:TOPK].to_broadcast(wide)
                nc.vector.tensor_tensor(above[:, :, :], rexp[:, :, :], fourth, ALU.is_gt).then_inc(router_steps, 1)
                nc.vector.tensor_tensor(equal[:, :, :], rexp[:, :, :], fourth, ALU.is_equal).then_inc(router_steps, 1)
                dve.wait_ge(router_steps, base + R_EQUAL)
                nc.vector.tensor_reduce(nabove[:, :], above[:, :, :], AX.X, ALU.add).then_inc(router_steps, 1)
                flat = "p k e -> p (k e)"
                nc.vector.tensor_tensor_scan(rank[:, :, :].rearrange(flat), const("reset"),
                                             equal[:, :, :].rearrange(flat), 0.0, ALU.mult,
                                             ALU.add).then_inc(router_steps, 1)
                dve.wait_ge(router_steps, base + R_RANK)
                nc.vector.tensor_tensor(rank2[:, :, :], rank[:, :, :], nabove[:, :].unsqueeze(2).to_broadcast(wide),
                                        ALU.add).then_inc(router_steps, 1)
                dve.wait_ge(router_steps, base + R_PLACE)
                nc.vector.scalar_tensor_tensor(out=ties[:, :, :].rearrange(flat), in0=rank2[:, :, :].rearrange(flat),
                                               scalar=float(TOPK), in1=equal[:, :, :].rearrange(flat), op0=ALU.is_le,
                                               op1=ALU.mult).then_inc(router_steps, 1)
                dve.wait_ge(router_steps, base + R_TIES)
                nc.vector.tensor_tensor(chosen[:, :, :], above[:, :, :], ties[:, :, :], ALU.add).then_inc(router_steps, 1)
                dve.wait_ge(router_steps, base + R_CHOSEN)
                nc.vector.tensor_tensor(prob[:, :, :], chosen[:, :, :], rexp[:, :, :], ALU.mult).then_inc(router_steps, 1)
                dve.wait_ge(router_steps, base + R_PROB)
                if i:
                    dve.wait_ge(gate_in_psum, i)
                nc.vector.tensor_tensor(gate[:, :, :], prob[:, :, :], rrec[:, :].unsqueeze(2).to_broadcast(wide),
                                        ALU.mult).then_inc(gate_ready, 1)

            def split_gate(i):
                cols = slice(i * PTOK, (i + 1) * PTOK)
                dve.wait_ge(gflat_ready, i + 1)
                dve.wait_ge(pool_consts, 2)
                nc.vector.tensor_copy(gateT[0:EXPERTS, cols], gflat[:, :]).then_inc(gate_hi, 1)
                dve.wait_ge(gate_hi, i + 1)
                nc.vector.tensor_tensor(gateT[LO:LO + EXPERTS, cols], gflat[:, :],
                                        gateT[0:EXPERTS, cols].bitcast(F32), ALU.subtract).then_inc(gateT_ready, 1)

            first_stats(0)
            nc.vector.memset(one1[:, :], 1.0)
            nc.vector.memset(eps_head[:, :], EPS_HEAD)
            dve.wait_ge(consts_loaded, 16)
            nc.vector.tensor_tensor(gwc[:, :, :].rearrange("p b c -> p (b c)"), const("gwk"), const("gwv"),
                                    ALU.add).then_inc(dve_consts, 1)
            first_norm(0)
            nc.vector.tensor_copy(sel[:, :, :], const("selcol").unsqueeze(2).to_broadcast([P, ROWS, P]))
            nc.vector.tensor_copy(esel[:, :, :], const("selcol").unsqueeze(2).to_broadcast([P, EXPERTS, HID]))
            dve.wait_ge(pool_consts, 1)
            gate_rows(0)
            read_rows(0)
            for b in range(STEPS):
                i = b // 2
                if b % 2 == 0 and 2 <= i:
                    router_differences(i - 2)
                if b % 2 == 0 and i + 1 < PAIRS:
                    first_stats(i + 1)
                if b % 2 == 1 and 1 <= i <= PAIRS:
                    second_norm(i - 1)
                if b < BATCH:
                    weigh_values(b)
                    weigh(2 * b)
                if b % 2 == 0 and i + 1 < PAIRS:
                    first_norm(i + 1)
                if b % 2 == 1 and i + 1 < PAIRS:
                    read_rows(i + 1)
                if b < BATCH:
                    mask_state(b)
                    weigh(2 * b + 1)
                if b % 2 == 0 and i + 1 < PAIRS:
                    gate_rows(i + 1)
                if b < BATCH:
                    norm_heads(b)
                if b % 2 == 0 and 2 <= i:
                    route(i - 2)
                if b % 2 == 1 and 2 <= i:
                    split_gate(i - 2)
                if b % 2 == 0 and 1 <= i <= PAIRS:
                    second_stats(i - 1)

            def finish(g):
                dve.wait_ge(y_turned, g + 1)
                if g >= 2:
                    dve.wait_ge(stored[g - 2], 16)
                nc.vector.tensor_tensor(res[:, g % 2, :, :], pS[:, :].rearrange("p (k d) -> p k d", k=PTILES),
                                        x1[:, g * PTILES:(g + 1) * PTILES, :], ALU.add).then_inc(res_ready, 1)

            for n in range(PAIRS * CHUNKS):
                g, c = divmod(n, CHUNKS)
                if c < EXPERTS // 2:
                    dve.wait_ge(gelu_ready, n + 1)
                    dve.wait_ge(spread_in_psum, routed(n))
                    if n >= 2:
                        dve.wait_ge(down_done, n - 1)
                    nc.vector.tensor_tensor(gact[:, n % 2, :], spread_bank(n), act[:, n % 2, :],
                                            ALU.mult).then_inc(gact_ready, 1)
                if c == 4 and g:
                    finish(g - 1)
            finish(PAIRS - 1)


def kernel(x, ctx_1024, L0_xattn_igate_w, L0_xattn_igate_b, L0_xattn_fgate_w, L0_xattn_fgate_b,
           L0_xattn_norm_w, L0_ffn_shared_up, L0_ffn_shared_down, L0_ffn_routed_up, L0_ffn_routed_down,
           L0_ffn_router_w):
    import numpy as np
    import concourse.bacc as bacc
    from concourse.bass_utils import run_bass_kernel_spmd

    f32 = np.float32
    tokens = BATCH * SEQ
    x_in = np.ascontiguousarray(np.asarray(x).reshape(tokens, DIM))
    ctx_in = np.ascontiguousarray(np.asarray(ctx_1024).reshape(tokens, DIM))
    igw, fgw = np.asarray(L0_xattn_igate_w), np.asarray(L0_xattn_fgate_w)

    def gate_window(part):
        w = np.zeros((DIM, 2, 48), f32)
        for bb in range(2):
            w[:, bb, bb * HEADS:(bb + 1) * HEADS] = fgw[:, part * DIM:(part + 1) * DIM].T
            w[:, bb, 32 + bb * HEADS:32 + (bb + 1) * HEADS] = igw[:, part * DIM:(part + 1) * DIM].T
        return w.reshape(DIM, 96)

    rows = np.arange(P)
    blockmask = np.zeros((P, HEADS, VW), f32)
    blockmask[rows, rows // HD, :] = 1.0
    headmask = np.zeros((P, HEADS), f32)
    headmask[rows, rows // HD] = HD ** -0.5
    spread = np.zeros((P, 2, P), f32)
    selcol = np.zeros((P, ROWS), f32)
    for r in range(ROWS):
        spread[r, r // HEADS, (r % HEADS) * HD:(r % HEADS + 1) * HD] = HD ** -0.5
        selcol[r, r] = selcol[LO + r, r] = 1.0
    gbias = np.zeros((P, 1), f32)
    for bb in range(2):
        gbias[bb * HEADS:(bb + 1) * HEADS, 0] = np.asarray(L0_xattn_fgate_b)
        gbias[32 + bb * HEADS:32 + (bb + 1) * HEADS, 0] = np.asarray(L0_xattn_igate_b)
    reset = np.ones((P, PTILES, EXPERTS), f32)
    reset[:, :, 0] = 0.0
    parts = {"ident": np.eye(P, dtype=f32), "headmask": headmask, "blockmask": blockmask.reshape(P, -1),
             "spread": spread.reshape(P, -1), "selcol": selcol,
             "normw": np.broadcast_to(np.asarray(L0_xattn_norm_w), (P, DIM)), "reset": reset.reshape(P, -1),
             "gwq": gate_window(0), "gwk": gate_window(1), "gwv": gate_window(2), "gbias": gbias,
             "router": np.asarray(L0_ffn_router_w).T}
    up = np.concatenate([np.asarray(L0_ffn_routed_up).reshape(-1, DIM), np.asarray(L0_ffn_shared_up).reshape(-1, DIM)])
    down = np.concatenate([np.asarray(w).transpose(0, 2, 1).reshape(-1, DIM)
                           for w in (L0_ffn_routed_down, L0_ffn_shared_down)])
    arrays = {
        "x": x_in, "ctx_rows": ctx_in, "ctx_cols": np.ascontiguousarray(ctx_in.T),
        "consts": np.concatenate([parts[name] for name, _ in CONST_PARTS], axis=1),
        "up_w": np.ascontiguousarray(up.T),
        "down_w": np.ascontiguousarray(down.reshape(CHUNKS, P, DIM).transpose(1, 0, 2)),
    }
    nc = bacc.Bacc("TRN2", target_bir_lowering=False, num_devices=1)
    args = [nc.dram_tensor(n, a.shape, mybir.dt.from_np(a.dtype), kind="ExternalInput").ap() for n, a in arrays.items()]
    out = nc.dram_tensor("out", (tokens, DIM), F32, kind="ExternalOutput").ap()
    build(nc, *args, out)
    r = run_bass_kernel_spmd(nc, [arrays], core_ids=[0])
    return r.results[0]["out"].reshape(BATCH, SEQ, DIM)
```

```python
from contextlib import ExitStack

import concourse.bass as bass
from concourse import mybir

P = 128
BATCH, SEQ, DIM = 8, 256, 128
HEADS, HD = 8, 16
TILES = SEQ // P
PAIRS = BATCH // 2
PTILES = 2 * TILES
PTOK = 2 * SEQ
NT = BATCH * TILES
UHEADS = HEADS // 2
VW = 32
ROWS = 2 * HEADS
LO = 32
EXPERTS, TOPK, HID = 16, 4, 64
CHUNKS = EXPERTS // 2 + 1
EPS_LN, EPS_HEAD, EPS_NORMALIZER = 1e-5, 1e-5, 1e-6
LOWEST = -3.0e38

F32 = mybir.dt.float32
F32R = mybir.dt.float32r
ALU = mybir.AluOpType
ACT = mybir.ActivationFunctionType
AX = mybir.AxisListType

CONST_PARTS = [("ident", P), ("blockmask", HEADS * VW), ("spread", 2 * P),
               ("selcol", ROWS), ("normw", DIM), ("reset", PTILES * EXPERTS), ("gwq", 2 * 48),
               ("gwk", 2 * 48), ("gwv", 2 * 48), ("gbias", 1), ("router", EXPERTS)]
CONST_AT, CONSTS = {}, 0
for _name, _width in CONST_PARTS:
    CONST_AT[_name] = (CONSTS, _width)
    CONSTS += _width

MIN_STEP, F_STEP, G_STEP, M_STEP, SUM_STEP, NEGC_STEP, GATE_STEPS = 1, 2, 3, 4, 5, 6, 6
N_NEG, N_MAX, N_EPS, N_INV, N_SCALED, N_SUM, N_CENTRED, N_VAR, NORM_STEPS = 1, 2, 3, 4, 5, 6, 7, 8, 8
(R_SUM, R_INV, R_TOP, R_ABOVE, R_EQUAL, R_NABOVE, R_RANK, R_PLACE, R_TIES, R_CHOSEN,
 R_PROB, ROUTER_STEPS) = 1, 2, 3, 4, 5, 6, 7, 8, 9, 10, 11, 11


def build(nc, x, ctx_rows, ctx_cols, consts, up_w, down_w, out):
    with ExitStack() as stack:
        def sb(name, shape, dt=F32):
            return stack.enter_context(nc.sbuf_tensor(name, shape, dt))

        def sem(name):
            return stack.enter_context(nc.semaphore(name))

        cst = sb("cst", [P, CONSTS])
        x_sb = sb("x_sb", [P, NT, DIM])
        ctx_sb = sb("ctx_sb", [P, NT, DIM])
        ctxT = sb("ctxT", [P, NT * P])
        up_sb = sb("up_sb", [P, CHUNKS * P])
        down_sb = sb("down_sb", [P, CHUNKS, DIM])
        kmask = sb("kmask", [P, 2, HEADS, PTOK])

        def const(name, rows=P):
            a, n = CONST_AT[name]
            return cst[0:rows, a:a + n]

        ident = const("ident")
        sel = sb("sel", [P, ROWS, P], F32R)
        esel = sb("esel", [P, EXPERTS, HID], F32R)
        gwc = sb("gwc", [P, 2, 48])
        gwq4 = sb("gwq4", [P, 2, 48])
        up_hi = sb("up_hi", [P, CHUNKS * P], F32R)
        up_lo = sb("up_lo", [P, CHUNKS * P], F32R)
        down_hi = sb("down_hi", [P, CHUNKS, DIM], F32R)
        down_lo = sb("down_lo", [P, CHUNKS, DIM], F32R)
        power = sb("power", [P, 2 * HEADS])
        st1 = sb("st1", [P, PTILES, 6])
        mv1 = sb("mv1", [P, 2, PTILES, 2])
        logvar1 = sb("logvar1", [P, PTILES])
        rstd1 = sb("rstd1", [P, 2, PTILES])
        shift1 = sb("shift1", [P, 2, PTILES])
        xhat = sb("xhat", [P, PTILES, DIM])
        qT = sb("qT", [P, 2, PTOK])
        z = sb("z", [ROWS, SEQ])
        ig = sb("ig", [ROWS, SEQ])
        zmin = sb("zmin", [ROWS, SEQ])
        soft = sb("soft", [ROWS, SEQ])
        Frow = sb("Frow", [ROWS, SEQ])
        Grow = sb("Grow", [ROWS, SEQ])
        Mrow = sb("Mrow", [ROWS, SEQ])
        FM = sb("FM", [ROWS, SEQ])
        negc = sb("negc", [ROWS, 1])
        rowq = sb("rowq", [48, SEQ])
        erow = sb("erow", [ROWS, P])
        Gst = sb("Gst", [P, 2, SEQ], F32R)
        Mst = sb("Mst", [P, 2, SEQ], F32R)
        tokq = sb("tokq", [P, 2, TILES, 48])
        qdec = sb("qdec", [P, 2, 2, P])
        vx = sb("vx", [P, 2, PTILES, HEADS, VW])
        vw = sb("vw", [P, 2, HEADS, VW])
        state = sb("state", [P, 2, HEADS * VW])
        D = sb("D", [P, 2, UHEADS, TILES, P])
        C = sb("C", [P, 2, UHEADS, TILES, P])
        hT = sb("hT", [P, 2, TILES * P])
        nrm = sb("nrm", [P, 16])
        nrm2 = sb("nrm2", [P, 16])
        nrm3 = sb("nrm3", [P, 16])
        rinv = sb("rinv", [P, 16])
        h = sb("h", [P, 16, HD])
        hsum = sb("hsum", [P, 16])
        hc = sb("hc", [P, 2, 16, HD])
        hsq = sb("hsq", [P, 16, HD])
        hvar = sb("hvar", [P, 2, 16])
        hln = sb("hln", [P, 2, 16])
        hrstd = sb("hrstd", [P, 2, 16])
        y1 = sb("y1", [P, 16, HD])
        y2 = sb("y2", [P, 16, HD])
        x1 = x_sb
        st2 = sb("st2", [P, PTILES, 6])
        mv2 = sb("mv2", [P, PTILES, 2])
        logvar2 = sb("logvar2", [P, PTILES])
        rstd2 = sb("rstd2", [P, PTILES])
        shift2 = sb("shift2", [P, PTILES])
        x2hat = sb("x2hat", [P, PTILES, DIM])
        x2T = sb("x2T", [P, PTOK])
        x2hi = sb("x2hi", [P, NT * P], F32R)
        x2lo = sb("x2lo", [P, NT * P], F32R)
        rmax = sb("rmax", [P, PTILES])
        rdif = sb("rdif", [P, 2, PTILES, EXPERTS])
        rexp = sb("rexp", [P, 2, PTILES, EXPERTS])
        rsum = sb("rsum", [P, PTILES])
        rrec = sb("rrec", [P, PTILES])
        top8 = sb("top8", [P, PTILES, 8])
        above = sb("above", [P, PTILES, EXPERTS])
        equal = sb("equal", [P, PTILES, EXPERTS])
        nabove = sb("nabove", [P, PTILES])
        rank = sb("rank", [P, PTILES, EXPERTS])
        rank2 = sb("rank2", [P, PTILES, EXPERTS])
        ties = sb("ties", [P, PTILES, EXPERTS])
        chosen = sb("chosen", [P, PTILES, EXPERTS])
        prob = sb("prob", [P, PTILES, EXPERTS])
        gate = sb("gate", [P, PTILES, EXPERTS])
        gflat = sb("gflat", [EXPERTS, PTOK])
        gateT = sb("gateT", [P, NT * P], F32R)
        kflat = kmask[:, :, :, :].rearrange("p i h t -> p (i h t)")
        selflat = sel[:, :, :].rearrange("p r s -> p (r s)")

        def spare(slot):
            return kflat[:, slot * PTOK:(slot + 1) * PTOK]

        act = [spare(k) for k in range(2)]
        gact = [spare(2 + k) for k in range(3)]
        yT = [spare(5 + k) for k in range(2)]
        res = [spare(7 + k) for k in range(2)]
        gact_hi = [selflat[:, k * PTOK:(k + 1) * PTOK] for k in range(3)]
        gact_lo = [selflat[:, 3 * PTOK:4 * PTOK], Gst[:, :, :].rearrange("p i s -> p (i s)"),
                   Mst[:, :, :].rearrange("p i s -> p (i s)")]
        one1 = sb("one1", [P, 1])
        eps_head = sb("eps_head", [P, 1])
        eps_ln = sb("eps_ln", [P, 1])

        pE = stack.enter_context(nc.psum_tensor("pE", [P, UHEADS, TILES, P], F32))
        pQK = stack.enter_context(nc.psum_tensor("pQK", [P, UHEADS, TILES, P], F32))
        pH = [stack.enter_context(nc.psum_tensor(f"pH{k}", [P, 512], F32)) for k in range(2)]
        pS = stack.enter_context(nc.psum_tensor("pS", [P, 512], F32))
        pT = stack.enter_context(nc.psum_tensor("pT", [P, 512], F32))

        def up_bank(n):
            return pE[:, 2 * (n % 2):2 * (n % 2) + 2, :, :].rearrange("p h k s -> p (h k s)")

        def spread_bank(n):
            return pQK[:, 2 * (n % 2):2 * (n % 2) + 2, :, :].rearrange("p h k s -> p (h k s)")

        def routed(n):
            g, c = divmod(n, CHUNKS)
            return g * (CHUNKS - 1) + min(c + 1, CHUNKS - 1)

        consts_loaded = sem("consts_loaded")
        weights_loaded = sem("weights_loaded")
        x_loaded = [sem(f"x_loaded{i}") for i in range(PAIRS)]
        ctx_loaded = [sem(f"ctx_loaded{i}") for i in range(PAIRS)]
        ctxT_loaded = [sem(f"ctxT_loaded{i}") for i in range(PAIRS)]
        pool_consts = sem("pool_consts")
        dve_consts = sem("dve_consts")
        vx_zeroed = sem("vx_zeroed")
        vx_ready = sem("vx_ready")
        ln1_stats = sem("ln1_stats")
        ln1_moments = sem("ln1_moments")
        ln1_logvar = sem("ln1_logvar")
        ln1_rstd = sem("ln1_rstd")
        ln1_shift = sem("ln1_shift")
        xhat_ready = sem("xhat_ready")
        qT_in_psum = sem("qT_in_psum")
        qT_ready = sem("qT_ready")
        kmask_zeroed = [sem(f"kmask_zeroed{k}") for k in range(2)]
        kmask_loaded = [sem(f"kmask_loaded{i}") for i in range(PAIRS)]
        gates_in_psum = sem("gates_in_psum")
        gates_ready = sem("gates_ready")
        softplus_steps = sem("softplus_steps")
        gate_steps = sem("gate_steps")
        split_hi = sem("split_hi")
        split_ready = sem("split_ready")
        row_exps = sem("row_exps")
        rows_in_psum = sem("rows_in_psum")
        rows_read = sem("rows_read")
        vw_ready = sem("vw_ready")
        state_in_psum = sem("state_in_psum")
        state_ready = sem("state_ready")
        E_in_psum = sem("E_in_psum")
        QK_in_psum = sem("QK_in_psum")
        exp_done = sem("exp_done")
        D_ready = sem("D_ready")
        C_ready = sem("C_ready")
        hT_in_psum = sem("hT_in_psum")
        hT_ready = sem("hT_ready")
        h_in_psum = sem("h_in_psum")
        norm_steps = sem("norm_steps")
        rstd_steps = sem("rstd_steps")
        hrstd_ready = sem("hrstd_ready")
        squared = sem("squared")
        late_rstd_steps = sem("late_rstd_steps")
        out_steps = sem("out_steps")
        x1_ready = sem("x1_ready")
        ln2_stats = sem("ln2_stats")
        ln2_moments = sem("ln2_moments")
        ln2_logvar = sem("ln2_logvar")
        ln2_rstd = sem("ln2_rstd")
        ln2_late_var = sem("ln2_late_var")
        ln2_late_rstd = sem("ln2_late_rstd")
        ln2_shift = sem("ln2_shift")
        x2hat_ready = sem("x2hat_ready")
        x2T_in_psum = sem("x2T_in_psum")
        x2T_ready = sem("x2T_ready")
        logits_in_psum = sem("logits_in_psum")
        diff_steps = sem("diff_steps")
        router_steps = sem("router_steps")
        rexp_ready = sem("rexp_ready")
        gate_ready = sem("gate_ready")
        gate_in_psum = sem("gate_in_psum")
        gflat_ready = sem("gflat_ready")
        x2lo_ready = sem("x2lo_ready")
        weights_hi = sem("weights_hi")
        weights_lo = sem("weights_lo")
        gateT_ready = sem("gateT_ready")
        spread_in_psum = sem("spread_in_psum")
        up_in_psum = sem("up_in_psum")
        gelu_ready = sem("gelu_ready")
        gact_ready = sem("gact_ready")
        gact_hi_ready = sem("gact_hi_ready")
        gact_lo_ready = sem("gact_lo_ready")
        down_done = sem("down_done")
        yT_ready = sem("yT_ready")
        y_turned = sem("y_turned")
        res_ready = sem("res_ready")
        stored = [sem(f"stored{g}") for g in range(PAIRS)]

        block = stack.enter_context(nc.Block())

        UNITS = 2 * BATCH
        LAST = BATCH - 1
        NCHUNK = PAIRS * CHUNKS
        SLOTS = UNITS + NCHUNK + 3
        SPLIT_FROM = CHUNKS
        LATE = 2
        LAG = 3
        STATS2, RSTD2, SHIFT2, NORM2 = [8, 12, 20, 23], [9, 13, 21, 23], [9, 13, 21, 24], [10, 14, 22, 25]
        TURN_X2, TAKE_X2, LOGITS, DIFFS = [10, 14, 23, 26], [11, 15, 24, 27], [11, 15, 25, 28], [12, 16, 26, 29]
        REXP, ROUTE, TURN_GATE, TAKE_GATE = [12, 16, 30, 30], [13, 19, 31, 32], [15, 21, 32, 34], [16, 21, 32, 34]
        LOW_GATE = [16, 22, 33, 35]
        TAKE_Y = [UNITS + CHUNKS * (g + 1) + LAG - 1 for g in range(PAIRS)]
        TURN_Y = [35] + [s + 1 for s in TAKE_Y[1:]]
        RESIDUAL = [s + 1 for s in TURN_Y]
        PIECES = 3
        PW = CHUNKS * P // PIECES
        down_flat = down_sb[:, :, :].rearrange("p c d -> p (c d)")
        down_hi_flat = down_hi[:, :, :].rearrange("p c d -> p (c d)")
        down_lo_flat = down_lo[:, :, :].rearrange("p c d -> p (c d)")

        def split_piece(k):
            a = slice((k % PIECES) * PW, (k % PIECES + 1) * PW)
            if k < PIECES:
                return up_sb[:, a], up_hi[:, a], up_lo[:, a]
            return down_flat[:, a], down_hi_flat[:, a], down_lo_flat[:, a]

        def down_bank(g):
            return pH[0][:, :] if g % 2 == 0 else pT[:, :]

        gates_psum = pH[1][:, 2 * P:4 * P]
        logits_psum = pH[1][:, 2 * P:2 * P + PTILES * EXPERTS]
        state_psum = pH[0][:, 2 * P:4 * P]

        @block.sync
        def _(sp):
            xr = x.rearrange("(i k p) d -> i p k d", k=PTILES, p=P)
            cr = ctx_rows.rearrange("(i k p) d -> i p k d", k=PTILES, p=P)
            orr = out.rearrange("(i k p) d -> i p k d", k=PTILES, p=P)

            def load_pair(i):
                t = slice(i * PTILES, (i + 1) * PTILES)
                sp.dma_start(x_sb[:, t, :], xr[i]).then_inc(x_loaded[i], 16)
                sp.dma_start(ctxT[:, i * PTOK:(i + 1) * PTOK],
                             ctx_cols[:, i * PTOK:(i + 1) * PTOK]).then_inc(ctxT_loaded[i], 16)
                sp.dma_start(ctx_sb[:, t, :], cr[i]).then_inc(ctx_loaded[i], 16)

            def load_keys(i):
                if i >= 2:
                    sp.wait_ge(QK_in_psum, 4 * (i - 1))
                for h_ in range(HEADS):
                    r = slice(h_ * HD, (h_ + 1) * HD)
                    sp.dma_start(kmask[r, i % 2, h_, :], ctx_cols[r, i * PTOK:(i + 1) * PTOK]
                                 ).then_inc(kmask_loaded[i], 16)

            load_pair(0)
            sp.wait_ge(kmask_zeroed[0], 1)
            sp.wait_ge(kmask_zeroed[1], 1)
            load_keys(0)
            load_pair(1)
            sp.wait_ge(kmask_zeroed[1], 2)
            load_keys(1)
            load_pair(2)
            sp.dma_start(up_sb[:, :], up_w).then_inc(weights_loaded, 16)
            sp.dma_start(down_sb[:, :, :], down_w).then_inc(weights_loaded, 16)
            load_pair(3)
            load_keys(2)
            load_keys(3)
            for g in range(PAIRS):
                sp.wait_ge(res_ready, g + 1)
                sp.dma_start(orr[g], res[g % 2].rearrange("p (k d) -> p k d", k=PTILES)).then_inc(stored[g], 16)
            for g in range(PAIRS):
                sp.wait_ge(stored[g], 16)

        @block.gpsimd
        def _(pool):
            def values(i):
                t = slice(i * PTILES, (i + 1) * PTILES)
                pool.wait_ge(ctx_loaded[i], 16)
                if i >= 2:
                    pool.wait_ge(hT_in_psum, 4 * (i - 1))
                nc.gpsimd.tensor_copy(vx[:, i % 2, :, :, 0:HD],
                                      ctx_sb[:, t, :].rearrange("p t (h d) -> p t h d", d=HD)).then_inc(vx_ready, 1)

            def causal(u):
                pool.wait_ge(exp_done, u + 1)
                d = D[:, u % 2, :, :, :].rearrange("p h k s -> p (h k) s")
                nc.gpsimd.affine_select(out=d, in_=d, pattern=[[0, UHEADS * TILES], [1, P]],
                                        compare_op=ALU.is_ge, fill=0.0, base=0,
                                        channel_multiplier=-1).then_inc(D_ready, 1)

            def head_rstd_late(b):
                pool.wait_ge(norm_steps, NORM_STEPS * (b + 1))
                nc.gpsimd.tensor_scalar(hln[:, b % 2, :], hvar[:, b % 2, :], 1.0 / HD, EPS_HEAD, ALU.mult,
                                        ALU.add).then_inc(late_rstd_steps, 1)
                pool.wait_ge(late_rstd_steps, 1)
                nc.gpsimd.tensor_tensor(hrstd[:, b % 2, :], hln[:, b % 2, :], power[:, :], ALU.pow
                                        ).then_inc(late_rstd_steps, 1)

            def finish(b):
                if b < LAST:
                    pool.wait_ge(hrstd_ready, b + 1)
                else:
                    pool.wait_ge(late_rstd_steps, 2)
                if b:
                    pool.wait_ge(x1_ready, b)
                nc.gpsimd.tensor_tensor(y1[:, :, :], hc[:, b % 2, :, :],
                                        hrstd[:, b % 2, :].unsqueeze(2).to_broadcast([P, 16, HD]),
                                        ALU.mult).then_inc(out_steps, 1)
                pool.wait_ge(out_steps, 2 * b + 1)
                w = const("normw").unsqueeze(1).to_broadcast([P, TILES, DIM])
                nc.gpsimd.tensor_tensor(y2[:, :, :].rearrange("p (k h) d -> p k (h d)", k=TILES),
                                        y1[:, :, :].rearrange("p (k h) d -> p k (h d)", k=TILES), w,
                                        ALU.mult).then_inc(out_steps, 1)
                pool.wait_ge(out_steps, 2 * b + 2)
                t = slice(2 * b, 2 * b + 2)
                nc.gpsimd.tensor_tensor(x1[:, t, :], y2[:, :, :].rearrange("p (k h) d -> p k (h d)", k=TILES),
                                        x_sb[:, t, :], ALU.add).then_inc(x1_ready, 1)

            def second_rstd_late(j):
                pool.wait_ge(ln2_moments, j + 1)
                pool.wait_ge(x2hat_ready, j)
                nc.gpsimd.tensor_scalar(logvar2[:, :], mv2[:, :, 1], EPS_LN, None, ALU.add).then_inc(ln2_late_var, 1)
                pool.wait_ge(ln2_late_var, j - LATE + 1)
                nc.gpsimd.tensor_tensor(rstd2[:, :], logvar2[:, :], power[:, 0:PTILES], ALU.pow
                                        ).then_inc(ln2_late_rstd, 1)

            def low_x2(j):
                cols = slice(j * PTOK, (j + 1) * PTOK)
                pool.wait_ge(x2T_ready, j + 1)
                nc.gpsimd.tensor_tensor(x2lo[:, cols], x2T[:, :], x2hi[:, cols].bitcast(F32),
                                        ALU.subtract).then_inc(x2lo_ready, 1)

            def low_weights(k):
                whole, high, low = split_piece(k)
                pool.wait_ge(weights_hi, k + 1)
                nc.gpsimd.tensor_tensor(low, whole, high.bitcast(F32), ALU.subtract).then_inc(weights_lo, 1)

            def low_gact(n):
                pool.wait_ge(gact_hi_ready, n - SPLIT_FROM + 1)
                nc.gpsimd.tensor_tensor(gact_lo[n % 3], gact[n % 3], gact_hi[n % 3].bitcast(F32),
                                        ALU.subtract).then_inc(gact_lo_ready, 1)

            nc.gpsimd.memset(kmask[:, 0, 0:HEADS // 2, :], 0.0).then_inc(kmask_zeroed[1], 1)
            nc.gpsimd.memset(Gst[:, :, :].bitcast(F32), 0.0)
            nc.gpsimd.memset(Mst[:, :, :].bitcast(F32), 0.0)
            nc.gpsimd.memset(rowq[:, :], 0.0)
            nc.gpsimd.memset(power[:, :], -0.5).then_inc(pool_consts, 1)
            nc.gpsimd.memset(vx[:, :, :, :, HD + 1:], 0.0)
            nc.gpsimd.memset(vx[:, :, :, :, HD:HD + 1], 1.0).then_inc(vx_zeroed, 1)
            values(0)
            nc.gpsimd.memset(kmask[:, 1, :, :], 0.0).then_inc(kmask_zeroed[1], 1)
            causal(0)
            values(1)
            for v in range(SLOTS):
                i, r = divmod(v, 4)
                if v + 1 < UNITS:
                    causal(v + 1)
                if v == 0:
                    nc.gpsimd.memset(gateT[:, :].bitcast(F32), 0.0).then_inc(pool_consts, 1)
                if v % 2 == 0 and (v - 4) // 2 == LAST:
                    head_rstd_late(LAST)
                if v % 2 == 1 and 0 <= (v - 5) // 2 < BATCH:
                    finish((v - 5) // 2)
                if r == 1 and 1 <= i and i + 1 < PAIRS:
                    values(i + 1)
                for j in range(PAIRS):
                    if v == RSTD2[j] and j >= LATE:
                        second_rstd_late(j)
                    if v == TAKE_X2[j]:
                        low_x2(j)
                if 0 <= v - 9 < 2 * PIECES:
                    low_weights(v - 9)
                n = v - UNITS
                if SPLIT_FROM <= n - 1 < NCHUNK:
                    low_gact(n - 1)

        @block.scalar
        def _(act_e):
            def first_rstd(i):
                act_e.wait_ge(ln1_moments, i + 1)
                nc.scalar.activation(logvar1[:, :], mv1[:, i % 2, :, 1], ACT.Ln, bias=eps_ln[:, :]
                                     ).then_inc(ln1_logvar, 1)
                act_e.wait_ge(ln1_logvar, i + 1)
                if i >= 2:
                    act_e.wait_ge(ln1_shift, i - 1)
                nc.scalar.activation(rstd1[:, i % 2, :], logvar1[:, :], ACT.Exp, scale=-0.5).then_inc(ln1_rstd, 1)

            def first_norm(i):
                act_e.wait_ge(ln1_shift, i + 1)
                if i:
                    act_e.wait_ge(qT_in_psum, i)
                for k in range(PTILES):
                    last = nc.scalar.activation(xhat[:, k, :], x_sb[:, i * PTILES + k, :], ACT.Identity,
                                                scale=rstd1[:, i % 2, k:k + 1], bias=shift1[:, i % 2, k:k + 1])
                last.then_inc(xhat_ready, 1)

            def take_queries(i):
                act_e.wait_ge(qT_in_psum, i + 1)
                if i >= 2:
                    act_e.wait_ge(QK_in_psum, 4 * (i - 1))
                    act_e.wait_ge(rows_read, i - 1)
                nc.scalar.activation(qT[:, i % 2, :], pS[:, :], ACT.Copy, scale=HD ** -0.5).then_inc(qT_ready, 1)

            def take_gates(i):
                act_e.wait_ge(gates_in_psum, i + 1)
                if i:
                    act_e.wait_ge(gate_steps, GATE_STEPS * i)
                nc.scalar.activation(z[:, :], gates_psum[0:ROWS, :], ACT.Identity, bias=const("gbias")[0:ROWS, :])
                nc.scalar.activation(ig[:, :], gates_psum[32:32 + ROWS, :], ACT.Identity,
                                     bias=const("gbias")[32:32 + ROWS, :]).then_inc(gates_ready, 1)
                act_e.wait_ge(gates_ready, i + 1)
                nc.scalar.activation(soft[:, :], z[:, :], ACT.Abs).then_inc(softplus_steps, 1)
                act_e.wait_ge(softplus_steps, 3 * i + 1)
                nc.scalar.activation(soft[:, :], soft[:, :], ACT.Exp, scale=-1.0).then_inc(softplus_steps, 1)
                act_e.wait_ge(softplus_steps, 3 * i + 2)
                nc.scalar.activation(soft[:, :], soft[:, :], ACT.Ln, bias=one1[0:ROWS, :]).then_inc(softplus_steps, 1)

            def high_rows(i):
                act_e.wait_ge(gate_steps, GATE_STEPS * i + G_STEP)
                if i == 0:
                    act_e.wait_ge(pool_consts, 1)
                if i >= 2:
                    act_e.wait_ge(E_in_psum, 4 * (i - 1))
                nc.scalar.activation(Gst[0:ROWS, i % 2, :], Grow[:, :], ACT.Copy).then_inc(split_hi, 1)
                act_e.wait_ge(gate_steps, GATE_STEPS * i + M_STEP)
                nc.scalar.activation(Mst[0:ROWS, i % 2, :], Mrow[:, :], ACT.Copy, scale=-1.0).then_inc(split_hi, 1)

            def row_factors(i):
                act_e.wait_ge(gate_steps, GATE_STEPS * i + NEGC_STEP)
                if i:
                    act_e.wait_ge(rows_in_psum, i)
                nc.scalar.activation(rowq[0:ROWS, 0:P], Grow[:, 0:P], ACT.Exp, bias=negc[:, :])
                nc.scalar.activation(rowq[32:32 + ROWS, :], FM[:, :], ACT.Exp, scale=-1.0)
                nc.scalar.activation(erow[:, :], Mrow[:, P:SEQ], ACT.Exp, scale=-1.0,
                                     bias=Mrow[:, P - 1:P]).then_inc(row_exps, 1)

            def decay(u):
                act_e.wait_ge(E_in_psum, u + 1)
                if u >= 2:
                    act_e.wait_ge(C_ready, u - 1)
                nc.scalar.activation(D[:, u % 2, :, :, :].rearrange("p h k s -> p (h k s)"),
                                     pE[:, :, :, :].rearrange("p h k s -> p (h k s)"), ACT.Exp).then_inc(exp_done, 1)

            def take_heads(u):
                act_e.wait_ge(hT_in_psum, u + 1)
                if u >= 2:
                    act_e.wait_ge(h_in_psum, u - 1)
                nc.scalar.activation(hT[:, u % 2, :], pH[u % 2][:, 0:TILES * P], ACT.Copy).then_inc(hT_ready, 1)

            def square_heads(b):
                act_e.wait_ge(norm_steps, NORM_STEPS * b + N_CENTRED)
                nc.scalar.activation(hsq[:, :, :], hc[:, b % 2, :, :], ACT.Square).then_inc(squared, 1)

            def head_rstd(b):
                act_e.wait_ge(norm_steps, NORM_STEPS * (b + 1))
                if b >= 2:
                    act_e.wait_ge(x1_ready, b - 1)
                nc.scalar.activation(hln[:, b % 2, :], hvar[:, b % 2, :], ACT.Ln, bias=eps_head[:, :], scale=1.0 / HD
                                     ).then_inc(rstd_steps, 1)
                act_e.wait_ge(rstd_steps, b + 1)
                nc.scalar.activation(hrstd[:, b % 2, :], hln[:, b % 2, :], ACT.Exp, scale=-0.5).then_inc(hrstd_ready, 1)

            def second_rstd(j):
                act_e.wait_ge(ln2_moments, j + 1)
                nc.scalar.activation(logvar2[:, :], mv2[:, :, 1], ACT.Ln, bias=eps_ln[:, :]).then_inc(ln2_logvar, 1)
                act_e.wait_ge(ln2_logvar, j + 1)
                nc.scalar.activation(rstd2[:, :], logvar2[:, :], ACT.Exp, scale=-0.5).then_inc(ln2_rstd, 1)

            def second_norm(j):
                act_e.wait_ge(ln2_shift, j + 1)
                if j:
                    act_e.wait_ge(x2T_in_psum, j)
                for k in range(PTILES):
                    last = nc.scalar.activation(x2hat[:, k, :], x1[:, j * PTILES + k, :], ACT.Identity,
                                                scale=rstd2[:, k:k + 1], bias=shift2[:, k:k + 1])
                last.then_inc(x2hat_ready, 1)

            def take_x2(j):
                act_e.wait_ge(x2T_in_psum, j + 1)
                if j:
                    act_e.wait_ge(x2lo_ready, j)
                    act_e.wait_ge(logits_in_psum, j)
                nc.scalar.activation(x2T[:, :], pS[:, :], ACT.Copy)
                nc.scalar.activation(x2hi[:, j * PTOK:(j + 1) * PTOK], pS[:, :], ACT.Copy).then_inc(x2T_ready, 1)

            def router_exp(j):
                act_e.wait_ge(diff_steps, 2 * j + 2)
                if j >= 2:
                    act_e.wait_ge(gate_ready, j - 1)
                nc.scalar.activation(rexp[:, j % 2, :, :], rdif[:, j % 2, :, :], ACT.Exp).then_inc(rexp_ready, 1)

            def take_gateT(j):
                act_e.wait_ge(gate_in_psum, j + 1)
                act_e.wait_ge(pool_consts, 2)
                if j:
                    act_e.wait_ge(gateT_ready, j)
                nc.scalar.activation(gflat[:, :], pS[0:EXPERTS, :], ACT.Copy)
                nc.scalar.activation(gateT[0:EXPERTS, j * PTOK:(j + 1) * PTOK], pS[0:EXPERTS, :], ACT.Copy
                                     ).then_inc(gflat_ready, 1)

            def high_weights(k):
                whole, high, _ = split_piece(k)
                nc.scalar.activation(high, whole, ACT.Copy).then_inc(weights_hi, 1)

            def gelu(n):
                act_e.wait_ge(up_in_psum, n + 1)
                if n % CHUNKS == CHUNKS - 1:
                    if n - 3 < SPLIT_FROM:
                        act_e.wait_ge(down_done, n - 2)
                    else:
                        act_e.wait_ge(gact_lo_ready, n - 3 - SPLIT_FROM + 1)
                    dst = gact[n % 3]
                else:
                    if n >= 2:
                        act_e.wait_ge(gact_ready, routed(n - 2))
                    dst = act[n % 2]
                nc.scalar.activation(dst, up_bank(n), ACT.Gelu).then_inc(gelu_ready, 1)

            def high_gact(n):
                if n % CHUNKS == CHUNKS - 1:
                    act_e.wait_ge(gelu_ready, n + 1)
                else:
                    act_e.wait_ge(gact_ready, routed(n))
                if n - 3 >= SPLIT_FROM:
                    act_e.wait_ge(down_done, n - 2)
                nc.scalar.activation(gact_hi[n % 3], gact[n % 3], ACT.Copy).then_inc(gact_hi_ready, 1)

            def take_y(g):
                act_e.wait_ge(down_done, CHUNKS * (g + 1))
                if g >= 2:
                    act_e.wait_ge(y_turned, g - 1)
                nc.scalar.activation(yT[g % 2], down_bank(g), ACT.Copy).then_inc(yT_ready, 1)

            act_e.dma_start(cst[:, :], consts).then_inc(consts_loaded, 16)
            nc.scalar.preload_act_table_set("natural_log_exp_and_others")
            act_e.wait_ge(dve_consts, 1)
            first_rstd(0)
            first_norm(0)
            take_queries(0)
            take_gates(0)
            high_rows(0)
            row_factors(0)
            decay(0)
            first_rstd(1)
            for v in range(SLOTS):
                i, r = divmod(v, 4)
                n = v - UNITS
                if v == UNITS:
                    take_gateT(0)
                    take_heads(v - 1)
                    head_rstd((v - 4) // 2)
                    router_exp(1)
                    nc.scalar.preload_act_table(ACT.Gelu)
                if v == REXP[LATE]:
                    nc.scalar.preload_act_table_set("natural_log_exp_and_others")
                    for j in range(LATE, PAIRS):
                        router_exp(j)
                    nc.scalar.preload_act_table(ACT.Gelu)
                if v + 1 < UNITS:
                    decay(v + 1)
                for j in range(PAIRS):
                    if v == TAKE_GATE[j] and j:
                        take_gateT(j)
                    if v == NORM2[j]:
                        second_norm(j)
                if r == 1 and i + 1 < PAIRS:
                    take_gates(i + 1)
                if 1 <= v < UNITS:
                    take_heads(v - 1)
                if r == 0 and i + 1 < PAIRS:
                    first_norm(i + 1)
                    take_queries(i + 1)
                if r == 2 and i + 1 < PAIRS:
                    high_rows(i + 1)
                    row_factors(i + 1)
                for j in range(PAIRS):
                    if v == TAKE_X2[j]:
                        take_x2(j)
                if 0 <= n < NCHUNK:
                    gelu(n)
                if r == 3 and i + 2 < PAIRS:
                    first_rstd(i + 2)
                if v % 2 == 1 and 0 <= (v - 3) // 2 < BATCH:
                    square_heads((v - 3) // 2)
                if v % 2 == 0 and 4 <= v < UNITS:
                    head_rstd((v - 4) // 2)
                for j in range(LATE):
                    if v == RSTD2[j]:
                        second_rstd(j)
                if v == REXP[0]:
                    router_exp(0)
                if 0 <= v - 8 < 2 * PIECES:
                    if v == 8:
                        act_e.wait_ge(weights_loaded, 32)
                    high_weights(v - 8)
                if SPLIT_FROM <= n - 1 < NCHUNK:
                    high_gact(n - 1)
                if v in TAKE_Y:
                    take_y(TAKE_Y.index(v))

        @block.tensor
        def _(pe):
            def turn_queries(i):
                pe.wait_ge(xhat_ready, i + 1)
                if i:
                    pe.wait_ge(rows_read, i)
                for k in range(PTILES):
                    last = nc.tensor.transpose(pS[:, k * P:(k + 1) * P], xhat[:, k, :], ident)
                last.then_inc(qT_in_psum, 1)

            def gates(i):
                pe.wait_ge(qT_ready, i + 1)
                pe.wait_ge(ctxT_loaded[i], 16)
                if i >= 2:
                    pe.wait_ge(hT_ready, 4 * (i - 1))
                for bb in range(2):
                    nc.tensor.matmul(gates_psum[0:48, :], gwq4[:, bb, :], qT[:, i % 2, bb * SEQ:(bb + 1) * SEQ],
                                     start=(bb == 0), stop=False)
                    a = i * PTOK + bb * SEQ
                    last = nc.tensor.matmul(gates_psum[0:48, :], gwc[:, bb, :], ctxT[:, a:a + SEQ],
                                            start=False, stop=(bb == 1))
                last.then_inc(gates_in_psum, 1)

            def turn_rows(i):
                pe.wait_ge(row_exps, i + 1)
                if i == 3:
                    pe.wait_ge(x2T_ready, 1)
                for bb in range(2):
                    nc.tensor.matmul(pS[:, bb * P:(bb + 1) * P], const("spread", ROWS)[:, bb * P:(bb + 1) * P],
                                     erow[:, :], start=True, stop=True)
                for k in range(TILES):
                    last = nc.tensor.transpose(pS[:, 256 + 64 * k:256 + 64 * k + 48],
                                               rowq[0:48, k * P:(k + 1) * P], ident[0:48, 0:48])
                last.then_inc(rows_in_psum, 1)

            def exponents(u):
                b, q = divmod(u, 2)
                i, bb = divmod(b, 2)
                pe.wait_ge(split_ready, i + 1)
                if u:
                    pe.wait_ge(exp_done, u)
                for k in range(TILES):
                    for half in range(2):
                        r = bb * HEADS + q * UHEADS + 2 * half
                        nc.tensor.matmul(pE[:, 2 * half:2 * half + 2, k, :], Gst[:, i % 2, k * P:(k + 1) * P],
                                         sel[:, r:r + 2, :], start=(k == 0), stop=False, skip_group_check=True)
                for j in range(UHEADS):
                    last = nc.tensor.matmul(pE[:, j, :, :], sel[:, bb * HEADS + q * UHEADS + j, :],
                                            Mst[:, i % 2, :], start=False, stop=True, skip_group_check=True)
                last.then_inc(E_in_psum, 1)

            def products(u):
                b, q = divmod(u, 2)
                i, bb = divmod(b, 2)
                pe.wait_ge(qT_ready, i + 1)
                pe.wait_ge(kmask_loaded[i], 16 * HEADS)
                if u:
                    pe.wait_ge(C_ready, u)
                for j in range(UHEADS):
                    for k in range(TILES):
                        t = (bb * TILES + k) * P
                        last = nc.tensor.matmul(pQK[:, j, k, :], kmask[:, i % 2, q * UHEADS + j, t:t + P],
                                                qT[:, i % 2, t:t + P], start=True, stop=True, skip_group_check=True)
                last.then_inc(QK_in_psum, 1)

            def make_state(b):
                pe.wait_ge(vw_ready, b + 1)
                if b:
                    pe.wait_ge(hT_ready, 2 * b - 1)
                nc.tensor.matmul(state_psum, ctx_sb[:, 2 * b, :],
                                 vw[:, b % 2, :, :].rearrange("p h v -> p (h v)"), start=True, stop=True
                                 ).then_inc(state_in_psum, 1)

            def heads(u):
                b, q = divmod(u, 2)
                i, bb = divmod(b, 2)
                bank = pH[u % 2]
                pe.wait_ge(C_ready, u + 1)
                pe.wait_ge(state_ready, b + 1)
                if u >= 2:
                    pe.wait_ge(hT_ready, u - 1)
                if u % 4 == 1 and u < 4 * (PAIRS - 1):
                    pe.wait_ge(gates_ready, u // 4 + 2)
                for j in range(LATE):
                    if u == LOGITS[j]:
                        pe.wait_ge(diff_steps, 2 * j + 2)
                t = bb * TILES
                for j in range(UHEADS):
                    nc.tensor.matmul(bank[32 * j:32 * j + 32, 0:P], vx[:, i % 2, t, q * UHEADS + j, :],
                                     C[:, u % 2, j, 0, :], start=True, stop=True, skip_group_check=True)
                nc.tensor.matmul(bank[:, P:2 * P], state[:, b % 2, q * P:(q + 1) * P], qdec[:, i % 2, bb, :],
                                 start=True, stop=False, skip_group_check=True)
                for j in range(UHEADS):
                    last = nc.tensor.matmul(bank[32 * j:32 * j + 32, P:2 * P], vx[:, i % 2, t + 1, q * UHEADS + j, :],
                                            C[:, u % 2, j, 1, :], start=False, stop=True, skip_group_check=True)
                last.then_inc(hT_in_psum, 1)

            def turn_heads(u):
                b, q = divmod(u, 2)
                pe.wait_ge(hT_ready, u + 1)
                if q == 0 and b:
                    pe.wait_ge(norm_steps, NORM_STEPS * (b - 1) + N_SCALED)
                for k in range(TILES):
                    a = k * 256 + q * P
                    last = nc.tensor.transpose(pT[:, a:a + P], hT[:, u % 2, k * P:(k + 1) * P], ident)
                last.then_inc(h_in_psum, 1)

            def turn_x2(j):
                pe.wait_ge(x2hat_ready, j + 1)
                if j == 0:
                    pe.wait_ge(qT_ready, PAIRS)
                elif j == 1:
                    pe.wait_ge(rows_read, PAIRS)
                elif j == 2:
                    pe.wait_ge(gflat_ready, 2)
                else:
                    pe.wait_ge(x2T_ready, 3)
                for k in range(PTILES):
                    last = nc.tensor.transpose(pS[:, k * P:(k + 1) * P], x2hat[:, k, :], ident)
                last.then_inc(x2T_in_psum, 1)

            def logits(j):
                pe.wait_ge(x2T_ready, j + 1)
                pe.wait_ge(hT_ready, LOGITS[j] - 1 if j < LATE else UNITS)
                if j:
                    pe.wait_ge(diff_steps, 2 * j)
                for k in range(PTILES):
                    last = nc.tensor.matmul(logits_psum[:, k * EXPERTS:(k + 1) * EXPERTS], x2T[:, k * P:(k + 1) * P],
                                            const("router"), start=True, stop=True)
                last.then_inc(logits_in_psum, 1)

            def turn_gate(j):
                pe.wait_ge(gate_ready, j + 1)
                if j == 0:
                    pe.wait_ge(x2T_ready, 2)
                elif j == 2:
                    pe.wait_ge(x2T_ready, PAIRS)
                else:
                    pe.wait_ge(gflat_ready, j)
                for k in range(PTILES):
                    last = nc.tensor.transpose(pS[0:EXPERTS, k * P:(k + 1) * P], gate[:, k, :], ident)
                last.then_inc(gate_in_psum, 1)

            def spread_gate(n):
                g, c = divmod(n, CHUNKS)
                pe.wait_ge(gateT_ready, g + 1)
                if n < 2:
                    pe.wait_ge(C_ready, UNITS)
                else:
                    pe.wait_ge(gact_ready, routed(n - 2))
                nc.tensor.matmul(spread_bank(n), esel[:, 2 * c:2 * c + 2, :].rearrange("p e n -> p (e n)"),
                                 gateT[:, g * PTOK:(g + 1) * PTOK], start=True, stop=True).then_inc(spread_in_psum, 1)

            def up(n):
                g, c = divmod(n, CHUNKS)
                w, t = slice(c * P, (c + 1) * P), slice(g * PTOK, (g + 1) * PTOK)
                pe.wait_ge(x2lo_ready, g + 1)
                if n >= 2:
                    pe.wait_ge(gelu_ready, n - 1)
                else:
                    pe.wait_ge(exp_done, UNITS)
                    pe.wait_ge(weights_lo, PIECES)
                nc.tensor.matmul(up_bank(n), up_hi[:, w], x2hi[:, t], start=True, stop=False)
                nc.tensor.matmul(up_bank(n), up_hi[:, w], x2lo[:, t], start=False, stop=False)
                nc.tensor.matmul(up_bank(n), up_lo[:, w], x2hi[:, t], start=False, stop=True).then_inc(up_in_psum, 1)

            def down(n):
                g, c = divmod(n, CHUNKS)
                first, final = c == 0, c == CHUNKS - 1
                bank = down_bank(g)
                if n < SPLIT_FROM:
                    if final:
                        pe.wait_ge(gelu_ready, n + 1)
                    else:
                        pe.wait_ge(gact_ready, routed(n))
                else:
                    pe.wait_ge(gact_hi_ready, n - SPLIT_FROM + 1)
                    pe.wait_ge(gact_lo_ready, n - SPLIT_FROM + 1)
                    pe.wait_ge(weights_lo, 2 * PIECES)
                if first:
                    pe.wait_ge(hT_ready, UNITS)
                    pe.wait_ge(norm_steps, NORM_STEPS * LAST + N_SCALED)
                    if g >= 2:
                        pe.wait_ge(yT_ready, g - 1)
                if n < SPLIT_FROM:
                    last = nc.tensor.matmul(bank, down_sb[:, c, :], gact[n % 3], start=first, stop=final)
                else:
                    nc.tensor.matmul(bank, down_hi[:, c, :], gact_hi[n % 3], start=first, stop=False)
                    nc.tensor.matmul(bank, down_lo[:, c, :], gact_hi[n % 3], start=False, stop=False)
                    last = nc.tensor.matmul(bank, down_hi[:, c, :], gact_lo[n % 3], start=False, stop=final)
                last.then_inc(down_done, 1)

            def turn_y(g):
                pe.wait_ge(yT_ready, g + 1)
                if g:
                    pe.wait_ge(res_ready, g)
                else:
                    pe.wait_ge(gflat_ready, PAIRS)
                for k in range(PTILES):
                    last = nc.tensor.transpose(pS[:, k * P:(k + 1) * P], yT[g % 2][:, k * P:(k + 1) * P], ident)
                last.then_inc(y_turned, 1)

            pe.wait_ge(consts_loaded, 16)
            turn_queries(0)
            pe.wait_ge(dve_consts, 2)
            gates(0)
            products(0)
            exponents(0)
            turn_rows(0)
            for v in range(SLOTS):
                i, r = divmod(v, 4)
                if v + 1 < UNITS:
                    exponents(v + 1)
                if v % 2 == 0 and v < UNITS:
                    make_state(v // 2)
                if v % 2 == 1 and 0 <= (v - 3) // 2 < BATCH:
                    turn_heads(v - 3)
                    turn_heads(v - 2)
                if r == 1 and i + 1 < PAIRS:
                    gates(i + 1)
                if 1 <= v <= UNITS:
                    heads(v - 1)
                if v + 1 < UNITS:
                    products(v + 1)
                if r == 0 and i + 1 < PAIRS:
                    turn_queries(i + 1)
                if r == 3 and i + 1 < PAIRS:
                    turn_rows(i + 1)
                for j in range(PAIRS):
                    if v == TURN_GATE[j]:
                        turn_gate(j)
                    if v == TURN_X2[j]:
                        turn_x2(j)
                    if v == LOGITS[j]:
                        logits(j)
                n = v - UNITS
                if 0 <= n < NCHUNK:
                    if n % CHUNKS < CHUNKS - 1:
                        spread_gate(n)
                    up(n)
                if n >= LAG:
                    down(n - LAG)
                if v in TURN_Y:
                    turn_y(TURN_Y.index(v))
            turn_y(PAIRS - 1)

        @block.vector
        def _(dve):
            def first_stats(i):
                dve.wait_ge(x_loaded[i], 16)
                for k in range(PTILES):
                    last = nc.vector.bn_stats(st1[:, k, :], x_sb[:, i * PTILES + k, :])
                last.then_inc(ln1_stats, 1)
                dve.wait_ge(ln1_stats, i + 1)
                if i >= 2:
                    dve.wait_ge(ln1_rstd, i - 1)
                for k in range(PTILES):
                    last = nc.vector.bn_aggr(mv1[:, i % 2, k, :], st1[:, k, :])
                last.then_inc(ln1_moments, 1)

            def first_shift(i):
                dve.wait_ge(ln1_rstd, i + 1)
                if i >= 2:
                    dve.wait_ge(xhat_ready, i - 1)
                nc.vector.scalar_tensor_tensor(out=shift1[:, i % 2, :], in0=mv1[:, i % 2, :, 0], scalar=-1.0,
                                               in1=rstd1[:, i % 2, :], op0=ALU.mult,
                                               op1=ALU.mult).then_inc(ln1_shift, 1)

            def gate_rows(i):
                base = GATE_STEPS * i
                dve.wait_ge(gates_ready, i + 1)
                nc.vector.tensor_scalar(zmin[:, :], z[:, :], 0.0, None, ALU.min).then_inc(gate_steps, 1)
                dve.wait_ge(gate_steps, base + MIN_STEP)
                dve.wait_ge(softplus_steps, 3 * i + 3)
                nc.vector.tensor_tensor_scan(Frow[:, :], zmin[:, :], soft[:, :], 0.0, ALU.add,
                                             ALU.subtract).then_inc(gate_steps, 1)
                dve.wait_ge(gate_steps, base + F_STEP)
                if i:
                    dve.wait_ge(row_exps, i)
                nc.vector.tensor_tensor(Grow[:, :], ig[:, :], Frow[:, :], ALU.subtract).then_inc(gate_steps, 1)
                dve.wait_ge(gate_steps, base + G_STEP)
                nc.vector.tensor_tensor_scan(Mrow[:, :], Grow[:, :], Grow[:, :], LOWEST, ALU.max,
                                             ALU.max).then_inc(gate_steps, 1)
                dve.wait_ge(gate_steps, base + M_STEP)
                nc.vector.tensor_tensor(FM[:, :], Frow[:, :], Mrow[:, :], ALU.add).then_inc(gate_steps, 1)
                nc.vector.tensor_scalar(negc[:, :], Mrow[:, P - 1:P], -1.0, None, ALU.mult).then_inc(gate_steps, 1)
                dve.wait_ge(split_hi, 2 * i + 1)
                nc.vector.tensor_tensor(Gst[LO:LO + ROWS, i % 2, :], Grow[:, :],
                                        Gst[0:ROWS, i % 2, :].bitcast(F32), ALU.subtract)
                dve.wait_ge(split_hi, 2 * i + 2)
                nc.vector.scalar_tensor_tensor(out=Mst[LO:LO + ROWS, i % 2, :], in0=Mrow[:, :], scalar=-1.0,
                                               in1=Mst[0:ROWS, i % 2, :].bitcast(F32), op0=ALU.mult,
                                               op1=ALU.subtract).then_inc(split_ready, 1)

            def read_rows(i):
                dve.wait_ge(rows_in_psum, i + 1)
                if i >= 2:
                    dve.wait_ge(hT_in_psum, 4 * (i - 1))
                nc.vector.tensor_tensor(qdec[:, i % 2, :, :], pS[:, 0:2 * P].rearrange("p (b s) -> p b s", b=2),
                                        qT[:, i % 2, :].rearrange("p (b s) -> p b s", b=2)[:, :, P:SEQ], ALU.mult)
                nc.vector.tensor_copy(tokq[:, i % 2, :, :],
                                      pS[:, 256:384].rearrange("p (k c) -> p k c", k=TILES)[:, :, 0:48]
                                      ).then_inc(rows_read, 1)

            def weigh_values(b):
                i, bb = divmod(b, 2)
                dve.wait_ge(rows_read, i + 1)
                dve.wait_ge(vx_zeroed, 1)
                dve.wait_ge(vx_ready, i + 1)
                if b >= 2:
                    dve.wait_ge(state_in_psum, b - 1)
                w = tokq[:, i % 2, 0, bb * HEADS:(bb + 1) * HEADS].unsqueeze(2).to_broadcast([P, HEADS, VW])
                nc.vector.tensor_tensor(vw[:, b % 2, :, :], vx[:, i % 2, bb * TILES, :, :], w, ALU.mult
                                        ).then_inc(vw_ready, 1)

            def weigh(u):
                dve.wait_ge(QK_in_psum, u + 1)
                dve.wait_ge(D_ready, u + 1)
                if u >= 2:
                    dve.wait_ge(hT_in_psum, u - 1)
                flat = "p h k s -> p (h k s)"
                nc.vector.tensor_tensor(C[:, u % 2, :, :, :].rearrange(flat), pQK[:, :, :, :].rearrange(flat),
                                        D[:, u % 2, :, :, :].rearrange(flat), ALU.mult).then_inc(C_ready, 1)

            def mask_state(b):
                dve.wait_ge(state_in_psum, b + 1)
                if b >= 2:
                    dve.wait_ge(hT_in_psum, 2 * b - 2)
                nc.vector.tensor_tensor(state[:, b % 2, :], state_psum, const("blockmask"),
                                        ALU.mult).then_inc(state_ready, 1)

            def centre_heads(b):
                i, bb = divmod(b, 2)
                base = NORM_STEPS * b
                hp = pT[:, :].rearrange("p (n v) -> p n v", v=VW)
                floor = tokq[:, i % 2, :, 32 + bb * HEADS:32 + (bb + 1) * HEADS]
                dve.wait_ge(h_in_psum, 2 * b + 2)
                nrm_rows = nrm[:, :].rearrange("p (k h) -> p k h", k=TILES)
                nsum = hp[:, :, HD].rearrange("p (k h) -> p k h", k=TILES)
                nc.vector.scalar_tensor_tensor(out=nrm_rows, in0=nsum, scalar=-1.0, in1=floor, op0=ALU.mult,
                                               op1=ALU.max).then_inc(norm_steps, 1)
                dve.wait_ge(norm_steps, base + N_NEG)
                nc.vector.tensor_tensor(nrm2[:, :].rearrange("p (k h) -> p k h", k=TILES), nsum, nrm_rows,
                                        ALU.max).then_inc(norm_steps, 1)
                dve.wait_ge(norm_steps, base + N_MAX)
                nc.vector.tensor_scalar(nrm3[:, :], nrm2[:, :], EPS_NORMALIZER, None, ALU.add).then_inc(norm_steps, 1)
                dve.wait_ge(norm_steps, base + N_EPS)
                nc.vector.reciprocal(rinv[:, :], nrm3[:, :]).then_inc(norm_steps, 1)
                dve.wait_ge(norm_steps, base + N_INV)
                nc.vector.tensor_tensor(h[:, :, :], hp[:, :, 0:HD], rinv[:, :].unsqueeze(2).to_broadcast([P, 16, HD]),
                                        ALU.mult).then_inc(norm_steps, 1)
                dve.wait_ge(norm_steps, base + N_SCALED)
                nc.vector.tensor_reduce(hsum[:, :], h[:, :, :], AX.X, ALU.add).then_inc(norm_steps, 1)
                dve.wait_ge(norm_steps, base + N_SUM)
                if b >= 2:
                    dve.wait_ge(x1_ready, b - 1)
                nc.vector.scalar_tensor_tensor(out=hc[:, b % 2, :, :],
                                               in0=hsum[:, :].unsqueeze(2).to_broadcast([P, 16, HD]),
                                               scalar=-1.0 / HD, in1=h[:, :, :], op0=ALU.mult,
                                               op1=ALU.add).then_inc(norm_steps, 1)

            def head_variance(b):
                dve.wait_ge(squared, b + 1)
                nc.vector.tensor_reduce(hvar[:, b % 2, :], hsq[:, :, :], AX.X, ALU.add).then_inc(norm_steps, 1)

            def second_stats(j):
                dve.wait_ge(x1_ready, 2 * j + 2)
                for k in range(PTILES):
                    last = nc.vector.bn_stats(st2[:, k, :], x1[:, j * PTILES + k, :])
                last.then_inc(ln2_stats, 1)
                dve.wait_ge(ln2_stats, j + 1)
                for k in range(PTILES):
                    last = nc.vector.bn_aggr(mv2[:, k, :], st2[:, k, :])
                last.then_inc(ln2_moments, 1)

            def second_shift(j):
                if j < LATE:
                    dve.wait_ge(ln2_rstd, j + 1)
                else:
                    dve.wait_ge(ln2_late_rstd, j - LATE + 1)
                if j:
                    dve.wait_ge(x2hat_ready, j)
                nc.vector.scalar_tensor_tensor(out=shift2[:, :], in0=mv2[:, :, 0], scalar=-1.0, in1=rstd2[:, :],
                                               op0=ALU.mult, op1=ALU.mult).then_inc(ln2_shift, 1)

            def router_differences(j):
                logit = logits_psum.rearrange("p (k e) -> p k e", k=PTILES)
                dve.wait_ge(logits_in_psum, j + 1)
                nc.vector.tensor_reduce(rmax[:, :], logit, AX.X, ALU.max).then_inc(diff_steps, 1)
                dve.wait_ge(diff_steps, 2 * j + 1)
                if j >= 2:
                    dve.wait_ge(rexp_ready, j - 1)
                nc.vector.tensor_tensor(rdif[:, j % 2, :, :], logit, rmax[:, :].unsqueeze(2).to_broadcast([P, PTILES, EXPERTS]),
                                        ALU.subtract).then_inc(diff_steps, 1)

            def route(i):
                base = ROUTER_STEPS * i
                wide = [P, PTILES, EXPERTS]
                rx = rexp[:, i % 2, :, :]
                dve.wait_ge(rexp_ready, i + 1)
                nc.vector.tensor_reduce(rsum[:, :], rx, AX.X, ALU.add).then_inc(router_steps, 1)
                dve.wait_ge(router_steps, base + R_SUM)
                nc.vector.reciprocal(rrec[:, :], rsum[:, :]).then_inc(router_steps, 1)
                for k in range(PTILES):
                    last = nc.vector.max(top8[:, k, :], rx[:, k, :])
                last.then_inc(router_steps, 1)
                dve.wait_ge(router_steps, base + R_TOP)
                fourth = top8[:, :, TOPK - 1:TOPK].to_broadcast(wide)
                nc.vector.tensor_tensor(above[:, :, :], rx, fourth, ALU.is_gt).then_inc(router_steps, 1)
                nc.vector.tensor_tensor(equal[:, :, :], rx, fourth, ALU.is_equal).then_inc(router_steps, 1)
                dve.wait_ge(router_steps, base + R_EQUAL)
                nc.vector.tensor_reduce(nabove[:, :], above[:, :, :], AX.X, ALU.add).then_inc(router_steps, 1)
                flat = "p k e -> p (k e)"
                nc.vector.tensor_tensor_scan(rank[:, :, :].rearrange(flat), const("reset"),
                                             equal[:, :, :].rearrange(flat), 0.0, ALU.mult,
                                             ALU.add).then_inc(router_steps, 1)
                dve.wait_ge(router_steps, base + R_RANK)
                nc.vector.tensor_tensor(rank2[:, :, :], rank[:, :, :], nabove[:, :].unsqueeze(2).to_broadcast(wide),
                                        ALU.add).then_inc(router_steps, 1)
                dve.wait_ge(router_steps, base + R_PLACE)
                nc.vector.scalar_tensor_tensor(out=ties[:, :, :].rearrange(flat), in0=rank2[:, :, :].rearrange(flat),
                                               scalar=float(TOPK), in1=equal[:, :, :].rearrange(flat), op0=ALU.is_le,
                                               op1=ALU.mult).then_inc(router_steps, 1)
                dve.wait_ge(router_steps, base + R_TIES)
                nc.vector.tensor_tensor(chosen[:, :, :], above[:, :, :], ties[:, :, :], ALU.add).then_inc(router_steps, 1)
                dve.wait_ge(router_steps, base + R_CHOSEN)
                nc.vector.tensor_tensor(prob[:, :, :], chosen[:, :, :], rx, ALU.mult).then_inc(router_steps, 1)
                dve.wait_ge(router_steps, base + R_PROB)
                if i:
                    dve.wait_ge(gate_in_psum, i)
                nc.vector.tensor_tensor(gate[:, :, :], prob[:, :, :], rrec[:, :].unsqueeze(2).to_broadcast(wide),
                                        ALU.mult).then_inc(gate_ready, 1)

            def low_gate(j):
                cols = slice(j * PTOK, (j + 1) * PTOK)
                dve.wait_ge(gflat_ready, j + 1)
                nc.vector.tensor_tensor(gateT[LO:LO + EXPERTS, cols], gflat[:, :],
                                        gateT[0:EXPERTS, cols].bitcast(F32), ALU.subtract).then_inc(gateT_ready, 1)

            def weigh_experts(n):
                dve.wait_ge(gelu_ready, n + 1)
                dve.wait_ge(spread_in_psum, routed(n))
                if 3 <= n < SPLIT_FROM + 3:
                    dve.wait_ge(down_done, n - 2)
                elif n >= 3:
                    dve.wait_ge(gact_lo_ready, n - 3 - SPLIT_FROM + 1)
                nc.vector.tensor_tensor(gact[n % 3], spread_bank(n), act[n % 2], ALU.mult).then_inc(gact_ready, 1)

            def add_residual(g):
                dve.wait_ge(y_turned, g + 1)
                if g >= 2:
                    dve.wait_ge(stored[g - 2], 16)
                nc.vector.tensor_tensor(res[g % 2].rearrange("p (k d) -> p k d", k=PTILES),
                                        pS[:, :].rearrange("p (k d) -> p k d", k=PTILES),
                                        x1[:, g * PTILES:(g + 1) * PTILES, :], ALU.add).then_inc(res_ready, 1)

            nc.vector.memset(one1[:, :], 1.0)
            nc.vector.memset(eps_head[:, :], EPS_HEAD)
            nc.vector.memset(eps_ln[:, :], EPS_LN).then_inc(dve_consts, 1)
            nc.vector.memset(kmask[:, 0, HEADS // 2:HEADS, :], 0.0).then_inc(kmask_zeroed[0], 1)
            first_stats(0)
            dve.wait_ge(consts_loaded, 16)
            first_shift(0)
            nc.vector.tensor_tensor(gwc[:, :, :].rearrange("p b c -> p (b c)"), const("gwk"), const("gwv"), ALU.add)
            nc.vector.tensor_scalar(gwq4[:, :, :].rearrange("p b c -> p (b c)"), const("gwq"), HD ** 0.5, None,
                                    ALU.mult).then_inc(dve_consts, 1)
            nc.vector.tensor_copy(sel[:, :, :], const("selcol").unsqueeze(2).to_broadcast([P, ROWS, P]))
            nc.vector.tensor_copy(esel[:, :, :], const("selcol").unsqueeze(2).to_broadcast([P, EXPERTS, HID]))
            first_stats(1)
            dve.wait_ge(pool_consts, 1)
            gate_rows(0)
            read_rows(0)
            weigh_values(0)
            for v in range(SLOTS):
                i, r = divmod(v, 4)
                n = v - UNITS
                for j in range(LATE):
                    if v == DIFFS[j]:
                        router_differences(j)
                if v < UNITS:
                    weigh(v)
                if 0 < n < NCHUNK and n % CHUNKS < CHUNKS - 1:
                    weigh_experts(n)
                if r == 0 and i + 1 < PAIRS:
                    first_shift(i + 1)
                for j in range(PAIRS):
                    if v == LOW_GATE[j]:
                        low_gate(j)
                    if v == DIFFS[j] and j >= LATE:
                        router_differences(j)
                if r == 2 and i + 1 < PAIRS:
                    gate_rows(i + 1)
                if v % 2 == 0 and v < UNITS:
                    mask_state(v // 2)
                if v % 2 == 0 and 0 <= (v - 4) // 2 < BATCH:
                    head_variance((v - 4) // 2)
                if v % 2 == 1 and 0 <= (v - 3) // 2 < BATCH:
                    centre_heads((v - 3) // 2)
                for j in range(PAIRS):
                    if v == SHIFT2[j]:
                        second_shift(j)
                if r == 3 and i + 1 < PAIRS:
                    read_rows(i + 1)
                if v % 2 == 1 and (v + 1) // 2 < BATCH:
                    weigh_values((v + 1) // 2)
                if r == 3 and i + 2 < PAIRS:
                    first_stats(i + 2)
                for j in range(PAIRS):
                    if v == STATS2[j]:
                        second_stats(j)
                    if v == ROUTE[j]:
                        route(j)
                if v in RESIDUAL:
                    add_residual(RESIDUAL.index(v))
                if n == 0:
                    weigh_experts(n)
            add_residual(PAIRS - 1)


def kernel(x, ctx_1024, L0_xattn_igate_w, L0_xattn_igate_b, L0_xattn_fgate_w, L0_xattn_fgate_b,
           L0_xattn_norm_w, L0_ffn_shared_up, L0_ffn_shared_down, L0_ffn_routed_up, L0_ffn_routed_down,
           L0_ffn_router_w):
    import numpy as np
    import concourse.bacc as bacc
    from concourse.bass_utils import run_bass_kernel_spmd

    f32 = np.float32
    tokens = BATCH * SEQ
    x_in = np.ascontiguousarray(np.asarray(x).reshape(tokens, DIM))
    ctx_in = np.ascontiguousarray(np.asarray(ctx_1024).reshape(tokens, DIM))
    igw, fgw = np.asarray(L0_xattn_igate_w), np.asarray(L0_xattn_fgate_w)

    def gate_window(part):
        w = np.zeros((DIM, 2, 48), f32)
        for bb in range(2):
            w[:, bb, bb * HEADS:(bb + 1) * HEADS] = fgw[:, part * DIM:(part + 1) * DIM].T
            w[:, bb, 32 + bb * HEADS:32 + (bb + 1) * HEADS] = igw[:, part * DIM:(part + 1) * DIM].T
        return w.reshape(DIM, 96)

    rows = np.arange(P)
    blockmask = np.zeros((P, HEADS, VW), f32)
    blockmask[rows, rows // HD, :] = 1.0
    spread = np.zeros((P, 2, P), f32)
    selcol = np.zeros((P, ROWS), f32)
    for r in range(ROWS):
        spread[r, r // HEADS, (r % HEADS) * HD:(r % HEADS + 1) * HD] = 1.0
        selcol[r, r] = selcol[LO + r, r] = 1.0
    gbias = np.zeros((P, 1), f32)
    for bb in range(2):
        gbias[bb * HEADS:(bb + 1) * HEADS, 0] = np.asarray(L0_xattn_fgate_b)
        gbias[32 + bb * HEADS:32 + (bb + 1) * HEADS, 0] = np.asarray(L0_xattn_igate_b)
    reset = np.ones((P, PTILES, EXPERTS), f32)
    reset[:, :, 0] = 0.0
    parts = {"ident": np.eye(P, dtype=f32), "blockmask": blockmask.reshape(P, -1),
             "spread": spread.reshape(P, -1), "selcol": selcol,
             "normw": np.broadcast_to(np.asarray(L0_xattn_norm_w), (P, DIM)), "reset": reset.reshape(P, -1),
             "gwq": gate_window(0), "gwk": gate_window(1), "gwv": gate_window(2), "gbias": gbias,
             "router": np.asarray(L0_ffn_router_w).T}
    up = np.concatenate([np.asarray(L0_ffn_routed_up).reshape(-1, DIM), np.asarray(L0_ffn_shared_up).reshape(-1, DIM)])
    down = np.concatenate([np.asarray(w).transpose(0, 2, 1).reshape(-1, DIM)
                           for w in (L0_ffn_routed_down, L0_ffn_shared_down)])
    arrays = {
        "x": x_in, "ctx_rows": ctx_in, "ctx_cols": np.ascontiguousarray(ctx_in.T),
        "consts": np.concatenate([parts[name] for name, _ in CONST_PARTS], axis=1),
        "up_w": np.ascontiguousarray(up.T),
        "down_w": np.ascontiguousarray(down.reshape(CHUNKS, P, DIM).transpose(1, 0, 2)),
    }
    nc = bacc.Bacc("TRN2", target_bir_lowering=False, num_devices=1)
    args = [nc.dram_tensor(n, a.shape, mybir.dt.from_np(a.dtype), kind="ExternalInput").ap() for n, a in arrays.items()]
    out = nc.dram_tensor("out", (tokens, DIM), F32, kind="ExternalOutput").ap()
    build(nc, *args, out)
    r = run_bass_kernel_spmd(nc, [arrays], core_ids=[0])
    return r.results[0]["out"].reshape(BATCH, SEQ, DIM)
```

```python
from contextlib import ExitStack

import concourse.bass as bass
from concourse import mybir

P = 128
BATCH, SEQ, DIM = 8, 256, 128
HEADS, HD = 8, 16
TILES = SEQ // P
PAIRS = BATCH // 2
PTILES = 2 * TILES
PTOK = 2 * SEQ
NT = BATCH * TILES
UHEADS = HEADS // 2
VW = 32
ROWS = 2 * HEADS
LO = 32
EXPERTS, TOPK, HID = 16, 4, 64
CHUNKS = EXPERTS // 2 + 1
EPS_LN, EPS_HEAD, EPS_NORMALIZER = 1e-5, 1e-5, 1e-6
LOWEST = -3.0e38

F32 = mybir.dt.float32
F32R = mybir.dt.float32r
ALU = mybir.AluOpType
ACT = mybir.ActivationFunctionType
AX = mybir.AxisListType

CONST_PARTS = [("ident", P), ("blockmask", HEADS * VW), ("spread", 2 * P),
               ("selcol", ROWS), ("normw", DIM), ("reset", PTILES * EXPERTS), ("gwq", 2 * 48),
               ("gwk", 2 * 48), ("gwv", 2 * 48), ("gbias", 1), ("router", EXPERTS)]
CONST_AT, CONSTS = {}, 0
for _name, _width in CONST_PARTS:
    CONST_AT[_name] = (CONSTS, _width)
    CONSTS += _width

MIN_STEP, F_STEP, G_STEP, M_STEP, SUM_STEP, NEGC_STEP, GATE_STEPS = 1, 2, 3, 4, 5, 6, 6
N_NEG, N_MAX, N_EPS, N_INV, N_SCALED, N_SUM, N_CENTRED, N_VAR, NORM_STEPS = 1, 2, 3, 4, 5, 6, 7, 8, 8
(R_SUM, R_TOP, R_INV, R_ABOVE, R_EQUAL, R_NABOVE, R_RANK, R_PLACE, R_TIES, R_CHOSEN,
 R_PROB, ROUTER_STEPS) = 1, 2, 3, 4, 5, 6, 7, 8, 9, 10, 11, 11


def build(nc, x, ctx_rows, ctx_cols, consts, up_w, down_w, out):
    with ExitStack() as stack:
        def sb(name, shape, dt=F32):
            return stack.enter_context(nc.sbuf_tensor(name, shape, dt))

        def sem(name):
            return stack.enter_context(nc.semaphore(name))

        cst = sb("cst", [P, CONSTS])
        x_sb = sb("x_sb", [P, NT, DIM])
        ctx_sb = sb("ctx_sb", [P, NT, DIM])
        ctxT = sb("ctxT", [P, NT * P])
        up_sb = sb("up_sb", [P, CHUNKS * P])
        down_sb = sb("down_sb", [P, CHUNKS, DIM])
        kmask = sb("kmask", [P, 2, HEADS, PTOK])

        def const(name, rows=P):
            a, n = CONST_AT[name]
            return cst[0:rows, a:a + n]

        ident = const("ident")
        sel = sb("sel", [P, ROWS, P], F32R)
        esel = sb("esel", [P, EXPERTS, HID], F32R)
        gwc = sb("gwc", [P, 2, 48])
        gwq4 = sb("gwq4", [P, 2, 48])
        up_hi = sb("up_hi", [P, CHUNKS * P], F32R)
        up_lo = sb("up_lo", [P, CHUNKS * P], F32R)
        down_hi = sb("down_hi", [P, CHUNKS, DIM], F32R)
        down_lo = sb("down_lo", [P, CHUNKS, DIM], F32R)
        power = sb("power", [P, TILES * HEADS])
        st1 = sb("st1", [P, PTILES, 6])
        mv1 = sb("mv1", [P, 2, PTILES, 2])
        logvar1 = sb("logvar1", [P, PTILES])
        rstd1 = sb("rstd1", [P, 2, PTILES])
        shift1 = sb("shift1", [P, 2, PTILES])
        xhat = sb("xhat", [P, PTILES, DIM])
        qT = sb("qT", [P, 2, PTOK])
        z = sb("z", [ROWS, SEQ])
        ig = sb("ig", [ROWS, SEQ])
        zmin = sb("zmin", [ROWS, SEQ])
        soft = sb("soft", [ROWS, SEQ])
        Frow = sb("Frow", [ROWS, SEQ])
        Grow = sb("Grow", [ROWS, SEQ])
        Mrow = sb("Mrow", [ROWS, SEQ])
        FM = sb("FM", [ROWS, SEQ])
        negc = sb("negc", [ROWS, 1])
        rowq = sb("rowq", [48, SEQ])
        erow = sb("erow", [ROWS, P])
        Gst = sb("Gst", [P, 2, SEQ], F32R)
        Mst = sb("Mst", [P, 2, SEQ], F32R)
        tokq = sb("tokq", [P, 2, TILES, 48])
        qdec = sb("qdec", [P, 2, 2, P])
        vx = sb("vx", [P, 2, PTILES, HEADS, VW])
        vw = sb("vw", [P, 2, HEADS, VW])
        state = sb("state", [P, 2, HEADS * VW])
        D = sb("D", [P, 2, UHEADS, TILES, P])
        C = sb("C", [P, 2, UHEADS, TILES, P])
        hT = sb("hT", [P, 2, TILES * P])
        nrm = sb("nrm", [P, 16])
        nrm2 = sb("nrm2", [P, 16])
        nrm3 = sb("nrm3", [P, 16])
        rinv = sb("rinv", [P, 16])
        h = sb("h", [P, 16, HD])
        hsum = sb("hsum", [P, 16])
        hc = sb("hc", [P, 2, 16, HD])
        hsq = sb("hsq", [P, 16, HD])
        hvar = sb("hvar", [P, 2, 16])
        hln = sb("hln", [P, 2, 16])
        hrstd = sb("hrstd", [P, 2, 16])
        y1 = sb("y1", [P, 16, HD])
        y2 = sb("y2", [P, 16, HD])
        x1 = x_sb
        st2 = sb("st2", [P, PTILES, 6])
        mv2 = sb("mv2", [P, PTILES, 2])
        logvar2 = sb("logvar2", [P, PTILES])
        rstd2 = sb("rstd2", [P, PTILES])
        shift2 = sb("shift2", [P, PTILES])
        x2hat = sb("x2hat", [P, 2, PTILES, DIM])
        x2T = sb("x2T", [P, PTOK])
        x2hi = sb("x2hi", [P, NT * P], F32R)
        x2lo = sb("x2lo", [P, NT * P], F32R)
        rmax = sb("rmax", [P, PTILES])
        rdif = sb("rdif", [P, 2, PTILES, EXPERTS])
        rexp = sb("rexp", [P, 2, PTILES, EXPERTS])
        rsum = sb("rsum", [P, PTILES])
        rrec = sb("rrec", [P, PTILES])
        top8 = sb("top8", [P, PTILES, 8])
        above = sb("above", [P, PTILES, EXPERTS])
        equal = sb("equal", [P, PTILES, EXPERTS])
        nabove = sb("nabove", [P, PTILES])
        rank = sb("rank", [P, PTILES, EXPERTS])
        rank2 = sb("rank2", [P, PTILES, EXPERTS])
        ties = sb("ties", [P, PTILES, EXPERTS])
        chosen = sb("chosen", [P, PTILES, EXPERTS])
        prob = sb("prob", [P, PTILES, EXPERTS])
        gate = sb("gate", [P, PTILES, EXPERTS])
        gateT = sb("gateT", [P, NT * P], F32R)
        kflat = kmask[:, :, :, :].rearrange("p i h t -> p (i h t)")
        selflat = sel[:, :, :].rearrange("p r s -> p (r s)")

        def spare(slot):
            return kflat[:, slot * PTOK:(slot + 1) * PTOK]

        act = [spare(k) for k in range(4)]
        gact = [spare(4 + k) for k in range(4)]
        yT = [spare(8 + k) for k in range(2)]
        res = [spare(10 + k) for k in range(2)]
        gact_hi = [selflat[:, k * PTOK:(k + 1) * PTOK] for k in range(3)]
        gact_lo = [selflat[:, 3 * PTOK:4 * PTOK], Gst[:, :, :].rearrange("p i s -> p (i s)"),
                   Mst[:, :, :].rearrange("p i s -> p (i s)")]
        one1 = sb("one1", [P, 1])
        eps_head = sb("eps_head", [P, 1])
        eps_ln = sb("eps_ln", [P, 1])

        pE = stack.enter_context(nc.psum_tensor("pE", [P, UHEADS, TILES, P], F32))
        pQK = stack.enter_context(nc.psum_tensor("pQK", [P, UHEADS, TILES, P], F32))
        pH = [stack.enter_context(nc.psum_tensor(f"pH{k}", [P, 512], F32)) for k in range(2)]
        pS = stack.enter_context(nc.psum_tensor("pS", [P, 512], F32))
        pT = stack.enter_context(nc.psum_tensor("pT", [P, 512], F32))

        def spread_bank(n):
            return pQK[:, 2 * (n % 2):2 * (n % 2) + 2, :, :].rearrange("p h k s -> p (h k s)")

        def routed(n):
            g, c = divmod(n, CHUNKS)
            return g * (CHUNKS - 1) + min(c + 1, CHUNKS - 1)

        consts_loaded = sem("consts_loaded")
        weights_loaded = sem("weights_loaded")
        x_loaded = [sem(f"x_loaded{i}") for i in range(PAIRS)]
        ctx_loaded = [sem(f"ctx_loaded{i}") for i in range(PAIRS)]
        ctxT_loaded = [sem(f"ctxT_loaded{i}") for i in range(PAIRS)]
        pool_consts = sem("pool_consts")
        dve_consts = sem("dve_consts")
        vx_zeroed = sem("vx_zeroed")
        vx_ready = sem("vx_ready")
        ln1_stats = sem("ln1_stats")
        ln1_moments = sem("ln1_moments")
        ln1_logvar = sem("ln1_logvar")
        ln1_rstd = sem("ln1_rstd")
        ln1_shift = sem("ln1_shift")
        xhat_ready = sem("xhat_ready")
        xhat_half = sem("xhat_half")
        D_zeroed = sem("D_zeroed")
        split_G = sem("split_G")
        last_head_var = sem("last_head_var")
        yT_rest = sem("yT_rest")
        qT_in_psum = sem("qT_in_psum")
        qT_ready = sem("qT_ready")
        kmask_zeroed = [sem(f"kmask_zeroed{k}") for k in range(2)]
        kmask_loaded = [sem(f"kmask_loaded{i}") for i in range(PAIRS)]
        gates_in_psum = sem("gates_in_psum")
        gates_ready = sem("gates_ready")
        softplus_steps = sem("softplus_steps")
        gate_steps = sem("gate_steps")
        split_hi = sem("split_hi")
        split_ready = sem("split_ready")
        row_exps = sem("row_exps")
        rows_in_psum = sem("rows_in_psum")
        rows_read = sem("rows_read")
        vw_ready = sem("vw_ready")
        state_in_psum = sem("state_in_psum")
        state_ready = sem("state_ready")
        E_in_psum = sem("E_in_psum")
        QK_in_psum = sem("QK_in_psum")
        exp_done = sem("exp_done")
        D_ready = sem("D_ready")
        C_ready = sem("C_ready")
        hT_in_psum = sem("hT_in_psum")
        hT_ready = sem("hT_ready")
        h_in_psum = sem("h_in_psum")
        norm_steps = sem("norm_steps")
        rstd_steps = sem("rstd_steps")
        hrstd_ready = sem("hrstd_ready")
        squared = sem("squared")
        out_steps = sem("out_steps")
        x1_ready = sem("x1_ready")
        ln2_stats = sem("ln2_stats")
        ln2_moments = sem("ln2_moments")
        ln2_logvar = sem("ln2_logvar")
        ln2_rstd = sem("ln2_rstd")
        ln2_late_var = sem("ln2_late_var")
        ln2_late_rstd = sem("ln2_late_rstd")
        ln2_shift = sem("ln2_shift")
        x2hat_ready = sem("x2hat_ready")
        x2T_in_psum = sem("x2T_in_psum")
        x2T_ready = sem("x2T_ready")
        logits_in_psum = sem("logits_in_psum")
        diff_steps = sem("diff_steps")
        router_steps = sem("router_steps")
        rexp_ready = sem("rexp_ready")
        gate_ready = sem("gate_ready")
        gate_in_psum = sem("gate_in_psum")
        gflat_ready = sem("gflat_ready")
        x2lo_ready = sem("x2lo_ready")
        weights_hi = sem("weights_hi")
        weights_lo = sem("weights_lo")
        gateT_ready = sem("gateT_ready")
        spread_in_psum = sem("spread_in_psum")
        up_in_psum = sem("up_in_psum")
        gelu_ready = sem("gelu_ready")
        gact_ready = sem("gact_ready")
        gact_hi_ready = sem("gact_hi_ready")
        gact_lo_ready = sem("gact_lo_ready")
        down_done = sem("down_done")
        yT_ready = sem("yT_ready")
        y_turned = sem("y_turned")
        res_ready = sem("res_ready")
        stored = [sem(f"stored{g}") for g in range(PAIRS)]

        block = stack.enter_context(nc.Block())

        UNITS = 2 * BATCH
        LAST = BATCH - 1
        NCHUNK = PAIRS * CHUNKS
        SLOTS = UNITS + NCHUNK + 3
        SPLIT_FROM, SPLIT_TO = 4, NCHUNK - 3
        LATE = 2
        LAG = 3
        CLOSING = None
        STATS2, RSTD2, SHIFT2, NORM2 = [8, 12, 15, 20], [8, 12, 17, 22], [9, 13, 17, 23], [10, 14, 19, 23]
        TURN_X2, TAKE_X2, LOGITS, DIFFS = (
            [10, 14, 23, 27], [10, 15, 23, 27], [11, CLOSING, 24, 28], [12, CLOSING, 25, 30])
        REXP, ROUTE_A, ROUTE_B, ROUTE_C = [11, CLOSING, 30, 30], [13, 16, 30, 31], [14, 19, 30, 31], [14, 20, 30, 33]
        TURN_GATE, TAKE_GATE, LOW_GATE = [CLOSING, 21, 32, 35], [CLOSING, 22, 32, 35], [CLOSING, 23, 33, 36]
        TAKE_Y = [UNITS + CHUNKS * (g + 1) + LAG - 1 for g in range(PAIRS)]
        TAKE_Y[0] += 2
        TURN_Y = [37, 41] + [s + 2 for s in TAKE_Y[2:]]
        RESIDUAL = [s + 1 for s in TURN_Y]
        LAST_FINISH = 18
        WARM_UP, WARM_GATES, HOLD = 3, 3, 2
        PIECES = 3
        PW = CHUNKS * P // PIECES
        down_flat = down_sb[:, :, :].rearrange("p c d -> p (c d)")
        down_hi_flat = down_hi[:, :, :].rearrange("p c d -> p (c d)")
        down_lo_flat = down_lo[:, :, :].rearrange("p c d -> p (c d)")

        def split_piece(k):
            a = slice((k % PIECES) * PW, (k % PIECES + 1) * PW)
            if k < PIECES:
                return up_sb[:, a], up_hi[:, a], up_lo[:, a]
            return down_flat[:, a], down_hi_flat[:, a], down_lo_flat[:, a]

        def down_bank(g):
            return pH[0][:, :] if g % 2 == 0 else pT[:, :]

        gates_psum = pH[1][:, 2 * P:4 * P]

        def up_bank(n):
            if n % 3 == 2:
                return pH[1][:, :]
            k = 2 * (n % 3)
            return pE[:, k:k + 2, :, :].rearrange("p h k s -> p (h k s)")

        def logits_psum(j):
            a = 2 * P if j < 2 else 0
            return (pH[1] if j < 2 else pS)[:, a:a + PTILES * EXPERTS]

        state_psum = pH[0][:, 2 * P:4 * P]

        @block.sync
        def _(sp):
            xr = x.rearrange("(i k p) d -> i p k d", k=PTILES, p=P)
            cr = ctx_rows.rearrange("(i k p) d -> i p k d", k=PTILES, p=P)
            orr = out.rearrange("(i k p) d -> i p k d", k=PTILES, p=P)

            def load_pair(i):
                t = slice(i * PTILES, (i + 1) * PTILES)
                sp.dma_start(x_sb[:, t, :], xr[i]).then_inc(x_loaded[i], 16)
                sp.dma_start(ctxT[:, i * PTOK:(i + 1) * PTOK],
                             ctx_cols[:, i * PTOK:(i + 1) * PTOK]).then_inc(ctxT_loaded[i], 16)
                sp.dma_start(ctx_sb[:, t, :], cr[i]).then_inc(ctx_loaded[i], 16)

            def load_keys(i):
                if i >= 2:
                    sp.wait_ge(QK_in_psum, 4 * (i - 1))
                for h_ in range(HEADS):
                    r = slice(h_ * HD, (h_ + 1) * HD)
                    sp.dma_start(kmask[r, i % 2, h_, :], ctx_cols[r, i * PTOK:(i + 1) * PTOK]
                                 ).then_inc(kmask_loaded[i], 16)

            load_pair(0)
            sp.wait_ge(kmask_zeroed[0], 1)
            sp.wait_ge(kmask_zeroed[1], 1)
            load_keys(0)
            load_pair(1)
            sp.wait_ge(kmask_zeroed[1], 2)
            load_keys(1)
            load_pair(2)
            sp.dma_start(up_sb[:, :], up_w).then_inc(weights_loaded, 16)
            sp.dma_start(down_sb[:, :, :], down_w).then_inc(weights_loaded, 16)
            load_pair(3)
            load_keys(2)
            load_keys(3)
            def store(g, tiles):
                sp.dma_start(orr[g][:, tiles, :], res[g % 2].rearrange("p (k d) -> p k d", k=PTILES)[:, tiles, :]
                             ).then_inc(stored[g], 16)

            for g in range(PAIRS - 1):
                sp.wait_ge(res_ready, g + 1)
                store(g, slice(0, PTILES))
            sp.wait_ge(res_ready, PAIRS)
            store(PAIRS - 1, slice(0, PTILES // 2))
            sp.wait_ge(res_ready, PAIRS + 1)
            store(PAIRS - 1, slice(PTILES // 2, PTILES))
            for g in range(PAIRS):
                sp.wait_ge(stored[g], 16 if g < PAIRS - 1 else 32)

        @block.gpsimd
        def _(pool):
            def values(i):
                t = slice(i * PTILES, (i + 1) * PTILES)
                pool.wait_ge(ctx_loaded[i], 16)
                if i >= 2:
                    pool.wait_ge(hT_in_psum, 4 * (i - 1))
                nc.gpsimd.tensor_copy(vx[:, i % 2, :, :, 0:HD],
                                      ctx_sb[:, t, :].rearrange("p t (h d) -> p t h d", d=HD)).then_inc(vx_ready, 1)

            def causal(u):
                pool.wait_ge(exp_done, u + 1)
                d = D[:, u % 2, :, :, :].rearrange("p h k s -> p (h k) s")
                nc.gpsimd.affine_select(out=d, in_=d, pattern=[[0, UHEADS * TILES], [1, P]],
                                        compare_op=ALU.is_ge, fill=0.0, base=0,
                                        channel_multiplier=-1).then_inc(D_ready, 1)

            def finish(b):
                pool.wait_ge(hrstd_ready, b + 1)
                if b:
                    pool.wait_ge(x1_ready, b)
                nc.gpsimd.tensor_tensor(y1[:, :, :], hc[:, b % 2, :, :],
                                        hrstd[:, b % 2, :].unsqueeze(2).to_broadcast([P, 16, HD]),
                                        ALU.mult).then_inc(out_steps, 1)
                pool.wait_ge(out_steps, 2 * b + 1)
                w = const("normw").unsqueeze(1).to_broadcast([P, TILES, DIM])
                nc.gpsimd.tensor_tensor(y2[:, :, :].rearrange("p (k h) d -> p k (h d)", k=TILES),
                                        y1[:, :, :].rearrange("p (k h) d -> p k (h d)", k=TILES), w,
                                        ALU.mult).then_inc(out_steps, 1)
                pool.wait_ge(out_steps, 2 * b + 2)
                t = slice(2 * b, 2 * b + 2)
                nc.gpsimd.tensor_tensor(x1[:, t, :], y2[:, :, :].rearrange("p (k h) d -> p k (h d)", k=TILES),
                                        x_sb[:, t, :], ALU.add).then_inc(x1_ready, 1)

            def last_head_rstd():
                pool.wait_ge(norm_steps, NORM_STEPS * BATCH)
                nc.gpsimd.tensor_scalar(hln[:, LAST % 2, :], hvar[:, LAST % 2, :], 1.0 / HD, EPS_HEAD, ALU.mult, ALU.add
                                        ).then_inc(last_head_var, 1)
                pool.wait_ge(last_head_var, 1)
                nc.gpsimd.tensor_tensor(hrstd[:, LAST % 2, :], hln[:, LAST % 2, :], power[:, :], ALU.pow
                                        ).then_inc(hrstd_ready, 1)

            def second_rstd_late(j):
                pool.wait_ge(ln2_moments, j + 1)
                pool.wait_ge(x2hat_ready, j)
                nc.gpsimd.tensor_scalar(logvar2[:, :], mv2[:, :, 1], EPS_LN, None, ALU.add).then_inc(ln2_late_var, 1)
                pool.wait_ge(ln2_late_var, j - LATE + 1)
                nc.gpsimd.tensor_tensor(rstd2[:, :], logvar2[:, :], power[:, 0:PTILES], ALU.pow
                                        ).then_inc(ln2_late_rstd, 1)

            def low_x2(j):
                cols = slice(j * PTOK, (j + 1) * PTOK)
                pool.wait_ge(x2T_ready, j + 1)
                nc.gpsimd.tensor_tensor(x2lo[:, cols], x2T[:, :], x2hi[:, cols].bitcast(F32),
                                        ALU.subtract).then_inc(x2lo_ready, 1)

            def low_weights(k):
                whole, high, low = split_piece(k)
                pool.wait_ge(weights_hi, k + 1)
                nc.gpsimd.tensor_tensor(low, whole, high.bitcast(F32), ALU.subtract).then_inc(weights_lo, 1)

            def low_gact(n):
                pool.wait_ge(gact_hi_ready, n - SPLIT_FROM + 1)
                nc.gpsimd.tensor_tensor(gact_lo[n % 3], gact[n % 4], gact_hi[n % 3].bitcast(F32),
                                        ALU.subtract).then_inc(gact_lo_ready, 1)

            nc.gpsimd.memset(kmask[:, 0, 0:HEADS // 2, :], 0.0).then_inc(kmask_zeroed[1], 1)
            nc.gpsimd.memset(Gst[:, :, :].bitcast(F32), 0.0)
            nc.gpsimd.memset(Mst[:, :, :].bitcast(F32), 0.0)
            nc.gpsimd.memset(rowq[:, :], 0.0)
            nc.gpsimd.memset(power[:, :], -0.5).then_inc(pool_consts, 1)
            nc.gpsimd.memset(vx[:, :, :, :, HD + 1:], 0.0)
            nc.gpsimd.memset(vx[:, :, :, :, HD:HD + 1], 1.0).then_inc(vx_zeroed, 1)
            values(0)
            nc.gpsimd.memset(kmask[:, 1, :, :], 0.0).then_inc(kmask_zeroed[1], 1)
            causal(0)
            values(1)
            for v in range(SLOTS):
                i, r = divmod(v, 4)
                if v + 1 < UNITS:
                    causal(v + 1)
                if v == 0:
                    nc.gpsimd.memset(gateT[:, :].bitcast(F32), 0.0).then_inc(pool_consts, 1)
                if v == UNITS:
                    finish(LAST - 1)
                if v == LAST_FINISH:
                    last_head_rstd()
                    finish(LAST)
                if v % 2 == 1 and 5 <= v < UNITS:
                    finish((v - 5) // 2)
                if r == 1 and 1 <= i and i + 1 < PAIRS:
                    values(i + 1)
                for j in range(PAIRS):
                    if v == RSTD2[j] and j >= LATE:
                        second_rstd_late(j)
                for j in range(PAIRS):
                    if v == TAKE_X2[j]:
                        low_x2(j)
                if 0 <= v - 9 < 2 * PIECES:
                    low_weights(v - 9)
                n = v - UNITS
                if SPLIT_FROM <= n - 1 < SPLIT_TO:
                    low_gact(n - 1)

        @block.scalar
        def _(act_e):
            def first_rstd(i):
                act_e.wait_ge(ln1_moments, i + 1)
                nc.scalar.activation(logvar1[:, :], mv1[:, i % 2, :, 1], ACT.Ln, bias=eps_ln[:, :]
                                     ).then_inc(ln1_logvar, 1)
                act_e.wait_ge(ln1_logvar, i + 1)
                if i >= 2:
                    act_e.wait_ge(ln1_shift, i - 1)
                nc.scalar.activation(rstd1[:, i % 2, :], logvar1[:, :], ACT.Exp, scale=-0.5).then_inc(ln1_rstd, 1)

            def first_norm(i):
                act_e.wait_ge(ln1_shift, i + 1)
                if i:
                    act_e.wait_ge(qT_in_psum, i)
                for k in range(PTILES if i else PTILES // 2):
                    last = nc.scalar.activation(xhat[:, k, :], x_sb[:, i * PTILES + k, :], ACT.Identity,
                                                scale=rstd1[:, i % 2, k:k + 1], bias=shift1[:, i % 2, k:k + 1])
                last.then_inc(xhat_ready, 1)

            def take_queries(i):
                act_e.wait_ge(qT_in_psum, i + 1)
                if i >= 2:
                    act_e.wait_ge(QK_in_psum, 4 * (i - 1))
                    act_e.wait_ge(rows_read, i - 1)
                nc.scalar.activation(qT[:, i % 2, :], pS[:, :], ACT.Copy, scale=HD ** -0.5).then_inc(qT_ready, 1)

            def take_gates(i):
                act_e.wait_ge(gates_in_psum, i + 1)
                if i:
                    act_e.wait_ge(gate_steps, GATE_STEPS * i)
                nc.scalar.activation(z[:, :], gates_psum[0:ROWS, :], ACT.Identity, bias=const("gbias")[0:ROWS, :])
                nc.scalar.activation(ig[:, :], gates_psum[32:32 + ROWS, :], ACT.Identity,
                                     bias=const("gbias")[32:32 + ROWS, :]).then_inc(gates_ready, 1)
                act_e.wait_ge(gates_ready, i + 1)
                nc.scalar.activation(soft[:, :], z[:, :], ACT.Abs).then_inc(softplus_steps, 1)
                act_e.wait_ge(softplus_steps, 3 * i + 1)
                nc.scalar.activation(soft[:, :], soft[:, :], ACT.Exp, scale=-1.0).then_inc(softplus_steps, 1)
                act_e.wait_ge(softplus_steps, 3 * i + 2)
                nc.scalar.activation(soft[:, :], soft[:, :], ACT.Ln, bias=one1[0:ROWS, :]).then_inc(softplus_steps, 1)

            def high_rows(i):
                act_e.wait_ge(gate_steps, GATE_STEPS * i + G_STEP)
                if i == 0:
                    act_e.wait_ge(pool_consts, 1)
                if i >= 2:
                    act_e.wait_ge(E_in_psum, 4 * (i - 1))
                nc.scalar.activation(Gst[0:ROWS, i % 2, :], Grow[:, :], ACT.Copy).then_inc(split_hi, 1)
                act_e.wait_ge(gate_steps, GATE_STEPS * i + M_STEP)
                nc.scalar.activation(Mst[0:ROWS, i % 2, :], Mrow[:, :], ACT.Copy, scale=-1.0).then_inc(split_hi, 1)

            def row_factors(i):
                act_e.wait_ge(gate_steps, GATE_STEPS * i + NEGC_STEP)
                if i:
                    act_e.wait_ge(rows_in_psum, i)
                nc.scalar.activation(rowq[0:ROWS, 0:P], Grow[:, 0:P], ACT.Exp, bias=negc[:, :])
                nc.scalar.activation(rowq[32:32 + ROWS, :], FM[:, :], ACT.Exp, scale=-1.0)
                nc.scalar.activation(erow[:, :], Mrow[:, P:SEQ], ACT.Exp, scale=-1.0,
                                     bias=Mrow[:, P - 1:P]).then_inc(row_exps, 1)

            def decay(u):
                act_e.wait_ge(E_in_psum, u + 1)
                if u >= 2:
                    act_e.wait_ge(C_ready, u - 1)
                nc.scalar.activation(D[:, u % 2, :, :, :].rearrange("p h k s -> p (h k s)"),
                                     pE[:, :, :, :].rearrange("p h k s -> p (h k s)"), ACT.Exp).then_inc(exp_done, 1)

            def take_heads(u):
                act_e.wait_ge(hT_in_psum, u + 1)
                if u >= 2:
                    act_e.wait_ge(h_in_psum, u - 1)
                nc.scalar.activation(hT[:, u % 2, :], pH[u % 2][:, 0:TILES * P], ACT.Copy).then_inc(hT_ready, 1)

            def square_heads(b):
                act_e.wait_ge(norm_steps, NORM_STEPS * b + N_CENTRED)
                nc.scalar.activation(hsq[:, :, :], hc[:, b % 2, :, :], ACT.Square).then_inc(squared, 1)

            def head_rstd(b):
                act_e.wait_ge(norm_steps, NORM_STEPS * (b + 1))
                if b >= 2:
                    act_e.wait_ge(x1_ready, b - 1)
                nc.scalar.activation(hln[:, b % 2, :], hvar[:, b % 2, :], ACT.Ln, bias=eps_head[:, :], scale=1.0 / HD
                                     ).then_inc(rstd_steps, 1)
                act_e.wait_ge(rstd_steps, b + 1)
                nc.scalar.activation(hrstd[:, b % 2, :], hln[:, b % 2, :], ACT.Exp, scale=-0.5).then_inc(hrstd_ready, 1)

            def second_rstd(j):
                act_e.wait_ge(ln2_moments, j + 1)
                nc.scalar.activation(logvar2[:, :], mv2[:, :, 1], ACT.Ln, bias=eps_ln[:, :]).then_inc(ln2_logvar, 1)
                act_e.wait_ge(ln2_logvar, j + 1)
                nc.scalar.activation(rstd2[:, :], logvar2[:, :], ACT.Exp, scale=-0.5).then_inc(ln2_rstd, 1)

            def second_norm(j, tiles):
                act_e.wait_ge(ln2_shift, j + 1)
                for k in tiles:
                    last = nc.scalar.activation(x2hat[:, j % 2, k, :], x1[:, j * PTILES + k, :], ACT.Identity,
                                                scale=rstd2[:, k:k + 1], bias=shift2[:, k:k + 1])
                if tiles[-1] == PTILES - 1:
                    last.then_inc(x2hat_ready, 1)

            def take_x2(j):
                act_e.wait_ge(x2T_in_psum, j + 1)
                if j:
                    act_e.wait_ge(x2lo_ready, j)
                    act_e.wait_ge(logits_in_psum, j)
                nc.scalar.activation(x2T[:, :], pS[:, :], ACT.Copy)
                nc.scalar.activation(x2hi[:, j * PTOK:(j + 1) * PTOK], pS[:, :], ACT.Copy).then_inc(x2T_ready, 1)

            def router_exp(j):
                act_e.wait_ge(diff_steps, 2 * j + 2)
                if j >= 2:
                    act_e.wait_ge(gate_ready, j - 1)
                nc.scalar.activation(rexp[:, j % 2, :, :], rdif[:, j % 2, :, :], ACT.Exp).then_inc(rexp_ready, 1)

            def take_gateT(j):
                act_e.wait_ge(gate_in_psum, j + 1)
                act_e.wait_ge(pool_consts, 2)
                nc.scalar.activation(gateT[0:EXPERTS, j * PTOK:(j + 1) * PTOK], pS[0:EXPERTS, :], ACT.Copy
                                     ).then_inc(gflat_ready, 1)

            def high_weights(k):
                whole, high, _ = split_piece(k)
                nc.scalar.activation(high, whole, ACT.Copy).then_inc(weights_hi, 1)

            def gelu(n):
                act_e.wait_ge(up_in_psum, n + 1)
                if n % CHUNKS == CHUNKS - 1:
                    if n - 4 < SPLIT_FROM:
                        act_e.wait_ge(down_done, n - 3)
                    else:
                        act_e.wait_ge(gact_lo_ready, n - 4 - SPLIT_FROM + 1)
                    dst = gact[n % 4]
                else:
                    if n >= 4:
                        act_e.wait_ge(gact_ready, routed(n - 4))
                    dst = act[n % 4]
                nc.scalar.activation(dst, up_bank(n), ACT.Gelu).then_inc(gelu_ready, 1)

            def high_gact(n):
                if n % CHUNKS == CHUNKS - 1:
                    act_e.wait_ge(gelu_ready, n + 1)
                else:
                    act_e.wait_ge(gact_ready, routed(n))
                if n - 3 >= SPLIT_FROM:
                    act_e.wait_ge(down_done, n - 2)
                nc.scalar.activation(gact_hi[n % 3], gact[n % 4], ACT.Copy).then_inc(gact_hi_ready, 1)

            def take_y(g):
                act_e.wait_ge(down_done, CHUNKS * (g + 1))
                if g >= 2:
                    act_e.wait_ge(y_turned, g - 1)
                halves = [slice(0, PTOK)] if g < PAIRS - 1 else [slice(0, PTOK // 2), slice(PTOK // 2, PTOK)]
                for cols, done in zip(halves, [yT_ready, yT_rest]):
                    nc.scalar.activation(yT[g % 2][:, cols], down_bank(g)[:, cols], ACT.Copy).then_inc(done, 1)

            act_e.dma_start(cst[:, :], consts).then_inc(consts_loaded, 16)
            nc.scalar.preload_act_table_set("natural_log_exp_and_others")
            act_e.wait_ge(dve_consts, 1)
            first_rstd(0)
            first_norm(0)
            take_queries(0)
            take_gates(0)
            high_rows(0)
            row_factors(0)
            decay(0)
            first_rstd(1)
            for v in range(SLOTS):
                i, r = divmod(v, 4)
                n = v - UNITS
                if v == UNITS:
                    take_heads(v - 1)
                    square_heads(LAST - 1)
                    head_rstd(LAST - 1)
                    router_exp(1)
                    take_gateT(0)
                    nc.scalar.preload_act_table(ACT.Gelu)
                if v + 1 < UNITS:
                    decay(v + 1)
                for j in range(PAIRS):
                    if j < 2 and v == NORM2[j]:
                        second_norm(j, range(PTILES))
                if r == 1 and i + 1 < PAIRS:
                    take_gates(i + 1)
                if 1 <= v < UNITS:
                    take_heads(v - 1)
                if r == 0 and i + 1 < PAIRS:
                    first_norm(i + 1)
                    take_queries(i + 1)
                if r == 2 and i + 1 < PAIRS:
                    high_rows(i + 1)
                    row_factors(i + 1)
                if v < UNITS and v in TAKE_X2:
                    take_x2(TAKE_X2.index(v))
                if 0 <= n < NCHUNK:
                    gelu(n)
                if n == 0:
                    square_heads(LAST)
                if v >= UNITS and v in TAKE_X2:
                    take_x2(TAKE_X2.index(v))
                if v in TAKE_GATE:
                    take_gateT(TAKE_GATE.index(v))
                if r == 1 and i + 2 < PAIRS:
                    first_rstd(i + 2)
                if v % 2 == 1 and 3 <= v < UNITS - 1:
                    square_heads((v - 3) // 2)
                for j in range(2, PAIRS):
                    if 0 <= v - NORM2[j] < PTILES:
                        second_norm(j, [v - NORM2[j]])
                if v % 2 == 0 and 4 <= v < UNITS:
                    head_rstd((v - 4) // 2)
                for j in range(LATE):
                    if v == RSTD2[j]:
                        second_rstd(j)
                if v == REXP[0]:
                    router_exp(0)
                if 0 <= v - 8 < 2 * PIECES:
                    if v == 8:
                        act_e.wait_ge(weights_loaded, 32)
                    high_weights(v - 8)
                if SPLIT_FROM <= n - 1 < SPLIT_TO:
                    high_gact(n - 1)
                if v == REXP[3]:
                    nc.scalar.preload_act_table_set("natural_log_exp_and_others")
                    router_exp(2)
                    router_exp(3)
                    nc.scalar.preload_act_table(ACT.Gelu)
                if v in TAKE_Y:
                    take_y(TAKE_Y.index(v))

        @block.tensor
        def _(pe):
            def turn_queries(i):
                pe.wait_ge(xhat_ready, i + 1)
                if i == 0:
                    pe.wait_ge(xhat_half, 1)
                if i:
                    pe.wait_ge(rows_read, i)
                for k in range(PTILES):
                    last = nc.tensor.transpose(pS[:, k * P:(k + 1) * P], xhat[:, k, :], ident)
                last.then_inc(qT_in_psum, 1)

            def gates(i):
                pe.wait_ge(ctxT_loaded[i], 16)
                if i >= 2:
                    pe.wait_ge(hT_ready, 4 * (i - 1))
                for bb in range(2):
                    a = i * PTOK + bb * SEQ
                    nc.tensor.matmul(gates_psum[0:48, :], gwc[:, bb, :], ctxT[:, a:a + SEQ],
                                     start=(bb == 0), stop=False)
                pe.wait_ge(qT_ready, i + 1)
                for bb in range(2):
                    last = nc.tensor.matmul(gates_psum[0:48, :], gwq4[:, bb, :], qT[:, i % 2, bb * SEQ:(bb + 1) * SEQ],
                                            start=False, stop=(bb == 1))
                last.then_inc(gates_in_psum, 1)

            def turn_rows(i):
                pe.wait_ge(row_exps, i + 1)
                if i == 3:
                    pe.wait_ge(x2T_ready, 1)
                for bb in range(2):
                    nc.tensor.matmul(pS[:, bb * P:(bb + 1) * P], const("spread", ROWS)[:, bb * P:(bb + 1) * P],
                                     erow[:, :], start=True, stop=True)
                for k in range(TILES):
                    last = nc.tensor.transpose(pS[:, 256 + 64 * k:256 + 64 * k + 48],
                                               rowq[0:48, k * P:(k + 1) * P], ident[0:48, 0:48])
                last.then_inc(rows_in_psum, 1)

            def exponents(u):
                b, q = divmod(u, 2)
                i, bb = divmod(b, 2)
                pe.wait_ge(split_G, i + 1)
                if u:
                    pe.wait_ge(exp_done, u)
                for k in range(TILES):
                    for half in range(2):
                        r = bb * HEADS + q * UHEADS + 2 * half
                        nc.tensor.matmul(pE[:, 2 * half:2 * half + 2, k, :], Gst[:, i % 2, k * P:(k + 1) * P],
                                         sel[:, r:r + 2, :], start=(k == 0), stop=False, skip_group_check=True)
                pe.wait_ge(split_ready, i + 1)
                for j in range(UHEADS):
                    last = nc.tensor.matmul(pE[:, j, :, :], sel[:, bb * HEADS + q * UHEADS + j, :],
                                            Mst[:, i % 2, :], start=False, stop=True, skip_group_check=True)
                last.then_inc(E_in_psum, 1)

            def products(u):
                b, q = divmod(u, 2)
                i, bb = divmod(b, 2)
                pe.wait_ge(qT_ready, i + 1)
                pe.wait_ge(kmask_loaded[i], 16 * HEADS)
                if u:
                    pe.wait_ge(C_ready, u)
                for j in range(UHEADS):
                    for k in range(TILES):
                        t = (bb * TILES + k) * P
                        last = nc.tensor.matmul(pQK[:, j, k, :], kmask[:, i % 2, q * UHEADS + j, t:t + P],
                                                qT[:, i % 2, t:t + P], start=True, stop=True, skip_group_check=True)
                last.then_inc(QK_in_psum, 1)

            def make_state(b):
                pe.wait_ge(vw_ready, b + 1)
                if b:
                    pe.wait_ge(hT_ready, 2 * b - 1)
                nc.tensor.matmul(state_psum, ctx_sb[:, 2 * b, :],
                                 vw[:, b % 2, :, :].rearrange("p h v -> p (h v)"), start=True, stop=True
                                 ).then_inc(state_in_psum, 1)

            def heads(u):
                b, q = divmod(u, 2)
                i, bb = divmod(b, 2)
                bank = pH[u % 2]
                pe.wait_ge(C_ready, u + 1)
                pe.wait_ge(state_ready, b + 1)
                if u >= 2:
                    pe.wait_ge(hT_ready, u - 1)
                if u % 4 == 1 and u < 4 * (PAIRS - 1):
                    pe.wait_ge(gates_ready, u // 4 + 2)
                if u == LOGITS[0]:
                    pe.wait_ge(diff_steps, 2)
                t = bb * TILES
                for j in range(UHEADS):
                    nc.tensor.matmul(bank[32 * j:32 * j + 32, 0:P], vx[:, i % 2, t, q * UHEADS + j, :],
                                     C[:, u % 2, j, 0, :], start=True, stop=True, skip_group_check=True)
                nc.tensor.matmul(bank[:, P:2 * P], state[:, b % 2, q * P:(q + 1) * P], qdec[:, i % 2, bb, :],
                                 start=True, stop=False, skip_group_check=True)
                for j in range(UHEADS):
                    last = nc.tensor.matmul(bank[32 * j:32 * j + 32, P:2 * P], vx[:, i % 2, t + 1, q * UHEADS + j, :],
                                            C[:, u % 2, j, 1, :], start=False, stop=True, skip_group_check=True)
                last.then_inc(hT_in_psum, 1)

            def turn_heads(u):
                b, q = divmod(u, 2)
                pe.wait_ge(hT_ready, u + 1)
                if q == 0 and b:
                    pe.wait_ge(norm_steps, NORM_STEPS * (b - 1) + N_SCALED)
                for k in range(TILES):
                    a = k * 256 + q * P
                    last = nc.tensor.transpose(pT[:, a:a + P], hT[:, u % 2, k * P:(k + 1) * P], ident)
                last.then_inc(h_in_psum, 1)

            def turn_x2(j):
                pe.wait_ge(x2hat_ready, j + 1)
                if j == 0:
                    pe.wait_ge(qT_ready, PAIRS)
                elif j == 1:
                    pe.wait_ge(rows_read, PAIRS)
                elif j == 2:
                    pe.wait_ge(gateT_ready, 2)
                else:
                    pe.wait_ge(diff_steps, 2 * j)
                for k in range(PTILES):
                    last = nc.tensor.transpose(pS[:, k * P:(k + 1) * P], x2hat[:, j % 2, k, :], ident)
                last.then_inc(x2T_in_psum, 1)

            def logits(j):
                pe.wait_ge(x2T_ready, j + 1)
                if j < 2:
                    pe.wait_ge(hT_ready, LOGITS[0] - 1 if j == 0 else UNITS)
                if j == 1:
                    pe.wait_ge(diff_steps, 2)
                for k in range(PTILES):
                    last = nc.tensor.matmul(logits_psum(j)[:, k * EXPERTS:(k + 1) * EXPERTS], x2T[:, k * P:(k + 1) * P],
                                            const("router"), start=True, stop=True)
                last.then_inc(logits_in_psum, 1)

            def turn_gate(j):
                pe.wait_ge(gate_ready, j + 1)
                if j == 0:
                    pe.wait_ge(x2T_ready, 2)
                elif j == 2:
                    pe.wait_ge(diff_steps, 2 * PAIRS)
                else:
                    pe.wait_ge(gateT_ready, j)
                for k in range(PTILES):
                    last = nc.tensor.transpose(pS[0:EXPERTS, k * P:(k + 1) * P], gate[:, k, :], ident)
                last.then_inc(gate_in_psum, 1)

            def spread_gate(n):
                g, c = divmod(n, CHUNKS)
                pe.wait_ge(gateT_ready, g + 1)
                if n < 2:
                    pe.wait_ge(C_ready, UNITS)
                else:
                    pe.wait_ge(gact_ready, routed(n - 2))
                nc.tensor.matmul(spread_bank(n), esel[:, 2 * c:2 * c + 2, :].rearrange("p e n -> p (e n)"),
                                 gateT[:, g * PTOK:(g + 1) * PTOK], start=True, stop=True).then_inc(spread_in_psum, 1)

            def up(n):
                g, c = divmod(n, CHUNKS)
                w, t = slice(c * P, (c + 1) * P), slice(g * PTOK, (g + 1) * PTOK)
                pe.wait_ge(x2lo_ready, g + 1)
                if n >= 3:
                    pe.wait_ge(gelu_ready, n - 2)
                elif n == 2:
                    pe.wait_ge(hT_ready, UNITS)
                    pe.wait_ge(diff_steps, 4)
                else:
                    pe.wait_ge(exp_done, UNITS)
                    pe.wait_ge(weights_lo, PIECES)
                nc.tensor.matmul(up_bank(n), up_hi[:, w], x2hi[:, t], start=True, stop=False)
                nc.tensor.matmul(up_bank(n), up_hi[:, w], x2lo[:, t], start=False, stop=False)
                nc.tensor.matmul(up_bank(n), up_lo[:, w], x2hi[:, t], start=False, stop=True).then_inc(up_in_psum, 1)

            def down(n):
                g, c = divmod(n, CHUNKS)
                first, final = c == 0, c == CHUNKS - 1
                bank = down_bank(g)
                split = SPLIT_FROM <= n < SPLIT_TO
                if not split:
                    if final:
                        pe.wait_ge(gelu_ready, n + 1)
                    else:
                        pe.wait_ge(gact_ready, routed(n))
                else:
                    pe.wait_ge(gact_hi_ready, n - SPLIT_FROM + 1)
                    pe.wait_ge(gact_lo_ready, n - SPLIT_FROM + 1)
                    pe.wait_ge(weights_lo, 2 * PIECES)
                if first:
                    pe.wait_ge(hT_ready, UNITS)
                    pe.wait_ge(norm_steps, NORM_STEPS * LAST + N_SCALED)
                    if g >= 2:
                        pe.wait_ge(yT_ready, g - 1)
                if not split:
                    last = nc.tensor.matmul(bank, down_sb[:, c, :], gact[n % 4], start=first, stop=final)
                else:
                    nc.tensor.matmul(bank, down_hi[:, c, :], gact_hi[n % 3], start=first, stop=False)
                    nc.tensor.matmul(bank, down_lo[:, c, :], gact_hi[n % 3], start=False, stop=False)
                    last = nc.tensor.matmul(bank, down_hi[:, c, :], gact_lo[n % 3], start=False, stop=final)
                last.then_inc(down_done, 1)

            def turn_y(g):
                pe.wait_ge(yT_ready, g + 1)
                if g:
                    pe.wait_ge(res_ready, g)
                else:
                    pe.wait_ge(gateT_ready, PAIRS)
                for k in range(PTILES if g < PAIRS - 1 else PTILES // 2):
                    last = nc.tensor.transpose(pS[:, k * P:(k + 1) * P], yT[g % 2][:, k * P:(k + 1) * P], ident)
                last.then_inc(y_turned, 1)

            def turn_last_half():
                pe.wait_ge(yT_rest, 1)
                for k in range(PTILES // 2, PTILES):
                    last = nc.tensor.transpose(up_bank(0)[:, k * P:(k + 1) * P],
                                               yT[(PAIRS - 1) % 2][:, k * P:(k + 1) * P], ident)
                last.then_inc(y_turned, 1)

            pe.wait_ge(D_zeroed, 1)
            zeros = D[:, 0, 0:2, :, :].rearrange("p h k s -> p (h k s)")
            for _ in range(WARM_UP):
                nc.tensor.matmul(up_bank(0), zeros[:, 0:P], zeros, start=True, stop=True)
            pe.wait_ge(consts_loaded, 16)
            turn_queries(0)
            pe.wait_ge(dve_consts, 2)
            gates(0)
            products(0)
            for _ in range(WARM_GATES):
                nc.tensor.matmul(up_bank(0), zeros[:, 0:P], zeros, start=True, stop=True)
            exponents(0)
            turn_rows(0)

            def router_products(v):
                for j in range(PAIRS):
                    if v == TURN_GATE[j]:
                        turn_gate(j)
                    if v == TURN_X2[j]:
                        turn_x2(j)
                    if v == LOGITS[j]:
                        logits(j)

            for v in range(SLOTS):
                i, r = divmod(v, 4)
                if v + 1 < UNITS:
                    exponents(v + 1)
                if v % 2 == 0 and v < UNITS:
                    make_state(v // 2)
                if v % 2 == 1 and 3 <= v < UNITS:
                    turn_heads(v - 3)
                    turn_heads(v - 2)
                if r == 1 and i + 1 < PAIRS:
                    gates(i + 1)
                if v == UNITS:
                    up(0)
                if 1 <= v <= UNITS:
                    heads(v - 1)
                if v + 1 < UNITS:
                    products(v + 1)
                if r == 0 and i + 1 < PAIRS:
                    turn_queries(i + 1)
                if r == 3 and i + 1 < PAIRS:
                    turn_rows(i + 1)
                n = v - UNITS
                if v < UNITS:
                    router_products(v)
                if n == 0:
                    turn_heads(UNITS - 2)
                    turn_heads(UNITS - 1)
                    logits(1)
                    up(1)
                    turn_gate(0)
                    up(2)
                    spread_gate(0)
                    for _ in range(HOLD):
                        nc.tensor.matmul(pS[:, :], up_hi[:, 0:P], x2hi[:, 0:PTOK], start=True, stop=True)
                elif 0 < n < NCHUNK:
                    if n + 2 < NCHUNK:
                        up(n + 2)
                    if n % CHUNKS < CHUNKS - 1:
                        spread_gate(n)
                if n > 0:
                    router_products(v)
                if n >= LAG:
                    down(n - LAG)
                if v in TURN_Y:
                    turn_y(TURN_Y.index(v))
            turn_y(PAIRS - 1)
            turn_last_half()

        @block.vector
        def _(dve):
            def first_stats(i):
                dve.wait_ge(x_loaded[i], 16)
                for k in range(PTILES):
                    last = nc.vector.bn_stats(st1[:, k, :], x_sb[:, i * PTILES + k, :])
                last.then_inc(ln1_stats, 1)
                dve.wait_ge(ln1_stats, i + 1)
                if i >= 2:
                    dve.wait_ge(ln1_rstd, i - 1)
                for k in range(PTILES):
                    last = nc.vector.bn_aggr(mv1[:, i % 2, k, :], st1[:, k, :])
                last.then_inc(ln1_moments, 1)

            def first_shift(i):
                dve.wait_ge(ln1_rstd, i + 1)
                if i >= 2:
                    dve.wait_ge(xhat_ready, i - 1)
                nc.vector.scalar_tensor_tensor(out=shift1[:, i % 2, :], in0=mv1[:, i % 2, :, 0], scalar=-1.0,
                                               in1=rstd1[:, i % 2, :], op0=ALU.mult,
                                               op1=ALU.mult).then_inc(ln1_shift, 1)

            def gate_rows(i):
                base = GATE_STEPS * i
                dve.wait_ge(gates_ready, i + 1)
                nc.vector.tensor_scalar(zmin[:, :], z[:, :], 0.0, None, ALU.min).then_inc(gate_steps, 1)
                dve.wait_ge(gate_steps, base + MIN_STEP)
                dve.wait_ge(softplus_steps, 3 * i + 3)
                nc.vector.tensor_tensor_scan(Frow[:, :], zmin[:, :], soft[:, :], 0.0, ALU.add,
                                             ALU.subtract).then_inc(gate_steps, 1)
                dve.wait_ge(gate_steps, base + F_STEP)
                if i:
                    dve.wait_ge(row_exps, i)
                nc.vector.tensor_tensor(Grow[:, :], ig[:, :], Frow[:, :], ALU.subtract).then_inc(gate_steps, 1)
                dve.wait_ge(gate_steps, base + G_STEP)
                nc.vector.tensor_tensor_scan(Mrow[:, :], Grow[:, :], Grow[:, :], LOWEST, ALU.max,
                                             ALU.max).then_inc(gate_steps, 1)
                dve.wait_ge(split_hi, 2 * i + 1)
                nc.vector.tensor_tensor(Gst[LO:LO + ROWS, i % 2, :], Grow[:, :],
                                        Gst[0:ROWS, i % 2, :].bitcast(F32), ALU.subtract).then_inc(split_G, 1)
                dve.wait_ge(gate_steps, base + M_STEP)
                dve.wait_ge(split_hi, 2 * i + 2)
                nc.vector.scalar_tensor_tensor(out=Mst[LO:LO + ROWS, i % 2, :], in0=Mrow[:, :], scalar=-1.0,
                                               in1=Mst[0:ROWS, i % 2, :].bitcast(F32), op0=ALU.mult,
                                               op1=ALU.subtract).then_inc(split_ready, 1)
                nc.vector.tensor_tensor(FM[:, :], Frow[:, :], Mrow[:, :], ALU.add).then_inc(gate_steps, 1)
                nc.vector.tensor_scalar(negc[:, :], Mrow[:, P - 1:P], -1.0, None, ALU.mult).then_inc(gate_steps, 1)

            def read_rows(i):
                dve.wait_ge(rows_in_psum, i + 1)
                if i >= 2:
                    dve.wait_ge(hT_in_psum, 4 * (i - 1))
                nc.vector.tensor_tensor(qdec[:, i % 2, :, :], pS[:, 0:2 * P].rearrange("p (b s) -> p b s", b=2),
                                        qT[:, i % 2, :].rearrange("p (b s) -> p b s", b=2)[:, :, P:SEQ], ALU.mult)
                nc.vector.tensor_copy(tokq[:, i % 2, :, :],
                                      pS[:, 256:384].rearrange("p (k c) -> p k c", k=TILES)[:, :, 0:48]
                                      ).then_inc(rows_read, 1)

            def weigh_values(b):
                i, bb = divmod(b, 2)
                dve.wait_ge(rows_read, i + 1)
                dve.wait_ge(vx_zeroed, 1)
                dve.wait_ge(vx_ready, i + 1)
                if b >= 2:
                    dve.wait_ge(state_in_psum, b - 1)
                w = tokq[:, i % 2, 0, bb * HEADS:(bb + 1) * HEADS].unsqueeze(2).to_broadcast([P, HEADS, VW])
                nc.vector.tensor_tensor(vw[:, b % 2, :, :], vx[:, i % 2, bb * TILES, :, :], w, ALU.mult
                                        ).then_inc(vw_ready, 1)

            def weigh(u):
                dve.wait_ge(QK_in_psum, u + 1)
                dve.wait_ge(D_ready, u + 1)
                if u >= 2:
                    dve.wait_ge(hT_in_psum, u - 1)
                flat = "p h k s -> p (h k s)"
                nc.vector.tensor_tensor(C[:, u % 2, :, :, :].rearrange(flat), pQK[:, :, :, :].rearrange(flat),
                                        D[:, u % 2, :, :, :].rearrange(flat), ALU.mult).then_inc(C_ready, 1)

            def mask_state(b):
                dve.wait_ge(state_in_psum, b + 1)
                if b >= 2:
                    dve.wait_ge(hT_in_psum, 2 * b - 2)
                nc.vector.tensor_tensor(state[:, b % 2, :], state_psum, const("blockmask"),
                                        ALU.mult).then_inc(state_ready, 1)

            def normalizers(b):
                i, bb = divmod(b, 2)
                base = NORM_STEPS * b
                hp = pT[:, :].rearrange("p (n v) -> p n v", v=VW)
                floor = tokq[:, i % 2, :, 32 + bb * HEADS:32 + (bb + 1) * HEADS]
                dve.wait_ge(h_in_psum, 2 * b + 2)
                nrm_rows = nrm[:, :].rearrange("p (k h) -> p k h", k=TILES)
                nsum = hp[:, :, HD].rearrange("p (k h) -> p k h", k=TILES)
                nc.vector.scalar_tensor_tensor(out=nrm_rows, in0=nsum, scalar=-1.0, in1=floor, op0=ALU.mult,
                                               op1=ALU.max).then_inc(norm_steps, 1)
                dve.wait_ge(norm_steps, base + N_NEG)
                nc.vector.tensor_tensor(nrm2[:, :].rearrange("p (k h) -> p k h", k=TILES), nsum, nrm_rows,
                                        ALU.max).then_inc(norm_steps, 1)
                dve.wait_ge(norm_steps, base + N_MAX)
                nc.vector.tensor_scalar(nrm3[:, :], nrm2[:, :], EPS_NORMALIZER, None, ALU.add).then_inc(norm_steps, 1)
                dve.wait_ge(norm_steps, base + N_EPS)
                nc.vector.reciprocal(rinv[:, :], nrm3[:, :]).then_inc(norm_steps, 1)

            def centre_heads(b):
                base = NORM_STEPS * b
                hp = pT[:, :].rearrange("p (n v) -> p n v", v=VW)
                dve.wait_ge(norm_steps, base + N_INV)
                nc.vector.tensor_tensor(h[:, :, :], hp[:, :, 0:HD], rinv[:, :].unsqueeze(2).to_broadcast([P, 16, HD]),
                                        ALU.mult).then_inc(norm_steps, 1)
                dve.wait_ge(norm_steps, base + N_SCALED)
                nc.vector.tensor_reduce(hsum[:, :], h[:, :, :], AX.X, ALU.add).then_inc(norm_steps, 1)
                dve.wait_ge(norm_steps, base + N_SUM)
                if b >= 2:
                    dve.wait_ge(x1_ready, b - 1)
                nc.vector.scalar_tensor_tensor(out=hc[:, b % 2, :, :],
                                               in0=hsum[:, :].unsqueeze(2).to_broadcast([P, 16, HD]),
                                               scalar=-1.0 / HD, in1=h[:, :, :], op0=ALU.mult,
                                               op1=ALU.add).then_inc(norm_steps, 1)

            def head_variance(b):
                dve.wait_ge(squared, b + 1)
                nc.vector.tensor_reduce(hvar[:, b % 2, :], hsq[:, :, :], AX.X, ALU.add).then_inc(norm_steps, 1)

            def second_stats(j):
                dve.wait_ge(x1_ready, 2 * j + 2)
                for k in range(PTILES):
                    last = nc.vector.bn_stats(st2[:, k, :], x1[:, j * PTILES + k, :])
                last.then_inc(ln2_stats, 1)
                dve.wait_ge(ln2_stats, j + 1)
                for k in range(PTILES):
                    last = nc.vector.bn_aggr(mv2[:, k, :], st2[:, k, :])
                last.then_inc(ln2_moments, 1)

            def second_shift(j):
                if j < LATE:
                    dve.wait_ge(ln2_rstd, j + 1)
                else:
                    dve.wait_ge(ln2_late_rstd, j - LATE + 1)
                if j:
                    dve.wait_ge(x2hat_ready, j)
                nc.vector.scalar_tensor_tensor(out=shift2[:, :], in0=mv2[:, :, 0], scalar=-1.0, in1=rstd2[:, :],
                                               op0=ALU.mult, op1=ALU.mult).then_inc(ln2_shift, 1)

            def router_differences(j):
                logit = logits_psum(j).rearrange("p (k e) -> p k e", k=PTILES)
                dve.wait_ge(logits_in_psum, j + 1)
                nc.vector.tensor_reduce(rmax[:, :], logit, AX.X, ALU.max).then_inc(diff_steps, 1)
                dve.wait_ge(diff_steps, 2 * j + 1)
                if j >= 2:
                    dve.wait_ge(rexp_ready, j - 1)
                nc.vector.tensor_tensor(rdif[:, j % 2, :, :], logit, rmax[:, :].unsqueeze(2).to_broadcast([P, PTILES, EXPERTS]),
                                        ALU.subtract).then_inc(diff_steps, 1)

            wide = [P, PTILES, EXPERTS]
            flat_e = "p k e -> p (k e)"

            def route_a(j):
                base = ROUTER_STEPS * j
                rx = rexp[:, j % 2, :, :]
                dve.wait_ge(rexp_ready, j + 1)
                nc.vector.tensor_reduce(rsum[:, :], rx, AX.X, ALU.add).then_inc(router_steps, 1)
                for k in range(PTILES):
                    last = nc.vector.max(top8[:, k, :], rx[:, k, :])
                last.then_inc(router_steps, 1)
                dve.wait_ge(router_steps, base + R_SUM)
                nc.vector.reciprocal(rrec[:, :], rsum[:, :]).then_inc(router_steps, 1)

            def route_b(j):
                base = ROUTER_STEPS * j
                rx = rexp[:, j % 2, :, :]
                dve.wait_ge(router_steps, base + R_TOP)
                fourth = top8[:, :, TOPK - 1:TOPK].to_broadcast(wide)
                nc.vector.tensor_tensor(above[:, :, :], rx, fourth, ALU.is_gt).then_inc(router_steps, 1)
                nc.vector.tensor_tensor(equal[:, :, :], rx, fourth, ALU.is_equal).then_inc(router_steps, 1)
                dve.wait_ge(router_steps, base + R_ABOVE)
                nc.vector.tensor_reduce(nabove[:, :], above[:, :, :], AX.X, ALU.add).then_inc(router_steps, 1)
                dve.wait_ge(router_steps, base + R_EQUAL)
                nc.vector.tensor_tensor_scan(rank[:, :, :].rearrange(flat_e), const("reset"),
                                             equal[:, :, :].rearrange(flat_e), 0.0, ALU.mult,
                                             ALU.add).then_inc(router_steps, 1)
                dve.wait_ge(router_steps, base + R_RANK)
                nc.vector.tensor_tensor(rank2[:, :, :], rank[:, :, :], nabove[:, :].unsqueeze(2).to_broadcast(wide),
                                        ALU.add).then_inc(router_steps, 1)

            def route_c(j):
                base = ROUTER_STEPS * j
                rx = rexp[:, j % 2, :, :]
                dve.wait_ge(router_steps, base + R_PLACE)
                nc.vector.scalar_tensor_tensor(out=ties[:, :, :].rearrange(flat_e), in0=rank2[:, :, :].rearrange(flat_e),
                                               scalar=float(TOPK), in1=equal[:, :, :].rearrange(flat_e), op0=ALU.is_le,
                                               op1=ALU.mult).then_inc(router_steps, 1)
                dve.wait_ge(router_steps, base + R_TIES)
                nc.vector.tensor_tensor(chosen[:, :, :], above[:, :, :], ties[:, :, :], ALU.add).then_inc(router_steps, 1)
                dve.wait_ge(router_steps, base + R_CHOSEN)
                nc.vector.tensor_tensor(prob[:, :, :], chosen[:, :, :], rx, ALU.mult).then_inc(router_steps, 1)
                dve.wait_ge(router_steps, base + R_PROB)
                if j:
                    dve.wait_ge(gate_in_psum, j)
                nc.vector.tensor_tensor(gate[:, :, :], prob[:, :, :], rrec[:, :].unsqueeze(2).to_broadcast(wide),
                                        ALU.mult).then_inc(gate_ready, 1)

            def low_gate(j):
                cols = slice(j * PTOK, (j + 1) * PTOK)
                dve.wait_ge(gflat_ready, j + 1)
                nc.vector.tensor_tensor(gateT[LO:LO + EXPERTS, cols], pS[0:EXPERTS, :],
                                        gateT[0:EXPERTS, cols].bitcast(F32), ALU.subtract).then_inc(gateT_ready, 1)

            def weigh_experts(n):
                dve.wait_ge(gelu_ready, n + 1)
                dve.wait_ge(spread_in_psum, routed(n))
                if 4 <= n < SPLIT_FROM + 4:
                    dve.wait_ge(down_done, n - 3)
                elif n >= 4:
                    dve.wait_ge(gact_lo_ready, n - 4 - SPLIT_FROM + 1)
                nc.vector.tensor_tensor(gact[n % 4], spread_bank(n), act[n % 4], ALU.mult).then_inc(gact_ready, 1)

            def residual_part(g, bank, tiles):
                view = "p (k d) -> p k d"
                nc.vector.tensor_tensor(res[g % 2].rearrange(view, k=PTILES)[:, tiles, :],
                                        bank[:, :].rearrange(view, k=PTILES)[:, tiles, :],
                                        x1[:, g * PTILES + tiles.start:g * PTILES + tiles.stop, :], ALU.add
                                        ).then_inc(res_ready, 1)

            def add_residual(g):
                dve.wait_ge(y_turned, g + 1)
                if g >= 2:
                    dve.wait_ge(stored[g - 2], 16)
                residual_part(g, pS, slice(0, PTILES if g < PAIRS - 1 else PTILES // 2))

            nc.vector.memset(D[:, 0, 0:2, :, :], 0.0).then_inc(D_zeroed, 1)
            nc.vector.memset(one1[:, :], 1.0)
            nc.vector.memset(eps_head[:, :], EPS_HEAD)
            nc.vector.memset(eps_ln[:, :], EPS_LN).then_inc(dve_consts, 1)
            nc.vector.memset(kmask[:, 0, HEADS // 2:HEADS, :], 0.0).then_inc(kmask_zeroed[0], 1)
            first_stats(0)
            first_shift(0)
            for k in range(PTILES // 2, PTILES):
                last = nc.vector.tensor_scalar(xhat[:, k, :], x_sb[:, k, :], mv1[:, 0, k, 0:1], rstd1[:, 0, k:k + 1],
                                               ALU.subtract, ALU.mult)
            last.then_inc(xhat_half, 1)
            dve.wait_ge(consts_loaded, 16)
            nc.vector.tensor_tensor(gwc[:, :, :].rearrange("p b c -> p (b c)"), const("gwk"), const("gwv"), ALU.add)
            nc.vector.tensor_scalar(gwq4[:, :, :].rearrange("p b c -> p (b c)"), const("gwq"), HD ** 0.5, None,
                                    ALU.mult).then_inc(dve_consts, 1)
            nc.vector.tensor_copy(sel[:, :, :], const("selcol").unsqueeze(2).to_broadcast([P, ROWS, P]))
            nc.vector.tensor_copy(esel[:, :, :], const("selcol").unsqueeze(2).to_broadcast([P, EXPERTS, HID]))
            dve.wait_ge(pool_consts, 1)
            gate_rows(0)
            first_stats(1)
            read_rows(0)
            weigh_values(0)
            for v in range(SLOTS):
                i, r = divmod(v, 4)
                n = v - UNITS
                if v == DIFFS[0]:
                    router_differences(0)
                for j in range(PAIRS):
                    if v == LOW_GATE[j]:
                        low_gate(j)
                if v == UNITS:
                    head_variance(LAST - 1)
                    normalizers(LAST)
                    router_differences(1)
                    centre_heads(LAST)
                    low_gate(0)
                    weigh_experts(0)
                    head_variance(LAST)
                if v < UNITS:
                    weigh(v)
                if 0 < n < NCHUNK and n % CHUNKS < CHUNKS - 1:
                    weigh_experts(n)
                if r == 0 and i + 1 < PAIRS:
                    first_shift(i + 1)
                for j in range(LATE, PAIRS):
                    if v == SHIFT2[j]:
                        second_shift(j)
                for j in range(PAIRS):
                    if v == DIFFS[j] and j:
                        router_differences(j)
                if r == 2 and i + 1 < PAIRS:
                    gate_rows(i + 1)
                if v % 2 == 0 and v < UNITS:
                    mask_state(v // 2)
                if v % 2 == 0 and 4 <= v < UNITS:
                    head_variance((v - 4) // 2)
                if v % 2 == 1 and 3 <= v < UNITS:
                    normalizers((v - 3) // 2)
                    centre_heads((v - 3) // 2)
                for j in range(LATE):
                    if v == SHIFT2[j]:
                        second_shift(j)
                if r == 3 and i + 1 < PAIRS:
                    read_rows(i + 1)
                if v % 2 == 1 and (v + 1) // 2 < BATCH:
                    weigh_values((v + 1) // 2)
                if r == 0 and i + 2 < PAIRS:
                    first_stats(i + 2)
                for j in range(PAIRS):
                    if v == STATS2[j]:
                        second_stats(j)
                    if v == ROUTE_A[j]:
                        route_a(j)
                    if v == ROUTE_B[j]:
                        route_b(j)
                    if v == ROUTE_C[j]:
                        route_c(j)
                if v in RESIDUAL:
                    add_residual(RESIDUAL.index(v))
            add_residual(PAIRS - 1)
            dve.wait_ge(y_turned, PAIRS + 1)
            residual_part(PAIRS - 1, up_bank(0), slice(PTILES // 2, PTILES))


def kernel(x, ctx_1024, L0_xattn_igate_w, L0_xattn_igate_b, L0_xattn_fgate_w, L0_xattn_fgate_b,
           L0_xattn_norm_w, L0_ffn_shared_up, L0_ffn_shared_down, L0_ffn_routed_up, L0_ffn_routed_down,
           L0_ffn_router_w):
    import numpy as np
    import concourse.bacc as bacc
    from concourse.bass_utils import run_bass_kernel_spmd

    f32 = np.float32
    tokens = BATCH * SEQ
    x_in = np.ascontiguousarray(np.asarray(x).reshape(tokens, DIM))
    ctx_in = np.ascontiguousarray(np.asarray(ctx_1024).reshape(tokens, DIM))
    igw, fgw = np.asarray(L0_xattn_igate_w), np.asarray(L0_xattn_fgate_w)

    def gate_window(part):
        w = np.zeros((DIM, 2, 48), f32)
        for bb in range(2):
            w[:, bb, bb * HEADS:(bb + 1) * HEADS] = fgw[:, part * DIM:(part + 1) * DIM].T
            w[:, bb, 32 + bb * HEADS:32 + (bb + 1) * HEADS] = igw[:, part * DIM:(part + 1) * DIM].T
        return w.reshape(DIM, 96)

    rows = np.arange(P)
    blockmask = np.zeros((P, HEADS, VW), f32)
    blockmask[rows, rows // HD, :] = 1.0
    spread = np.zeros((P, 2, P), f32)
    selcol = np.zeros((P, ROWS), f32)
    for r in range(ROWS):
        spread[r, r // HEADS, (r % HEADS) * HD:(r % HEADS + 1) * HD] = 1.0
        selcol[r, r] = selcol[LO + r, r] = 1.0
    gbias = np.zeros((P, 1), f32)
    for bb in range(2):
        gbias[bb * HEADS:(bb + 1) * HEADS, 0] = np.asarray(L0_xattn_fgate_b)
        gbias[32 + bb * HEADS:32 + (bb + 1) * HEADS, 0] = np.asarray(L0_xattn_igate_b)
    reset = np.ones((P, PTILES, EXPERTS), f32)
    reset[:, :, 0] = 0.0
    parts = {"ident": np.eye(P, dtype=f32), "blockmask": blockmask.reshape(P, -1),
             "spread": spread.reshape(P, -1), "selcol": selcol,
             "normw": np.broadcast_to(np.asarray(L0_xattn_norm_w), (P, DIM)), "reset": reset.reshape(P, -1),
             "gwq": gate_window(0), "gwk": gate_window(1), "gwv": gate_window(2), "gbias": gbias,
             "router": np.asarray(L0_ffn_router_w).T}
    up = np.concatenate([np.asarray(L0_ffn_routed_up).reshape(-1, DIM), np.asarray(L0_ffn_shared_up).reshape(-1, DIM)])
    down = np.concatenate([np.asarray(w).transpose(0, 2, 1).reshape(-1, DIM)
                           for w in (L0_ffn_routed_down, L0_ffn_shared_down)])
    arrays = {
        "x": x_in, "ctx_rows": ctx_in, "ctx_cols": np.ascontiguousarray(ctx_in.T),
        "consts": np.concatenate([parts[name] for name, _ in CONST_PARTS], axis=1),
        "up_w": np.ascontiguousarray(up.T),
        "down_w": np.ascontiguousarray(down.reshape(CHUNKS, P, DIM).transpose(1, 0, 2)),
    }
    nc = bacc.Bacc("TRN2", target_bir_lowering=False, num_devices=1)
    args = [nc.dram_tensor(n, a.shape, mybir.dt.from_np(a.dtype), kind="ExternalInput").ap() for n, a in arrays.items()]
    out = nc.dram_tensor("out", (tokens, DIM), F32, kind="ExternalOutput").ap()
    build(nc, *args, out)
    r = run_bass_kernel_spmd(nc, [arrays], core_ids=[0])
    return r.results[0]["out"].reshape(BATCH, SEQ, DIM)
```
